# Optimizing a Trainium2 kernel written in Bass

```python
import numpy as np
import jax
import jax.numpy as jnp

def _softmax(x, axis=-1):
    return jax.nn.softmax(x, axis=axis)

def _gelu(x):
    return jax.nn.gelu(x, approximate=True)

def _silu(x):
    return jax.nn.silu(x)

def _sigmoid(x):
    return jax.nn.sigmoid(x)

def _layernorm(x, axis=-1, eps=1e-05):
    m = jnp.mean(x, axis=axis, keepdims=True)
    v = jnp.var(x, axis=axis, keepdims=True)
    return (x - m) / jnp.sqrt(v + eps)

def _scatter_add(tgt, idx, src, axis=0):
    return tgt.at[idx].add(src)

def _segment_sum(src, seg, n):
    return jax.ops.segment_sum(src, seg, n)
kernel_name = 'mk_macaron_d2_jaxref_r8_098385'

def setup_inputs(seed: int=0):
    np.random.seed(seed)
    _w = jnp.asarray

    def _L0_attn_setup():
        import jax, jax.numpy as jnp
        import numpy as np
        import math
        D = 32
        N = 256
        B = 8
        N_PLUS_1 = 256
        key = jax.random.key(seed)
        k1, k2, k3, k4, k5 = jax.random.split(key, 5)
        scale = 1.0 / math.sqrt(D)
        return {'Z_in': jax.random.normal(k1, (B, D + 1, N), dtype=jnp.float32), 'A_l': jax.random.normal(k2, (D, D), dtype=jnp.float32) * scale, 'r_l': jax.random.normal(k3, (1,), dtype=jnp.float32), 'B_l': jax.random.normal(k4, (D, D), dtype=jnp.float32) * scale, 'C_l': jax.random.normal(k5, (D, D), dtype=jnp.float32) * scale}
    _L0_attn_in = _L0_attn_setup()

    def _L0_ffn_setup():
        import jax, jax.numpy as jnp
        import numpy as np
        H = 256
        I = 1024
        MI = 128
        E = 8
        K = 2
        B, S = (2, 128)
        EPS = 1e-06
        ROOT = H ** (-0.5)

        def _rms(x, w=None, eps=EPS):
            ms = jnp.mean(x * x, axis=-1, keepdims=True) + eps
            y = x * jax.lax.rsqrt(ms)
            return y * w if w is not None else y

        def _gelu_tanh(x):
            return jax.nn.gelu(x, approximate=True)
        key = jax.random.key(seed)
        ks = jax.random.split(key, 10)
        s = 0.02
        return {'hidden_states': jax.random.normal(ks[0], (B, S, H), jnp.float32), 'rn_pre1': jnp.ones((H,), jnp.float32), 'rn_pre2': jnp.ones((H,), jnp.float32), 'rn_post1': jnp.ones((H,), jnp.float32), 'rn_post2': jnp.ones((H,), jnp.float32), 'rn_post': jnp.ones((H,), jnp.float32), 'w_gate': jax.random.normal(ks[1], (H, I), jnp.float32) * s, 'w_up': jax.random.normal(ks[2], (H, I), jnp.float32) * s, 'w_down': jax.random.normal(ks[3], (I, H), jnp.float32) * s, 'router_w': jax.random.normal(ks[4], (H, E), jnp.float32) * s, 'router_scale': jnp.ones((H,), jnp.float32), 'per_expert_scale': jnp.ones((E,), jnp.float32), 'we_gate': jax.random.normal(ks[5], (E, H, MI), jnp.float32) * s, 'we_up': jax.random.normal(ks[6], (E, H, MI), jnp.float32) * s, 'we_down': jax.random.normal(ks[7], (E, MI, H), jnp.float32) * s}
    _L0_ffn_in = _L0_ffn_setup()

    def _L1_attn_setup():
        import jax, jax.numpy as jnp
        import numpy as np
        HIDDEN = 256
        HEADS = 16
        HEAD_DIM = HIDDEN // HEADS
        KV_DIM = 128
        SLOPE = 0.0625

        def alibi_bias(seq_len):
            i = jnp.arange(seq_len)[:, None]
            j = jnp.arange(seq_len)[None, :]
            return jnp.where(j <= i, -SLOPE * (i - j).astype(jnp.float32), -jnp.inf)
        key = jax.random.key(seed)
        ks = jax.random.split(key, 6)
        B, S = (2, 256)
        s = 0.02
        return {'hidden_states': jax.random.normal(ks[0], (B, S, HIDDEN), jnp.float32), 'w_dkv': jax.random.normal(ks[1], (KV_DIM, HIDDEN), jnp.float32) * s, 'w_q': jax.random.normal(ks[2], (HIDDEN, HIDDEN), jnp.float32) * s, 'w_uk': jax.random.normal(ks[3], (HIDDEN, KV_DIM), jnp.float32) * s, 'w_uv': jax.random.normal(ks[4], (HIDDEN, KV_DIM), jnp.float32) * s, 'w_o': jax.random.normal(ks[5], (HIDDEN, HIDDEN), jnp.float32) * s}
    _L1_attn_in = _L1_attn_setup()

    def _L1_ffn_setup():
        import jax, jax.numpy as jnp
        import numpy as np
        TOP_K = 4
        key = jax.random.key(seed)
        k1, k2, k3, k4 = jax.random.split(key, 4)
        B, S, D, E, H, O = (4, 256, 256, 8, 128, 256)
        scale = 0.02
        return {'x': jax.random.normal(k1, (B, S, D), dtype=jnp.float32), 'wg': jax.random.normal(k2, (D, E), dtype=jnp.float32) * scale, 'w1': jax.random.normal(k3, (E, H, D), dtype=jnp.float32) * scale, 'w2': jax.random.normal(k4, (E, O, H), dtype=jnp.float32) * scale}
    _L1_ffn_in = _L1_ffn_setup()
    _d = {'L0_attn_Z_in': _L0_attn_in['Z_in'], 'L0_attn_A_l': _L0_attn_in['A_l'], 'L0_attn_r_l': _L0_attn_in['r_l'], 'L0_attn_B_l': _L0_attn_in['B_l'], 'L0_attn_C_l': _L0_attn_in['C_l'], 'L0_ffn_rn_pre1': _L0_ffn_in['rn_pre1'], 'L0_ffn_rn_pre2': _L0_ffn_in['rn_pre2'], 'L0_ffn_rn_post1': _L0_ffn_in['rn_post1'], 'L0_ffn_rn_post2': _L0_ffn_in['rn_post2'], 'L0_ffn_rn_post': _L0_ffn_in['rn_post'], 'L0_ffn_w_gate': _L0_ffn_in['w_gate'], 'L0_ffn_w_up': _L0_ffn_in['w_up'], 'L0_ffn_w_down': _L0_ffn_in['w_down'], 'L0_ffn_router_w': _L0_ffn_in['router_w'], 'L0_ffn_router_scale': _L0_ffn_in['router_scale'], 'L0_ffn_per_expert_scale': _L0_ffn_in['per_expert_scale'], 'L0_ffn_we_gate': _L0_ffn_in['we_gate'], 'L0_ffn_we_up': _L0_ffn_in['we_up'], 'L0_ffn_we_down': _L0_ffn_in['we_down'], 'L1_attn_w_dkv': _L1_attn_in['w_dkv'], 'L1_attn_w_q': _L1_attn_in['w_q'], 'L1_attn_w_uk': _L1_attn_in['w_uk'], 'L1_attn_w_uv': _L1_attn_in['w_uv'], 'L1_attn_w_o': _L1_attn_in['w_o'], 'L1_ffn_wg': _L1_ffn_in['wg'], 'L1_ffn_w1': _L1_ffn_in['w1'], 'L1_ffn_w2': _L1_ffn_in['w2']}
    _x0 = _d['L0_attn_Z_in']
    _d['L0_attn_Z_in'] = jax.random.normal(jax.random.fold_in(jax.random.key(seed), 1), (4, 256, 256), dtype=_x0.dtype)
    del _x0
    return _d

def reference(L0_attn_Z_in, L0_attn_A_l, L0_attn_r_l, L0_attn_B_l, L0_attn_C_l, L0_ffn_rn_pre1, L0_ffn_rn_pre2, L0_ffn_rn_post1, L0_ffn_rn_post2, L0_ffn_rn_post, L0_ffn_w_gate, L0_ffn_w_up, L0_ffn_w_down, L0_ffn_router_w, L0_ffn_router_scale, L0_ffn_per_expert_scale, L0_ffn_we_gate, L0_ffn_we_up, L0_ffn_we_down, L1_attn_w_dkv, L1_attn_w_q, L1_attn_w_uk, L1_attn_w_uv, L1_attn_w_o, L1_ffn_wg, L1_ffn_w1, L1_ffn_w2):

    def _L0_attn_ref(Z_in, A_l, r_l, B_l, C_l):
        import jax, jax.numpy as jnp
        import numpy as np
        import math
        D = 32
        N = 256
        B = 8
        N_PLUS_1 = 256
        X = Z_in[:, :D, :]
        Y = Z_in[:, D:, :]
        U = jnp.einsum('ij,bjn->bin', B_l, X)
        W = jnp.einsum('ij,bjn->bin', C_l, X)
        scores = jnp.einsum('bdn,bdm->bnm', U, W)
        att = jax.nn.relu(scores)
        att = att.at[:, N_PLUS_1 - 1, N_PLUS_1 - 1].set(0.0)
        X_att = jnp.einsum('bdn,bnm->bdm', X, att)
        X_out = X + jnp.einsum('ij,bjm->bim', A_l, X_att)
        Y_out = Y + r_l * jnp.einsum('bdn,bnm->bdm', Y, att)
        return jnp.concatenate([X_out, Y_out], axis=1)

    def _L0_ffn_ref(hidden_states, rn_pre1, rn_pre2, rn_post1, rn_post2, rn_post, w_gate, w_up, w_down, router_w, router_scale, per_expert_scale, we_gate, we_up, we_down):
        import jax, jax.numpy as jnp
        import numpy as np
        H = 256
        I = 1024
        MI = 128
        E = 8
        K = 2
        B, S = (2, 128)
        EPS = 1e-06
        ROOT = H ** (-0.5)

        def _rms(x, w=None, eps=EPS):
            ms = jnp.mean(x * x, axis=-1, keepdims=True) + eps
            y = x * jax.lax.rsqrt(ms)
            return y * w if w is not None else y

        def _gelu_tanh(x):
            return jax.nn.gelu(x, approximate=True)
        b, s, h = hidden_states.shape
        T = b * s
        dense_in = _rms(hidden_states, rn_pre1)
        dense_out = _gelu_tanh(dense_in @ w_gate) * (dense_in @ w_up) @ w_down
        dense_out = _rms(dense_out, rn_post1)
        x = hidden_states.reshape(T, h)
        xr = _rms(x) * router_scale * ROOT
        router_logits = xr @ router_w
        probs = jax.nn.softmax(router_logits, axis=-1)
        top_w, top_i = jax.lax.top_k(probs, K)
        top_w = top_w / jnp.sum(top_w, axis=-1, keepdims=True)
        top_w = top_w * per_expert_scale[top_i]
        aff = jnp.zeros((T, E), x.dtype).at[jnp.arange(T)[:, None], top_i].set(top_w)
        moe_in = _rms(hidden_states, rn_pre2).reshape(T, h)
        g = jnp.einsum('th,ehm->tem', moe_in, we_gate)
        u = jnp.einsum('th,ehm->tem', moe_in, we_up)
        eo = jnp.einsum('tem,emh->teh', _gelu_tanh(g) * u, we_down)
        moe_out = jnp.einsum('te,teh->th', aff, eo).reshape(b, s, h)
        moe_out = _rms(moe_out, rn_post2)
        return _rms(dense_out + moe_out, rn_post)

    def _L1_attn_ref(hidden_states, w_dkv, w_q, w_uk, w_uv, w_o):
        import jax, jax.numpy as jnp
        import numpy as np
        HIDDEN = 256
        HEADS = 16
        HEAD_DIM = HIDDEN // HEADS
        KV_DIM = 128
        SLOPE = 0.0625

        def alibi_bias(seq_len):
            i = jnp.arange(seq_len)[:, None]
            j = jnp.arange(seq_len)[None, :]
            return jnp.where(j <= i, -SLOPE * (i - j).astype(jnp.float32), -jnp.inf)
        B, S, _ = hidden_states.shape
        scale = HEAD_DIM ** (-0.5)
        c_kv = hidden_states @ w_dkv.T
        q = (hidden_states @ w_q.T).reshape(B, S, HEADS, HEAD_DIM)
        k = (c_kv @ w_uk.T).reshape(B, S, HEADS, HEAD_DIM)
        v = (c_kv @ w_uv.T).reshape(B, S, HEADS, HEAD_DIM)
        scores = jnp.einsum('bqhd,bkhd->bhqk', q, k) * scale
        scores = scores + alibi_bias(S)[None, None]
        attn = jax.nn.softmax(scores, axis=-1)
        out = jnp.einsum('bhqk,bkhd->bqhd', attn, v).reshape(B, S, HIDDEN)
        return out @ w_o.T

    def _L1_ffn_ref(x, wg, w1, w2):
        import jax, jax.numpy as jnp
        import numpy as np
        TOP_K = 4
        B, S, D = x.shape
        xt = x.reshape(B * S, D)
        gate = xt @ wg
        top_val, top_idx = jax.lax.top_k(gate, TOP_K)
        gs = jax.nn.softmax(top_val, axis=-1)
        gs_eff = jnp.ones_like(gs) + gs - jax.lax.stop_gradient(gs)
        h = jax.nn.relu(jnp.einsum('nd,ehd->neh', xt, w1))
        out_all = jnp.einsum('neh,eoh->neo', h, w2)
        out_k = jnp.take_along_axis(out_all, top_idx[:, :, None], axis=1)
        out = jnp.einsum('nk,nko->no', gs_eff, out_k)
        return out.reshape(B, S, -1)
    x = L0_attn_Z_in
    x = x + 0.5 * _L0_ffn_ref(_layernorm(x, axis=-1), L0_ffn_rn_pre1, L0_ffn_rn_pre2, L0_ffn_rn_post1, L0_ffn_rn_post2, L0_ffn_rn_post, L0_ffn_w_gate, L0_ffn_w_up, L0_ffn_w_down, L0_ffn_router_w, L0_ffn_router_scale, L0_ffn_per_expert_scale, L0_ffn_we_gate, L0_ffn_we_up, L0_ffn_we_down)
    x = x + _L0_attn_ref(_layernorm(x, axis=-1), L0_attn_A_l, L0_attn_r_l, L0_attn_B_l, L0_attn_C_l)
    x = x + 0.5 * _L0_ffn_ref(_layernorm(x, axis=-1), L0_ffn_rn_pre1, L0_ffn_rn_pre2, L0_ffn_rn_post1, L0_ffn_rn_post2, L0_ffn_rn_post, L0_ffn_w_gate, L0_ffn_w_up, L0_ffn_w_down, L0_ffn_router_w, L0_ffn_router_scale, L0_ffn_per_expert_scale, L0_ffn_we_gate, L0_ffn_we_up, L0_ffn_we_down)
    x = x + 0.5 * _L1_ffn_ref(_layernorm(x, axis=-1), L1_ffn_wg, L1_ffn_w1, L1_ffn_w2)
    x = x + _L1_attn_ref(_layernorm(x, axis=-1), L1_attn_w_dkv, L1_attn_w_q, L1_attn_w_uk, L1_attn_w_uv, L1_attn_w_o)
    x = x + 0.5 * _L1_ffn_ref(_layernorm(x, axis=-1), L1_ffn_wg, L1_ffn_w1, L1_ffn_w2)
    return x

_drawn_inputs = setup_inputs


def setup_inputs(seed=0):
    import zlib

    import numpy as np

    out = dict(_drawn_inputs(seed))
    spreads = {'L0_ffn_rn_pre1': (1.0, 0.2),
     'L0_ffn_rn_pre2': (1.0, 0.2),
     'L0_ffn_rn_post1': (1.0, 0.2),
     'L0_ffn_rn_post2': (1.0, 0.2),
     'L0_ffn_rn_post': (1.0, 0.2),
     'L0_ffn_router_scale': (1.0, 0.2),
     'L0_ffn_per_expert_scale': (1.0, 0.2)}
    factors = {'L1_attn_w_dkv': 8.0,
     'L1_attn_w_q': 8.0,
     'L1_attn_w_uk': 8.0,
     'L1_attn_w_uv': 8.0,
     'L1_attn_w_o': 8.0,
     'L1_ffn_wg': 8.0,
     'L1_ffn_w1': 8.0,
     'L1_ffn_w2': 8.0}
    for name, (base, spread) in spreads.items():
        noise = np.random.default_rng([zlib.crc32(name.encode()), seed]).standard_normal(out[name].shape)
        drawn = base * np.exp(spread * noise) if base else spread * noise
        out[name] = jnp.asarray(drawn.astype(out[name].dtype))
    for name, factor in factors.items():
        out[name] = (out[name] * factor).astype(out[name].dtype)
    return out
```

```python
from contextlib import ExitStack

import concourse.bass as bass
from concourse import mybir

F32 = mybir.dt.float32
F32R = mybir.dt.float32r
U32 = mybir.dt.uint32
ALU = mybir.AluOpType
ACT = mybir.ActivationFunctionType
AX = mybir.AxisListType

P = 128
D = 256
TOKENS = 1024
TILES = TOKENS // P
BT = 4
BLK = BT * P
KC = D // P
E = 8
J0 = 8
U0 = J0 + E
U1 = E
LN_EPS = 1e-5
RMS_EPS = 1e-6
ROOT = float(D) ** -0.5
SA = 32
HEADS = 16
HD = D // HEADS
SLOT = 32
SEQ = 256
LAG = 2

STAGES = ["ffn0", "attn0", "ffn0", "ffn1", "attn1", "ffn1"]

WA = 2 * D + 2 * P + D + D + 2 * D
W_Q, W_C, W_K, W_V, W_O = 0, 2 * D, 3 * D, 4 * D, 5 * D
ROWS = 3 * HD
STEP = 64
FAR = 3.0e38
N_SETUP = 8


def program(nc, x_in, w0, w1, wr, pre, posts, att0, r0, ident_in, cap_in, iota_in, wa, sel_in, bias_in, out,
            stages=STAGES):
    with ExitStack() as ctx:
        def sb(name, shape, dt=F32):
            return ctx.enter_context(nc.sbuf_tensor(name, shape, dt))

        def sem(name):
            return ctx.enter_context(nc.semaphore(name))

        ps = ctx.enter_context(nc.psum_tensor("ps", [P, 8, 512], F32))
        x = sb("x", [P, TILES, D])
        z = sb("z", [P, BT, D])
        zh = sb("zh", [P, KC, BLK], F32R)
        zl = sb("zl", [P, KC, BLK], F32R)
        w1_h = sb("w1_h", [P, E, 2 * D], F32R)
        w1_l = sb("w1_l", [P, E, 2 * D], F32R)
        NST = 2
        stage = sb("stage", [P, NST, 3 * D])
        stage1 = stage
        wr_raw = sb("wr_raw", [P, 2, KC, E])
        wr_h = sb("wr_h", [P, 2, KC, P], F32R)
        wr_l = sb("wr_l", [P, 2, KC, P], F32R)
        pre_c = sb("pre_c", [P, 3, KC])
        post_b = sb("post_b", [P, 3 * D + E])
        ident = sb("ident", [P, P])
        cap_c = sb("cap_c", [P, 1])
        iota_b = sb("iota_b", [P, BT * E])
        gel = sb("gel", [P, 2, BLK])
        act32 = sb("act32", [P, 2, BLK])
        ah = sb("ah", [P, 2, BLK], F32R)
        al = sb("al", [P, 2, BLK], F32R)
        macc = sb("macc", [P, BT, D])
        comb = sb("comb", [P, BT, D])
        tmp = sb("tmp", [P, BT, D])
        sq = sb("sq", [P, BT, D], mybir.dt.bfloat16)
        bn = sb("bn", [P, BT, 6])
        mv = sb("mv", [P, BT, 2])
        zs = sb("zs", [P, BT])
        zs_e = sb("zs_e", [P, BT])
        half = sb("half", [P, BT])
        ssq = sb("ssq", [P, 3, BT])
        ssq_e = sb("ssq_e", [P, 3, BT])
        rinv = sb("rinv", [P, 3, BT])
        lgt = sb("lgt", [E, BLK])
        lg = sb("lg", [P, BT, E])
        mx = sb("mx", [P, BT, 8])
        mi = sb("mi", [P, BT, 8], U32)
        mif = sb("mif", [P, BT, 8])
        lsh = sb("lsh", [P, BT, E])
        lex = sb("lex", [P, BT, E])
        eq = sb("eq", [P, BT, E, 4])
        selm = sb("selm", [P, BT, E])
        em = sb("em", [P, BT, E])
        esum = sb("esum", [P, BT])
        erec = sb("erec", [P, BT])
        gs = sb("gs", [P, BT, E])
        gs1 = sb("gs1", [P, BT, E])
        aff = sb("aff", [P, 2, BT, E])
        a0 = sb("a0", [SA, 3 * SA])
        r0c = sb("r0c", [P, 1])
        m0 = sb("m0", [P, 2, P])
        pt = sb("pt", [SA, SA])
        pxs = sb("pxs", [SA, 2, D])
        mt = gel[:, :, :].rearrange("p s (c d) -> p s c d", c=2)
        att = act32[:, :, :].rearrange("p s (c d) -> p s c d", c=2)
        xz = tmp[:, :, :].rearrange("p (s t) d -> p s t d", s=2)

        with ExitStack() as first:
            def sb0(name, shape, dt=F32R):
                return first.enter_context(nc.sbuf_tensor(name, shape, dt))

            w0u_h = sb0("w0u_h", [P, U0, KC, 2, P])
            w0u_l = sb0("w0u_l", [P, U0, KC, 2, P])
            w0d_h = sb0("w0d_h", [P, U0, D])
            w0d_l = sb0("w0d_l", [P, U0, D])
        wa_h = sb("wa_h", [P, WA], F32R)
        wa_l = sb("wa_l", [P, WA], F32R)
        sel = sb("sel", [P, 4, 4, P], F32R)
        bias = sb("bias", [P, 3 * P])
        ch = sb("ch", [P, BLK], F32R)
        cl = sb("cl", [P, BLK], F32R)
        qh = sb("qh", [P, 2, BLK], F32R)
        ql = sb("ql", [P, 2, BLK], F32R)
        kh, kl = ah, al
        qs = sb("qs", [P, HEADS // 2, BLK], F32R)
        ks = sb("ks", [P, HEADS // 2, BLK], F32R)
        va = sb("va", [P, BT, HEADS, SLOT])
        pb = sb("pb", [P, 3, 3 * P])
        pbt = sb("pbt", [P, 2, 4, 3 * P])
        wa_raw = va[:, :, :, :].rearrange("p t h s -> p (t h s)")[:, 0:WA]
        sel_raw = pbt[:, :, :, :].rearrange("p g j q -> p (g j q)")[:, 0:16 * P]
        ot = [b[:, :, :].rearrange("p s (g q) -> p (s g) q", q=SEQ) for b in (gel, act32)]
        on = comb[:, 0:2, :]
        oth = sb("oth", [P, 2, KC, P], F32R)
        otl = sb("otl", [P, 2, KC, P], F32R)
        mark = sb("mark", [P, 1])
        nmin = sb("nmin", [P, 4, 2])
        rec = sb("rec", [P, 2, HEADS])

        x_in_s = sem("x_loaded")
        const_s = sem("consts_loaded")
        stage_s = [sem(f"stage_loaded{i}") for i in range(NST)]
        out_s = sem("out_stored")
        setup_pool = sem("setup_pool")
        wr_split = sem("router_split")
        w_hi = sem("weights_hi")
        w_lo = sem("weights_lo")
        bn_s = sem("ln_stats")
        mv_s = sem("ln_mean_var")
        zse_s = sem("ln_var_eps")
        zs_s = sem("ln_scale")
        z_s = sem("z_ready")
        zt_s = sem("zt_ready")
        zh_s = sem("zh_ready")
        zl_s = sem("zl_ready")
        gu_s = sem("gate_up_ready")
        gelu_s = sem("gelu_ready")
        prod_s = sem("prod_ready")
        ah_s = sem("act_hi_ready")
        al_s = sem("act_lo_ready")
        down_s = sem("down_ready")
        acc_s = sem("moe_accumulated")
        h1_s = sem("hidden1_ready")
        ah1_s = sem("hidden1_hi_ready")
        al1_s = sem("hidden1_lo_ready")
        down1_s = sem("down1_ready")
        lgt_ps_s = sem("logits_t_in_psum")
        lgt_s = sem("logits_t_ready")
        lg_ps_s = sem("logits_in_psum")
        tk = sem("topk_steps")
        lsh_s = sem("logits_shifted")
        lex_s = sem("logits_exp")
        dsq_s = sem("dense_squares")
        msq_s = sem("moe_squares")
        csq_s = sem("sum_squares")
        rms_e_s = sem("rms_eps_added")
        rd_s = sem("dense_rms_ready")
        rm_s = sem("moe_rms_ready")
        rc_s = sem("sum_rms_ready")
        dn_s = sem("dense_normed")
        mn_s = sem("moe_normed")
        comb_s = sem("sum_ready")
        fin_s = sem("ffn_out_ready")
        x_s = sem("x_done")
        a0_set = sem("attn0_setup")
        pt_ps_s = sem("attn0_bc_in_psum")
        mt_ps_s = sem("attn0_mt_in_psum")
        mt_s = sem("attn0_mt")
        px_s = sem("attn0_px")
        sc_ps_s = sem("attn0_scores_in_psum")
        att_s = sem("attn0_relu")
        attz_s = sem("attn0_corner")
        xz_s = sem("attn0_xz")
        o0_s = sem("attn0_out_in_psum")
        upd_s = sem("attn0_updated")

        wa_s = sem("attn1_consts_loaded")
        wah_s = sem("attn1_weights_hi")
        wal_s = sem("attn1_weights_lo")
        q_ps = sem("q_in_psum")
        qh_s = sem("q_hi")
        ql_s = sem("q_lo")
        c_ps = sem("ckv_in_psum")
        ch_s = sem("ckv_hi")
        cl_s = sem("ckv_lo")
        k_ps = sem("k_in_psum")
        kh_s = sem("k_hi")
        kl_s = sem("k_lo")
        v_ps = sem("v_in_psum")
        v_s = sem("v_ready")
        st_ps = sem("stack_in_psum")
        sta_s = sem("stack_by_act")
        std_s = sem("stack_by_dve")
        s_ps = sem("scores_in_psum")
        sm_s = sem("scores_biased")
        exp_s = sem("probs_ready")
        t_ps = sem("probs_t_in_psum")
        ptd_s = sem("probs_t_by_dve")
        pta_s = sem("probs_t_by_act")
        pv_ps = sem("pv_in_psum")
        ot_s = sem("out_t_ready")
        ob_ps = sem("out_back_in_psum")
        rec_s = sem("softmax_reciprocal")
        on_s = sem("out_normed")
        o2_ps = sem("out_normed_t_in_psum")
        oth_s = sem("out_hi")
        otl_s = sem("out_lo")
        y_ps = sem("attn1_out_in_psum")
        yt_s = sem("attn1_tile_added")

        block = ctx.enter_context(nc.Block())

        plan, f0, f1, a0n = [], 0, 0, 0
        for s, kind in enumerate(stages):
            plan.append((kind, 2 * s, {"ffn0": f0, "ffn1": f1, "attn0": a0n, "attn1": 0}[kind]))
            f0 += 2 * (kind == "ffn0")
            f1 += 2 * (kind == "ffn1")
            a0n += 4 * (kind == "attn0")
        routed = {}
        for kind, p, k in plan:
            if kind.startswith("ffn"):
                for b in range(2):
                    routed[kind, k + b] = len(routed)
        def zt_count(p):
            return sum(1 for kind, q, k in plan if kind != "attn0" for b in range(2) if q + b <= p)

        last_ffn0 = max(p for kind, p, _ in plan if kind == "ffn0")
        TK = 11

        @block.sync
        def _(sp):
            for b in range(2):
                sp.dma_start(x[:, BT * b:BT * (b + 1), :],
                             x_in[BLK * b:BLK * (b + 1), :].rearrange("(t p) d -> p t d", p=P)).then_inc(x_in_s, 16)
            sp.dma_start(pre_c[:, :, :], pre).then_inc(const_s, 16)
            for u in range(U0 + U1):
                if u >= NST:
                    sp.wait_ge(w_lo, u - NST + 1)
                src, n = (w0[u], 3 * D) if u < U0 else (w1[u - U0], 2 * D)
                sp.dma_start(stage[:, u % NST, 0:n], src).then_inc(stage_s[u % NST], 16)
            if "attn1" in stages:
                sp.wait_ge(x_s, last_ffn0 + 2)
                sp.dma_start(wa_raw, wa).then_inc(wa_s, 16)
                sp.dma_start(sel_raw, sel_in.rearrange("p a b c -> p (a b c)")).then_inc(wa_s, 16)
                sp.dma_start(bias[:, :], bias_in).then_inc(wa_s, 16)
            for b in range(2):
                sp.wait_ge(x_s, 2 * (len(stages) - 1) + b + 1)
                sp.dma_start(out[BLK * b:BLK * (b + 1), :].rearrange("(t p) d -> p t d", p=P),
                             x[:, BT * b:BT * (b + 1), :]).then_inc(out_s, 16)
            sp.wait_ge(out_s, 32)

        @block.gpsimd
        def _(pool):
            nc.gpsimd.memset(half[:, :], -0.5).then_inc(setup_pool, 1)
            pool.wait_ge(setup_pool, 1)
            state = {"rms": 0}

            def ln_scale(kind, p):
                if kind == "ffn0":
                    mul, add = 1.0 + RMS_EPS, RMS_EPS * LN_EPS
                else:
                    mul, add = 1.0, LN_EPS
                pool.wait_ge(mv_s, p + 1)
                if p:
                    pool.wait_ge(zs_s, p)
                nc.gpsimd.tensor_scalar(zs_e[:, :], mv[:, :, 1], mul, add, ALU.mult, ALU.add).then_inc(zse_s, 1)
                pool.wait_ge(zse_s, p + 1)
                if p:
                    pool.wait_ge(z_s, p)
                nc.gpsimd.tensor_tensor(zs[:, :], zs_e[:, :], half[:, :], ALU.pow).then_inc(zs_s, 1)

            def rms(i, squares, ready, fb, mul, add):
                pool.wait_ge(squares, fb + 1)
                nc.gpsimd.tensor_scalar(ssq_e[:, i, :], ssq[:, i, :], mul, add, ALU.mult, ALU.add).then_inc(rms_e_s, 1)
                state["rms"] += 1
                pool.wait_ge(rms_e_s, state["rms"])
                nc.gpsimd.tensor_tensor(rinv[:, i, :], ssq_e[:, i, :], half[:, :], ALU.pow).then_inc(ready, 1)

            for kind, p, k in plan:
                ln_scale(kind, p)
                if kind == "ffn0":
                    for b in range(2):
                        rms(0, dsq_s, rd_s, k + b, 1.0 / D, RMS_EPS)
                        if b == 0:
                            ln_scale(kind, p + 1)
                        rms(1, msq_s, rm_s, k + b, 1.0 / D, RMS_EPS)
                        rms(2, csq_s, rc_s, k + b, 4.0 / D, 4.0 * RMS_EPS)
                else:
                    ln_scale(kind, p + 1)
                if kind == "ffn1" and k == 0 and "attn1" in stages:
                    pool.wait_ge(wa_s, 48)
                    nc.gpsimd.tensor_copy(sel[:, :, :, :].rearrange("p a b c -> p (a b c)"), sel_raw).then_inc(wal_s, 1)
                    pool.wait_ge(wah_s, 1)
                    nc.gpsimd.tensor_tensor(wa_l[:, :], wa_raw, wa_h[:, :].bitcast(F32), ALU.subtract)\
                      .then_inc(wal_s, 1)
                    pool.wait_ge(wal_s, 2)
                    nc.gpsimd.memset(va[:, :, :, :], 0.0).then_inc(wal_s, 1)
                    pool.wait_ge(wal_s, 3)
                    nc.gpsimd.memset(va[:, :, :, HD:HD + 1], 1.0).then_inc(wal_s, 1)

        @block.tensor
        def _(pe):
            def split3(o, lh, ll, rh, rl, start, stop, **kw):
                pe.matmul(o, lh, rh, start=start, stop=False, **kw)
                pe.matmul(o, ll, rh, start=False, stop=False, **kw)
                return pe.matmul(o, lh, rl, start=False, stop=stop, **kw)

            def transposes(p):
                pe.wait_ge(z_s, p + 1)
                if p == 0:
                    pe.wait_ge(const_s, 16 * N_SETUP)
                for kc in range(KC):
                    for t in range(BT):
                        mm = pe.transpose(ps[:, kc, t * P:(t + 1) * P], z[:, t, kc * P:(kc + 1) * P], ident[:, :])
                mm.then_inc(zt_s, 1)

            def logits_t(which, bank, first):
                if first:
                    pe.wait_ge(wr_split, 1)
                for kc in range(KC):
                    mm = split3(ps[:, bank, :], wr_h[:, which, kc, :], wr_l[:, which, kc, :],
                                zh[:, kc, :], zl[:, kc, :], kc == 0, kc == KC - 1)
                mm.then_inc(lgt_ps_s, 1)

            def logits(bank, n):
                pe.wait_ge(lgt_s, n + 1)
                for t in range(BT):
                    mm = pe.transpose(ps[:, bank, t * E:(t + 1) * E], lgt[:, t * P:(t + 1) * P], ident[0:E, 0:E])
                mm.then_inc(lg_ps_s, 1)

            def ffn0(p, k):
                for b in range(2):
                    for c in range(U0):
                        n, fb = U0 * (k + b) + c, k + b
                        if c == 0:
                            if fb:
                                pe.wait_ge(prod_s, n)
                            transposes(p + b)
                            if b:
                                down0(n - LAG)
                            pe.wait_ge(zh_s, zt_count(p + b))
                            pe.wait_ge(zl_s, zt_count(p + b))
                        if fb == 0:
                            pe.wait_ge(w_hi, c + 1)
                            pe.wait_ge(w_lo, c + 1)
                        if n >= 2:
                            pe.wait_ge(prod_s, n - 1)
                        for g in range(2):
                            for kc in range(KC):
                                mm = split3(ps[:, 2 * (n % 2) + g, :], w0u_h[:, c, kc, g, :], w0u_l[:, c, kc, g, :],
                                            zh[:, kc, :], zl[:, kc, :], kc == 0, kc == KC - 1)
                        mm.then_inc(gu_s, 1)
                        if c == 1:
                            if fb:
                                pe.wait_ge(acc_s, E * fb - 1)
                            logits_t(0, 6, fb == 0)
                        if c == 3:
                            logits(6, routed["ffn0", fb])
                        if c >= LAG or (b and c):
                            down0(n - LAG)
                for i in range(LAG):
                    down0(U0 * (k + 2) - LAG + i)

            def down0(n):
                fb, c = divmod(n, U0)
                pe.wait_ge(ah_s, n + 1)
                pe.wait_ge(al_s, n + 1)
                if c == 0 and fb:
                    pe.wait_ge(acc_s, E * fb)
                if c == J0:
                    pe.wait_ge(tk, TK * routed["ffn0", fb] + 1)
                if c == J0 + 1:
                    pe.wait_ge(dn_s, fb + 1)
                if c >= J0 + 2:
                    pe.wait_ge(acc_s, E * fb + c - J0 - 1)
                base = 4 if c < J0 or (c - J0) % 2 else 6
                for t in range(BT):
                    o = ps[:, base + t // 2, (t % 2) * D:(t % 2 + 1) * D]
                    start = (c == 0 and t % 2 == 0) if c < J0 else True
                    mm = split3(o, ah[:, n % 2, t * P:(t + 1) * P], al[:, n % 2, t * P:(t + 1) * P],
                                w0d_h[:, c, :], w0d_l[:, c, :], start, c >= J0 - 1, skip_group_check=c < J0)
                mm.then_inc(down_s, 1)

            def ffn1(p, k):
                for b in range(2):
                    for c in range(U1):
                        n, fb = U1 * (k + b) + c, k + b
                        if c == 0:
                            if fb:
                                pe.wait_ge(al1_s, n)
                            transposes(p + b)
                            if b:
                                down1(n - LAG)
                            pe.wait_ge(zh_s, zt_count(p + b))
                            pe.wait_ge(zl_s, zt_count(p + b))
                            if fb:
                                pe.wait_ge(tk, TK * routed["ffn1", fb - 1] + 1)
                            logits_t(1, 3, not f0)
                        if fb == 0:
                            pe.wait_ge(w_hi, U0 + c + 1)
                            pe.wait_ge(w_lo, U0 + c + 1)
                        if n >= 3:
                            pe.wait_ge(al1_s, n - 2)
                        for kc in range(KC):
                            mm = split3(ps[:, n % 3, :], w1_h[:, c, kc * P:(kc + 1) * P], w1_l[:, c, kc * P:(kc + 1) * P],
                                        zh[:, kc, :], zl[:, kc, :], kc == 0, kc == KC - 1)
                        mm.then_inc(h1_s, 1)
                        if c == 1:
                            logits(3, routed["ffn1", fb])
                        if c >= LAG or (b and c):
                            down1(n - LAG)
                for i in range(LAG):
                    down1(U1 * (k + 2) - LAG + i)

            def down1(n):
                fb, c = divmod(n, U1)
                pe.wait_ge(al1_s, n + 1)
                if n >= 2:
                    pe.wait_ge(acc_s, E * f0 + n - 1)
                for t in range(BT):
                    mm = split3(ps[:, 4 + 2 * (n % 2) + t // 2, (t % 2) * D:(t % 2 + 1) * D],
                                ah[:, n % 2, t * P:(t + 1) * P], al[:, n % 2, t * P:(t + 1) * P],
                                w1_h[:, c, D:], w1_l[:, c, D:], True, True)
                mm.then_inc(down1_s, 1)

            def attn1(p, k):
                for b in range(2):
                    transposes(p + b)
                    pe.wait_ge(wal_s, 4)
                    pe.wait_ge(zh_s, zt_count(p + b))
                    pe.wait_ge(zl_s, zt_count(p + b))
                    for m in range(2):
                        for kc in range(KC):
                            w = W_Q + kc * D + m * P
                            mm = split3(ps[:, 2 + m, :], wa_h[:, w:w + P], wa_l[:, w:w + P], zh[:, kc, :], zl[:, kc, :],
                                        kc == 0, kc == KC - 1)
                        mm.then_inc(q_ps, 1)
                    for kc in range(KC):
                        w = W_C + kc * P
                        mm = split3(ps[:, 4, :], wa_h[:, w:w + P], wa_l[:, w:w + P], zh[:, kc, :], zl[:, kc, :],
                                    kc == 0, kc == KC - 1)
                    mm.then_inc(c_ps, 1)
                    for s in range(4):
                        stack(b, s)
                    pe.wait_ge(ch_s, b + 1)
                    pe.wait_ge(cl_s, b + 1)
                    for m in range(2):
                        w = W_K + m * P
                        split3(ps[:, 5 + m, :], wa_h[:, w:w + P], wa_l[:, w:w + P], ch[:, :], cl[:, :], True, True)\
                            .then_inc(k_ps, 1)
                    for t in range(BT):
                        mm = split3(ps[:, 7 * (1 - t // 2), (t % 2) * D:(t % 2 + 1) * D], ch[:, t * P:(t + 1) * P],
                                    cl[:, t * P:(t + 1) * P], wa_h[:, W_V:W_V + D], wa_l[:, W_V:W_V + D], True, True)
                    mm.then_inc(v_ps, 1)
                    for s in range(4, HEADS):
                        stack(b, s)
                    pe.wait_ge(sta_s, 8 * (b + 1))
                    pe.wait_ge(std_s, 8 * (b + 1))
                    pe.wait_ge(v_s, b + 1)
                    for hb in range(2 * HEADS):
                        hd = 2 * HEADS * b + hb
                        scores(hd)
                        if hb >= 1:
                            probs_turn(hd - 1)
                        if hb % 4 == 3 and hb >= 7:
                            pv(hd // 4 - 1)
                        if hb >= HEADS + 4:
                            out_steps(2 * b, hb - HEADS - 4)
                    probs_turn(2 * HEADS * (b + 1) - 1)
                    pv(8 * (b + 1) - 1)
                    for i in range(12):
                        out_steps(2 * b + 1, i)

            def stack(b, s):
                half, i = divmod(s, HEADS // 2)
                m, pair = divmod(i, 4)
                if half == 0:
                    pe.wait_ge(qh_s, 2 * b + m + 1)
                    pe.wait_ge(ql_s, 2 * b + m + 1)
                else:
                    pe.wait_ge(kh_s, 2 * b + m + 1)
                    pe.wait_ge(kl_s, 2 * b + m + 1)
                if s == 2:
                    pe.wait_ge(ql_s, 2 * b + 2)
                if s == 3:
                    pe.wait_ge(cl_s, b + 1)
                if s >= 4:
                    done = (HEADS * b + s - 4) // 2 + 1
                    pe.wait_ge(std_s if s % 2 else sta_s, done)
                hi, lo = (qh, ql) if half == 0 else (kh, kl)
                pe.matmul(ps[:, 1 + s % 4, :], sel[:, 2 * half, pair, :], hi[:, m, :], start=True, stop=False)
                pe.matmul(ps[:, 1 + s % 4, :], sel[:, 2 * half + 1, pair, :], lo[:, m, :], start=False, stop=True)\
                  .then_inc(st_ps, 1)

            def scores(hd):
                t0, h = (hd // HEADS % 2) * SEQ, hd % HEADS
                r0, r1 = STEP * (h % 2), STEP * (h % 2) + ROWS
                if hd >= 3:
                    pe.wait_ge(exp_s, hd - 2)
                pe.matmul(ps[:, hd % 3, 0:P], qs[r0:r1, h // 2, t0:t0 + P], ks[r0:r1, h // 2, t0:t0 + P],
                          start=True, stop=True)
                pe.matmul(ps[:, hd % 3, P:3 * P], qs[r0:r1, h // 2, t0 + P:t0 + 2 * P],
                          ks[r0:r1, h // 2, t0:t0 + 2 * P], start=True, stop=True).then_inc(s_ps, 1)

            def probs_turn(hd):
                pe.wait_ge(exp_s, hd + 1)
                if hd >= 2:
                    if (hd - 2) % 4 == 3:
                        pe.wait_ge(pta_s, (hd - 2) // 4 + 1)
                    else:
                        pe.wait_ge(ptd_s, 3 * ((hd - 2) // 4) + (hd - 2) % 4 + 1)
                for c in range(3):
                    mm = pe.transpose(ps[:, 3 + hd % 2, c * P:(c + 1) * P], pb[:, hd % 3, c * P:(c + 1) * P],
                                      ident[:, :])
                mm.then_inc(t_ps, 1)

            def pv(g):
                n, gi = divmod(g, 4)
                pe.wait_ge(ptd_s, 3 * (g + 1))
                pe.wait_ge(pta_s, g + 1)
                if g >= 2:
                    pe.wait_ge(ot_s, g - 1)
                for c in range(2):
                    for j in range(4):
                        o = ps[SLOT * j:SLOT * (j + 1), 5 + g % 2, c * P:SEQ]
                        mm = pe.matmul(o, va[:, 2 * (n % 2) + c, 4 * gi + j, :],
                                       pbt[:, g % 2, j, c * SEQ:SEQ + c * P], start=c == 0, stop=c == 1,
                                       skip_group_check=True, tile_position=(0, SLOT * j))
                mm.then_inc(pv_ps, 1)

            def out_steps(n, i):
                t = int(i >= 6)
                if i == 6 * t:
                    pe.wait_ge(ot_s, 4 * (n + 1))
                    if n or t:
                        pe.wait_ge(yt_s, 2 * n + t)
                    else:
                        pe.wait_ge(v_s, 1)
                    for g in range(4):
                        mm = pe.transpose(ps[:, 7, g * P:(g + 1) * P], ot[n % 2][:, g, t * P:(t + 1) * P], ident[:, :])
                    mm.then_inc(ob_ps, 1)
                if i == 6 * t + 2:
                    pe.wait_ge(on_s, 2 * n + t + 1)
                    for kc in range(KC):
                        mm = pe.transpose(ps[:, 7, kc * P:(kc + 1) * P], on[:, t, kc * P:(kc + 1) * P], ident[:, :])
                    mm.then_inc(o2_ps, 1)
                if i == 6 * t + 4:
                    pe.wait_ge(oth_s, 2 * n + t + 1)
                    pe.wait_ge(otl_s, 2 * n + t + 1)
                    for kc in range(KC):
                        w = W_O + kc * D
                        mm = split3(ps[:, 7, 0:D], oth[:, t, kc, :], otl[:, t, kc, :], wa_h[:, w:w + D], wa_l[:, w:w + D],
                                    kc == 0, kc == KC - 1)
                    mm.then_inc(y_ps, 1)

            def attn0(p, k):
                pe.wait_ge(const_s, 16 * N_SETUP)
                pe.wait_ge(x_s, p)
                pe.matmul(ps[0:SA, 7, 0:SA], a0[:, 2 * SA:3 * SA], a0[:, SA:2 * SA], start=True, stop=True)\
                  .then_inc(pt_ps_s, 1)
                for q in range(4):
                    s, n = q % 2, k + q
                    t0 = 2 * (q % 2)
                    pe.wait_ge(z_s, p + q // 2 + 1)
                    pe.wait_ge(a0_set, 3)
                    if q >= 2:
                        pe.wait_ge(mt_s, n - 1)
                        pe.wait_ge(px_s, n - 1)
                    for c in range(2):
                        for t in range(2):
                            pe.matmul(ps[:, s, c * D + t * P:c * D + (t + 1) * P], z[:, t0 + t, c * P:(c + 1) * P],
                                      m0[:, t, :], start=True, stop=True)
                    pe.matmul(ps[0:SA, 2 + s, 0:D], pt[:, :], z[0:SA, t0, :], start=True, stop=True)\
                      .then_inc(mt_ps_s, 1)
                    pe.wait_ge(px_s, n + 1)
                    if q >= 2:
                        pe.wait_ge(att_s, n - 1)
                    for c in range(2):
                        mm = pe.matmul(ps[:, 4 + s, c * D:(c + 1) * D], z[0:SA, t0, c * P:(c + 1) * P],
                                       pxs[:, s, :], start=True, stop=True)
                    mm.then_inc(sc_ps_s, 1)
                    pe.wait_ge(mt_s, n + 1)
                    pe.wait_ge(attz_s, n + 1)
                    if q == 2:
                        pe.wait_ge(upd_s, n // 2)
                    if q == 3:
                        pe.wait_ge(x_s, p + 1)
                    for dt in range(2):
                        for c in range(2):
                            mm = pe.matmul(ps[:, 6 + s, dt * D:(dt + 1) * D], mt[:, s, c, dt * P:(dt + 1) * P],
                                           att[:, s, c, :], start=c == 0, stop=c == 1)
                    mm.then_inc(o0_s, 1)

            for kind, p, k in plan:
                {"ffn0": ffn0, "ffn1": ffn1, "attn0": attn0, "attn1": attn1}[kind](p, k)

        @block.scalar
        def _(act):
            def weights_hi(u):
                act.wait_ge(stage_s[u % NST], 16 * (u // NST + 1))
                raw = stage[:, u % NST, :]
                if u < U0:
                    if u == 0:
                        act.wait_ge(const_s, 16 * N_SETUP)
                    for kc in range(KC):
                        nc.scalar.activation(w0u_h[:, u, kc, :, :], raw[:, kc * D:(kc + 1) * D], ACT.Copy,
                                             scale=pre_c[:, int(u >= J0), kc:kc + 1])
                    nc.scalar.activation(w0d_h[:, u, :], raw[:, 2 * D:3 * D], ACT.Copy).then_inc(w_hi, 1)
                else:
                    nc.scalar.activation(w1_h[:, u - U0, :], raw[:, 0:2 * D], ACT.Copy).then_inc(w_hi, 1)

            def z_hi(p):
                act.wait_ge(zt_s, zt_count(p))
                for kc in range(KC):
                    a = nc.scalar.activation(zh[:, kc, :], ps[:, kc, :], ACT.Copy)
                a.then_inc(zh_s, 1)

            def squares(i, src, wait, before, done, fb):
                act.wait_ge(*wait)
                if before[1]:
                    act.wait_ge(*before)
                for t in range(BT):
                    a = nc.scalar.activation(sq[:, t, :], src(t), ACT.Square, accum_out=ssq[:, i, t:t + 1])
                a.then_inc(done, 1)

            def exps(n):
                act.wait_ge(lsh_s, n + 1)
                nc.scalar.activation(lex[:, :, :], lsh[:, :, :], ACT.Exp).then_inc(lex_s, 1)

            def gelu(n):
                act.wait_ge(gu_s, n + 1)
                if n >= 2:
                    act.wait_ge(prod_s, n - 1)
                nc.scalar.activation(gel[:, n % 2, :], ps[:, 2 * (n % 2), :], ACT.Gelu_apprx_tanh).then_inc(gelu_s, 1)

            def act_hi(n):
                act.wait_ge(prod_s, n + 1)
                if n >= 2:
                    act.wait_ge(down_s, n - 1)
                nc.scalar.activation(ah[:, n % 2, :], act32[:, n % 2, :], ACT.Copy).then_inc(ah_s, 1)

            def moe_squares(fb):
                squares(1, lambda t: macc[:, t, :], (acc_s, E * (fb + 1)), (dsq_s, fb + 1), msq_s, fb)

            def sum_squares(fb):
                squares(2, lambda t: comb[:, t, :], (comb_s, fb + 1), (msq_s, fb + 1), csq_s, fb)

            def ffn0(p, k):
                for b in range(2):
                    for c in range(U0):
                        n, fb = U0 * (k + b) + c, k + b
                        if c == 0:
                            z_hi(p + b)
                        if fb == 0 and c + 2 < U0:
                            weights_hi(c + 2)
                        if fb == 1 and c < U1:
                            weights_hi(U0 + c)
                        gelu(n)
                        if c or b:
                            act_hi(n - 1)
                        if b and c == 3:
                            moe_squares(fb - 1)
                        if b and c == 5:
                            sum_squares(fb - 1)
                        if c == 6:
                            exps(routed["ffn0", fb])
                        if c == J0 + 1:
                            squares(0, lambda t: ps[:, 4 + t // 2, (t % 2) * D:(t % 2 + 1) * D],
                                    (down_s, U0 * fb + J0), (csq_s, fb), dsq_s, fb)
                act_hi(U0 * (k + 2) - 1)
                moe_squares(k + 1)
                sum_squares(k + 1)

            def ffn1(p, k):
                for b in range(2):
                    for c in range(U1):
                        n, fb = U1 * (k + b) + c, k + b
                        if c == 0:
                            z_hi(p + b)
                        act.wait_ge(h1_s, n + 1)
                        if n >= 2:
                            act.wait_ge(down1_s, n - 1)
                        nc.scalar.activation(ah[:, n % 2, :], ps[:, n % 3, :], ACT.Relu).then_inc(ah1_s, 1)
                        if c == 2:
                            exps(routed["ffn1", fb])
                        if fb == 1 and c == 3 and "attn1" in stages:
                            act.wait_ge(wa_s, 48)
                            nc.scalar.activation(wa_h[:, :], wa_raw, ACT.Copy).then_inc(wah_s, 1)

            def attn1(p, k):
                for b in range(2):
                    z_hi(p + b)
                    for m in range(2):
                        act.wait_ge(q_ps, 2 * b + m + 1)
                        nc.scalar.activation(qh[:, m, :], ps[:, 2 + m, :], ACT.Copy, scale=-(HD ** -0.5))\
                          .then_inc(qh_s, 1)
                    act.wait_ge(c_ps, b + 1)
                    nc.scalar.activation(ch[:, :], ps[:, 4, :], ACT.Copy).then_inc(ch_s, 1)
                    for m in range(2):
                        act.wait_ge(k_ps, 2 * b + m + 1)
                        nc.scalar.activation(kh[:, m, :], ps[:, 5 + m, :], ACT.Copy).then_inc(kh_s, 1)
                    for s in range(0, HEADS, 2):
                        act.wait_ge(st_ps, HEADS * b + s + 1)
                        dst = (qs if s < HEADS // 2 else ks)[:, s % (HEADS // 2), :]
                        nc.scalar.activation(dst, ps[:, 1 + s % 4, :], ACT.Copy).then_inc(sta_s, 1)
                    for hb in range(2 * HEADS):
                        hd = 2 * HEADS * b + hb
                        act.wait_ge(sm_s, hd + 1)
                        if hd >= 3:
                            act.wait_ge(t_ps, hd - 2)
                        nc.scalar.activation(pb[:, hd % 3, 0:P], ps[:, hd % 3, 0:P], ACT.Exp,
                                             bias=nmin[:, hd % 4, 0:1], scale=-1.0)
                        nc.scalar.activation(pb[:, hd % 3, P:3 * P], ps[:, hd % 3, P:3 * P], ACT.Exp,
                                             bias=nmin[:, hd % 4, 1:2], scale=-1.0).then_inc(exp_s, 1)
                        if hb % 4 == 1 and hb >= 5:
                            probs_t(hd - 2)
                        if hb % 4 == 3 and hb >= 7:
                            out_t(hd // 4 - 1)
                        if hb == HEADS + 7:
                            out_hi(2 * b)
                        if hb == HEADS + 13:
                            out_hi(2 * b, 1)
                    probs_t(2 * HEADS * (b + 1) - 1)
                    out_t(8 * (b + 1) - 1)
                    out_hi(2 * b + 1)
                    out_hi(2 * b + 1, 1)

            def probs_t(hd):
                act.wait_ge(t_ps, hd + 1)
                if hd >= 8:
                    act.wait_ge(pv_ps, hd // 4 - 1)
                nc.scalar.activation(pbt[:, hd // 4 % 2, hd % 4, :], ps[:, 3 + hd % 2, 0:3 * P], ACT.Copy)\
                  .then_inc(pta_s, 1)

            def out_t(g):
                act.wait_ge(pv_ps, g + 1)
                if g >= 8:
                    act.wait_ge(ob_ps, 2 * (g // 4 - 1))
                nc.scalar.activation(ot[g // 4 % 2][:, g % 4, :], ps[:, 5 + g % 2, 0:SEQ], ACT.Copy).then_inc(ot_s, 1)

            def out_hi(n, t=0):
                act.wait_ge(o2_ps, 2 * n + t + 1)
                nc.scalar.activation(oth[:, t, :, :].rearrange("p c q -> p (c q)"), ps[:, 7, 0:D], ACT.Copy)\
                  .then_inc(oth_s, 1)

            def attn0(p, k):
                for q in range(4):
                    s, n = q % 2, k + q
                    act.wait_ge(mt_ps_s, n + 1)
                    if q >= 2:
                        act.wait_ge(o0_s, n - 1)
                    nc.scalar.activation(mt[:, s, :, :], ps[:, s, :], ACT.Copy).then_inc(mt_s, 1)
                    act.wait_ge(sc_ps_s, n + 1)
                    nc.scalar.activation(att[:, s, :, :], ps[:, 4 + s, :], ACT.Relu).then_inc(att_s, 1)

            act.dma_start(ident[:, :], ident_in).then_inc(const_s, 16)
            act.dma_start(wr_raw[:, :, :, :], wr).then_inc(const_s, 16)
            act.dma_start(post_b[:, :], posts.partition_broadcast(P)).then_inc(const_s, 16)
            act.dma_start(iota_b[:, :], iota_in.partition_broadcast(P)).then_inc(const_s, 16)
            act.dma_start(a0[:, :], att0).then_inc(const_s, 16)
            act.dma_start(r0c[:, :], r0.partition_broadcast(P)).then_inc(const_s, 16)
            act.dma_start(cap_c[:, :], cap_in).then_inc(const_s, 16)
            if "ffn0" in stages:
                weights_hi(0)
                weights_hi(1)
            for kind, p, k in plan:
                {"ffn0": ffn0, "ffn1": ffn1, "attn0": attn0, "attn1": attn1}[kind](p, k)

        @block.vector
        def _(dve):
            steps = {"tk": 0}
            step = sem("setup_dve")
            V = nc.vector

            def weights_lo(u):
                dve.wait_ge(w_hi, u + 1)
                raw = stage[:, u % NST, :]
                if u < U0:
                    for kc in range(KC):
                        V.scalar_tensor_tensor(w0u_l[:, u, kc, :, :].rearrange("p g m -> p (g m)"), raw[:, kc * D:(kc + 1) * D],
                                               pre_c[:, int(u >= J0), kc:kc + 1],
                                               w0u_h[:, u, kc, :, :].rearrange("p g m -> p (g m)").bitcast(F32),
                                               ALU.mult, ALU.subtract)
                    V.tensor_tensor(w0d_l[:, u, :], raw[:, 2 * D:3 * D], w0d_h[:, u, :].bitcast(F32),
                                    ALU.subtract).then_inc(w_lo, 1)
                else:
                    V.tensor_tensor(w1_l[:, u - U0, :], raw[:, 0:2 * D], w1_h[:, u - U0, :].bitcast(F32),
                                    ALU.subtract).then_inc(w_lo, 1)

            def router_weights():
                dve.wait_ge(const_s, 16 * N_SETUP)
                V.memset(wr_h[:, :, :, :].bitcast(F32), 0.0)
                V.memset(wr_l[:, :, :, :].bitcast(F32), 0.0).then_inc(step, 1)
                dve.wait_ge(step, 1)
                for kc in range(KC):
                    V.tensor_scalar(wr_raw[:, 0, kc, :], wr_raw[:, 0, kc, :], pre_c[:, 2, kc:kc + 1], ROOT,
                                    ALU.mult, ALU.mult).then_inc(step, 1)
                dve.wait_ge(step, 1 + KC)
                V.tensor_copy(wr_h[:, :, :, 0:E], wr_raw[:, :, :, :]).then_inc(step, 1)
                dve.wait_ge(step, 2 + KC)
                V.tensor_tensor(wr_l[:, :, :, 0:E], wr_raw[:, :, :, :], wr_h[:, :, :, 0:E].bitcast(F32),
                                ALU.subtract).then_inc(wr_split, 1)

            def ln_stats(p, p_first):
                b = p % 2
                if p < 2:
                    dve.wait_ge(x_in_s, 32)
                else:
                    dve.wait_ge(x_s, p - 1)
                for t in range(BT):
                    i = V.bn_stats(bn[:, t, :], x[:, BT * b + t, :])
                i.then_inc(bn_s, 1)
                dve.wait_ge(bn_s, p + 1)
                if p:
                    dve.wait_ge(z_s, p)
                for t in range(BT):
                    i = V.bn_aggr(mv[:, t, :], bn[:, t, :])
                i.then_inc(mv_s, 1)

            def normalise(p, z_free):
                b = p % 2
                dve.wait_ge(zs_s, p + 1)
                for s, v in z_free:
                    dve.wait_ge(s, v)
                for t in range(BT):
                    i = V.tensor_scalar(z[:, t, :], x[:, BT * b + t, :], mv[:, t, 0:1], zs[:, t:t + 1],
                                        ALU.subtract, ALU.mult)
                i.then_inc(z_s, 1)

            def z_lo(p):
                dve.wait_ge(zh_s, zt_count(p))
                for kc in range(KC):
                    i = V.tensor_tensor(zl[:, kc, :], ps[:, kc, :], zh[:, kc, :].bitcast(F32), ALU.subtract)
                i.then_inc(zl_s, 1)

            def logits_t_out(n, bank):
                dve.wait_ge(lgt_ps_s, n + 1)
                V.tensor_copy(lgt[:, :], ps[0:E, bank, :]).then_inc(lgt_s, 1)

            def tstep(i):
                i.then_inc(tk, 1)
                steps["tk"] += 1

            def tdone():
                dve.wait_ge(tk, steps["tk"])

            def shift_logits(n, bank, top):
                dve.wait_ge(lg_ps_s, n + 1)
                tstep(V.tensor_copy(lg[:, :, :].rearrange("p t e -> p (t e)"), ps[:, bank, 0:BT * E]))
                tdone()
                for t in range(BT):
                    i = V.max(mx[:, t, :], lg[:, t, :])
                tstep(i)
                tdone()
                V.tensor_tensor(lsh[:, :, :], lg[:, :, :], mx[:, :, 0:1].broadcast_to([P, BT, E]),
                                ALU.subtract).then_inc(lsh_s, 1)
                for t in range(BT):
                    i = V.max_index(mi[:, t, :], mx[:, t, :], lg[:, t, :])
                tstep(i)
                tdone()
                tstep(V.tensor_copy(mif[:, :, :], mi[:, :, :]))
                tdone()
                for r in range(top):
                    i = V.tensor_tensor(eq[:, :, :, r], iota_b[:, :].rearrange("p (t e) -> p t e", t=BT),
                                        mif[:, :, r:r + 1].broadcast_to([P, BT, E]), ALU.is_equal)
                tstep(i)
                tdone()
                tstep(V.tensor_reduce(selm[:, :, :], eq[:, :, :, 0:top], AX.X, ALU.add))

            def expert_weights(n, kind, slot):
                dve.wait_ge(lex_s, n + 1)
                tdone()
                tstep(V.tensor_tensor(em[:, :, :], lex[:, :, :], selm[:, :, :], ALU.mult))
                tdone()
                tstep(V.tensor_reduce(esum[:, :], em[:, :, :], AX.X, ALU.add))
                tdone()
                tstep(V.reciprocal(erec[:, :], esum[:, :]))
                tdone()
                tstep(V.tensor_tensor(gs[:, :, :], em[:, :, :], erec[:, :].rearrange("p (t o) -> p t o", o=1)
                                      .broadcast_to([P, BT, E]), ALU.mult))
                tdone()
                if kind == "ffn0":
                    pes = post_b[:, 3 * D:3 * D + E].rearrange("p (o e) -> p o e", o=1).broadcast_to([P, BT, E])
                    tstep(V.tensor_tensor(aff[:, slot, :, :], gs[:, :, :], pes, ALU.mult))
                else:
                    V.tensor_scalar(gs1[:, :, :], gs[:, :, :], 1.0, None, ALU.add).then_inc(step, 1)
                    steps["f1"] = steps.get("f1", 0) + 1
                    dve.wait_ge(step, 2 + KC + 2 * steps["f1"] - 1)
                    V.tensor_tensor(gs1[:, :, :], gs1[:, :, :], gs[:, :, :], ALU.subtract).then_inc(step, 1)
                    dve.wait_ge(step, 2 + KC + 2 * steps["f1"])
                    tstep(V.tensor_tensor(aff[:, slot, :, :], gs1[:, :, :], selm[:, :, :], ALU.mult))
                assert steps["tk"] == TK * (n + 1)

            def accumulate(ready, count, total, e, base, slot, n_tk):
                dve.wait_ge(ready, count)
                if e == 0:
                    dve.wait_ge(tk, n_tk)
                if total:
                    dve.wait_ge(acc_s, total)
                for t in range(BT):
                    o = ps[:, base + t // 2, (t % 2) * D:(t % 2 + 1) * D]
                    a = aff[:, slot, t, e:e + 1]
                    if e == 0:
                        i = V.tensor_scalar(macc[:, t, :], o, a, None, ALU.mult)
                    else:
                        i = V.scalar_tensor_tensor(macc[:, t, :], o, a, macc[:, t, :], ALU.mult, ALU.add)
                i.then_inc(acc_s, 1)

            def acc0(n):
                fb, c = divmod(n, U0)
                if c < J0:
                    return
                e = c - J0
                if e == 0 and fb:
                    dve.wait_ge(mn_s, fb)
                accumulate(down_s, n + 1, E * fb + e, e, 6 if e % 2 == 0 else 4, fb % 2,
                           TK * (routed["ffn0", fb] + 1))

            def product(n):
                dve.wait_ge(gelu_s, n + 1)
                if n >= 2:
                    dve.wait_ge(ah_s, n - 1)
                    dve.wait_ge(al_s, n - 1)
                V.tensor_tensor(act32[:, n % 2, :], gel[:, n % 2, :], ps[:, 2 * (n % 2) + 1, :], ALU.mult)\
                 .then_inc(prod_s, 1)

            def act_lo(n):
                dve.wait_ge(ah_s, n + 1)
                if n >= 2:
                    dve.wait_ge(down_s, n - 1)
                V.tensor_tensor(al[:, n % 2, :], act32[:, n % 2, :], ah[:, n % 2, :].bitcast(F32), ALU.subtract)\
                 .then_inc(al_s, 1)

            def dense_norm(fb):
                dve.wait_ge(rd_s, fb + 1)
                if fb:
                    dve.wait_ge(fin_s, fb)
                for t in range(BT):
                    i = V.scalar_tensor_tensor(comb[:, t, :], ps[:, 4 + t // 2, (t % 2) * D:(t % 2 + 1) * D],
                                               rinv[:, 0, t:t + 1], post_b[:, 0:D], ALU.mult, ALU.mult)
                i.then_inc(dn_s, 1)

            def moe_norm(fb):
                dve.wait_ge(rm_s, fb + 1)
                dve.wait_ge(dn_s, fb + 1)
                if fb:
                    dve.wait_ge(x_s, x_count(fb - 1))
                for t in range(BT):
                    i = V.scalar_tensor_tensor(tmp[:, t, :], macc[:, t, :], rinv[:, 1, t:t + 1],
                                               post_b[:, D:2 * D], ALU.mult, ALU.mult)
                i.then_inc(mn_s, 1)
                dve.wait_ge(mn_s, fb + 1)
                V.tensor_tensor(comb[:, :, :], comb[:, :, :], tmp[:, :, :], ALU.add).then_inc(comb_s, 1)

            def finish0(fb, b):
                dve.wait_ge(rc_s, fb + 1)
                dve.wait_ge(comb_s, fb + 1)
                for t in range(BT):
                    i = V.scalar_tensor_tensor(tmp[:, t, :], comb[:, t, :], rinv[:, 2, t:t + 1],
                                               post_b[:, 2 * D:3 * D], ALU.mult, ALU.mult)
                i.then_inc(fin_s, 1)
                dve.wait_ge(fin_s, fb + 1)
                xb = x[:, BT * b:BT * (b + 1), :]
                V.tensor_tensor(xb, xb, tmp[:, :, :], ALU.add).then_inc(x_s, 1)

            def x_count(fb):
                p = [q + b for kind, q, k in plan if kind == "ffn0" for b in range(2) if k + b == fb][0]
                return p + 1

            def ffn0(p, k):
                for b in range(2):
                    for c in range(U0):
                        n, fb = U0 * (k + b) + c, k + b
                        if c == 0:
                            z_lo(p + b)
                        if fb == 0 and c + 2 < U0:
                            weights_lo(c + 2)
                        if fb == 1 and c < U1:
                            weights_lo(U0 + c)
                        product(n)
                        if c or b:
                            act_lo(n - 1)
                        if c >= 3 or b:
                            acc0(n - 3)
                        if c == 2:
                            logits_t_out(routed["ffn0", fb], 6)
                        if c == 4:
                            shift_logits(routed["ffn0", fb], 6, 2)
                        if c == 7:
                            expert_weights(routed["ffn0", fb], "ffn0", fb % 2)
                        if c == J0 + 2:
                            dense_norm(fb)
                        if b and c == 4:
                            moe_norm(fb - 1)
                        if b and c == 6:
                            finish0(fb - 1, 0)
                        if b == 0 and c == 12:
                            ln_stats(p + 1, p)
                        if b == 0 and c == 13:
                            normalise(p + 1, [(zt_s, zt_count(p + 1) - 1)])
                last = U0 * (k + 2)
                act_lo(last - 1)
                for i in (3, 2, 1):
                    acc0(last - i)
                moe_norm(k + 1)
                finish0(k + 1, 1)

            def ffn1(p, k):
                for b in range(2):
                    for c in range(U1):
                        n, fb = U1 * (k + b) + c, k + b
                        if c == 0:
                            z_lo(p + b)
                            logits_t_out(routed["ffn1", fb], 3)
                        dve.wait_ge(ah1_s, n + 1)
                        V.scalar_tensor_tensor(al[:, n % 2, :], ps[:, n % 3, :], 0.0, ah[:, n % 2, :].bitcast(F32),
                                               ALU.max, ALU.subtract).then_inc(al1_s, 1)
                        if c == 1:
                            shift_logits(routed["ffn1", fb], 3, 4)
                        if c >= 3 or b:
                            acc1(n - 3, b - (c < 3))
                        if c == 2:
                            expert_weights(routed["ffn1", fb], "ffn1", fb % 2)
                        if b == 0 and c == 4:
                            ln_stats(p + 1, p)
                        if b == 0 and c == 5:
                            normalise(p + 1, [(zt_s, zt_count(p + 1) - 1)])
                for i in (3, 2, 1):
                    acc1(U1 * (k + 2) - i, 1)

            def acc1(n, b):
                fb, e = divmod(n, U1)
                if e == 0 and (fb or f0):
                    dve.wait_ge(x_s, 1)
                accumulate(down1_s, n + 1, E * f0 + n, e, 4 + 2 * (n % 2), fb % 2, TK * (routed["ffn1", fb] + 1))
                if e == E - 1:
                    dve.wait_ge(acc_s, E * f0 + n + 1)
                    xb = x[:, BT * b:BT * (b + 1), :]
                    V.scalar_tensor_tensor(xb, macc[:, :, :], 0.5, xb, ALU.mult, ALU.add).then_inc(x_s, 1)

            def attn1(p, k):
                for b in range(2):
                    if b:
                        ln_stats(p + 1, p)
                        normalise(p + 1, [(zt_s, zt_count(p + 1) - 1)])
                    z_lo(p + b)
                    for m in range(2):
                        dve.wait_ge(qh_s, 2 * b + m + 1)
                        V.scalar_tensor_tensor(ql[:, m, :], ps[:, 2 + m, :], -(HD ** -0.5), qh[:, m, :].bitcast(F32),
                                               ALU.mult, ALU.subtract).then_inc(ql_s, 1)
                    dve.wait_ge(ch_s, b + 1)
                    V.tensor_tensor(cl[:, :], ps[:, 4, :], ch[:, :].bitcast(F32), ALU.subtract).then_inc(cl_s, 1)
                    for s in (1, 3):
                        stack_out(b, s)
                    for m in range(2):
                        dve.wait_ge(kh_s, 2 * b + m + 1)
                        V.tensor_tensor(kl[:, m, :], ps[:, 5 + m, :], kh[:, m, :].bitcast(F32), ALU.subtract)\
                         .then_inc(kl_s, 1)
                    dve.wait_ge(v_ps, b + 1)
                    for t in range(BT):
                        v = ps[:, 7 * (1 - t // 2), (t % 2) * D:(t % 2 + 1) * D].rearrange("p (h d) -> p h d", d=HD)
                        i = V.tensor_copy(va[:, t, :, 0:HD], v)
                    i.then_inc(v_s, 1)
                    for s in range(5, HEADS, 2):
                        stack_out(b, s)
                    for hb in range(2 * HEADS):
                        hd = 2 * HEADS * b + hb
                        bias_min(hd)
                        if hb >= 2 and (hd - 2) % 4 != 3:
                            probs_t(hd - 2)
                        if hb >= HEADS + 4:
                            out_steps(p, 2 * b, hb - HEADS - 4)
                    probs_t(2 * HEADS * (b + 1) - 2)
                    for i in range(12):
                        out_steps(p, 2 * b + 1, i)

            def stack_out(b, s):
                dve.wait_ge(st_ps, HEADS * b + s + 1)
                V.tensor_copy((qs if s < HEADS // 2 else ks)[:, s % (HEADS // 2), :], ps[:, 1 + s % 4, :])\
                 .then_inc(std_s, 1)

            def bias_min(hd):
                dve.wait_ge(s_ps, hd + 1)
                if hd >= 4:
                    dve.wait_ge(exp_s, hd - 3)
                if hd == 0:
                    dve.wait_ge(wa_s, 48)
                for c, (lo, hi) in enumerate(((0, P), (P, 3 * P))):
                    s = ps[:, hd % 3, lo:hi]
                    i = V.tensor_tensor_reduce(s, s, bias[:, lo:hi], 1.0, FAR, ALU.add, ALU.min,
                                               nmin[:, hd % 4, c:c + 1])
                i.then_inc(sm_s, 1)

            def probs_t(hd):
                dve.wait_ge(t_ps, hd + 1)
                if hd >= 8:
                    dve.wait_ge(pv_ps, hd // 4 - 1)
                V.tensor_copy(pbt[:, hd // 4 % 2, hd % 4, :], ps[:, 3 + hd % 2, 0:3 * P]).then_inc(ptd_s, 1)

            def out_steps(p, n, i):
                t, c = int(i >= 6), 2 * n + int(i >= 6) + 1
                if i == 6 * t + 1:
                    dve.wait_ge(ob_ps, c)
                    if c > 2:
                        dve.wait_ge(o2_ps, c - 2)
                    o = ps[:, 7, :].rearrange("p (h s) -> p h s", s=SLOT)
                    V.reciprocal(rec[:, t, :], o[:, :, HD]).then_inc(rec_s, 1)
                    dve.wait_ge(rec_s, c)
                    V.tensor_tensor(on[:, t, :].rearrange("p (h d) -> p h d", d=HD), o[:, :, 0:HD],
                                    rec[:, t, :].rearrange("p (h o) -> p h o", o=1).broadcast_to([P, HEADS, HD]),
                                    ALU.mult).then_inc(on_s, 1)
                if i == 6 * t + 3:
                    dve.wait_ge(oth_s, c)
                    V.tensor_tensor(otl[:, t, :, :].rearrange("p c q -> p (c q)"), ps[:, 7, 0:D],
                                    oth[:, t, :, :].rearrange("p c q -> p (c q)").bitcast(F32), ALU.subtract)\
                     .then_inc(otl_s, 1)
                if i == 6 * t + 5:
                    dve.wait_ge(y_ps, c)
                    xt = x[:, 2 * n + t, :]
                    V.tensor_tensor(xt, xt, ps[:, 7, 0:D], ALU.add).then_inc(yt_s, 1)
                    if t == 1 and n % 2:
                        dve.wait_ge(yt_s, c)
                        V.memset(mark[:, :], 0.0).then_inc(x_s, 1)

            def attn0_setup():
                dve.wait_ge(const_s, 16 * N_SETUP)
                for t in range(2):
                    i = V.tensor_scalar(m0[:, t, :], ident[:, :], r0c[:, 0:1], None, ALU.mult)
                i.then_inc(a0_set, 1)
                dve.wait_ge(a0_set, 1)
                V.tensor_copy(m0[0:SA, 0, 0:SA], a0[:, 0:SA]).then_inc(a0_set, 1)

            def attn0(p, k):
                dve.wait_ge(pt_ps_s, k // 4 + 1)
                V.tensor_copy(pt[:, :], ps[0:SA, 7, 0:SA]).then_inc(a0_set, 1)
                for q in range(4):
                    s, n = q % 2, k + q
                    if q == 2:
                        ln_stats(p + 1, p)
                        normalise(p + 1, [(o0_s, k + 2), (xz_s, k + 2)])
                    dve.wait_ge(mt_ps_s, n + 1)
                    if q >= 2:
                        dve.wait_ge(sc_ps_s, n - 1)
                    V.tensor_copy(pxs[:, s, :], ps[0:SA, 2 + s, 0:D]).then_inc(px_s, 1)
                    xb = x[:, 2 * q:2 * q + 2, :]
                    if q == 2:
                        dve.wait_ge(upd_s, n // 2)
                    if q == 3:
                        dve.wait_ge(x_s, p + 1)
                    V.tensor_tensor(xz[:, s, :, :], xb, z[:, 2 * s:2 * s + 2, :], ALU.add).then_inc(xz_s, 1)
                    dve.wait_ge(att_s, n + 1)
                    V.tensor_tensor(att[96:P, s, 1, D - 1:D], att[96:P, s, 1, D - 1:D], cap_c[96:P, :], ALU.min)\
                     .then_inc(attz_s, 1)
                    dve.wait_ge(o0_s, n + 1)
                    dve.wait_ge(xz_s, n + 1)
                    i = V.tensor_tensor(xb, xz[:, s, :, :], ps[:, 6 + s, :].rearrange("p (t d) -> p t d", t=2), ALU.add)
                    i.then_inc(x_s if q % 2 else upd_s, 1)

            router_weights()
            if "attn0" in stages:
                attn0_setup()
            for s, (kind, p, k) in enumerate(plan):
                if kind == "ffn0" and k == 0:
                    weights_lo(0)
                    weights_lo(1)
                ln_stats(p, p)
                free = [] if s == 0 else \
                    [(o0_s, plan[s - 1][2] + 4), (xz_s, plan[s - 1][2] + 4)] if plan[s - 1][0] == "attn0" else \
                    [(zt_s, zt_count(p - 1))]
                normalise(p, free)
                {"ffn0": ffn0, "ffn1": ffn1, "attn0": attn0, "attn1": attn1}[kind](p, k)


def kernel(**inputs):
    import numpy as np
    import concourse.bacc as bacc
    from concourse.bass_utils import run_bass_kernel_spmd

    a = {k: np.asarray(v) for k, v in inputs.items()}
    f = {k[7:]: v for k, v in a.items() if k.startswith("L0_ffn_")}
    dense = [f[n].reshape(KC, P, J0, P) for n in ("w_gate", "w_up")]
    dense = np.stack(dense).transpose(3, 2, 1, 0, 4)
    moe = [f[n].reshape(E, KC, P, P) for n in ("we_gate", "we_up")]
    moe = np.stack(moe).transpose(1, 3, 2, 0, 4)
    down = np.concatenate([f["w_down"].reshape(J0, P, D), f["we_down"]])
    w0 = np.concatenate([np.concatenate([dense, moe]).reshape(U0, P, 2 * D), down], axis=2)
    w1u = a["L1_ffn_w1"].reshape(E, P, KC, P).transpose(0, 3, 2, 1).reshape(E, P, D)
    w1 = np.concatenate([w1u, a["L1_ffn_w2"].transpose(0, 2, 1)], axis=2)
    wr = np.stack([f["router_w"].reshape(KC, P, E), a["L1_ffn_wg"].reshape(KC, P, E)]).transpose(2, 0, 1, 3)
    pre = np.stack([f[n].reshape(KC, P) for n in ("rn_pre1", "rn_pre2", "router_scale")]).transpose(2, 0, 1)
    posts = np.concatenate([f["rn_post1"], f["rn_post2"], f["rn_post"], f["per_expert_scale"]])
    att0 = np.concatenate([a["L0_attn_A_l"].T, a["L0_attn_B_l"], a["L0_attn_C_l"]], axis=1)
    cap = np.full((P, 1), 3.4028235e38, np.float32)
    cap[P - 1] = 0.0
    t = {n: a["L1_attn_" + n].T for n in ("w_q", "w_dkv", "w_uk", "w_uv", "w_o")}
    chunks = {n: v.reshape(-1, P, v.shape[1]).transpose(1, 0, 2).reshape(P, -1) for n, v in t.items()}
    wa = np.concatenate([chunks[n] for n in ("w_q", "w_dkv", "w_uk", "w_uv", "w_o")], axis=1)
    sel = np.zeros((P, 4, 4, P), np.float32)
    for pair in range(4):
        for e in range(2):
            for r in range(HD):
                for part, kinds in enumerate(((0, 2), (1, 2), (0, 3))):
                    for kind in kinds:
                        sel[(2 * pair + e) * HD + r, kind, pair, STEP * e + HD * part + r] = 1.0
    q, j = np.arange(SEQ)[:, None], np.arange(SEQ)[None, :]
    far = np.where(j <= q, 0.0625 * (q - j), FAR).astype(np.float32)
    bias = np.concatenate([far[:P, :P], far[P:, :]], axis=1)
    arrays = {
        "x": a["L0_attn_Z_in"].reshape(TOKENS, D), "w0": w0, "w1": w1, "wr": wr, "pre": pre, "posts": posts,
        "att0": att0, "r0": a["L0_attn_r_l"], "ident": np.eye(P, dtype=np.float32), "cap": cap,
        "iota": np.tile(np.arange(E, dtype=np.float32), BT), "wa": wa, "sel": sel, "bias": bias,
    }
    arrays = {k: np.ascontiguousarray(v) for k, v in arrays.items()}
    nc = bacc.Bacc("TRN2", target_bir_lowering=False, num_devices=1)
    args = [nc.dram_tensor(f"in_{k}_dram", v.shape, mybir.dt.from_np(v.dtype), kind="ExternalInput").ap()
            for k, v in arrays.items()]
    out = nc.dram_tensor("out_dram", (TOKENS, D), F32, kind="ExternalOutput").ap()
    program(nc, *args, out)
    got = run_bass_kernel_spmd(nc, [{f"in_{k}_dram": v for k, v in arrays.items()}], core_ids=[0])
    return got.results[0]["out_dram"].reshape(4, SEQ, D)
```

```python
from collections import namedtuple
from contextlib import ExitStack

import concourse.bass as bass
from concourse import mybir

F32 = mybir.dt.float32
F32R = mybir.dt.float32r
U32 = mybir.dt.uint32
ALU = mybir.AluOpType
ACT = mybir.ActivationFunctionType
AX = mybir.AxisListType

P = 128
D = 256
TOKENS = 1024
TILES = TOKENS // P
BT = 4
BLK = BT * P
KC = D // P
E = 8
J0 = 8
U0 = J0 + E
U1 = E
LN_EPS = 1e-5
RMS_EPS = 1e-6
ROOT = float(D) ** -0.5
SA = 32
HEADS = 16
HD = D // HEADS
SLOT = 32
SEQ = 256
LAG = 2

STAGES = ["ffn0", "attn0", "ffn0", "ffn1", "attn1", "ffn1"]

WA = 2 * D + 2 * P + D + D + 2 * D
W_Q, W_C, W_K, W_V, W_O = 0, 2 * D, 3 * D, 4 * D, 5 * D
ROWS = 3 * HD
STEP = 64
Stage = namedtuple("Stage", "s kind p k before after d0 d1")
FAR = 3.0e38
NA = 3
N_SETUP = 8


def program(nc, x_in, w0, w1, wr, pre, posts, att0, r0, ident_in, cap_in, iota_in, wa, sel_in, bias_in, out,
            stages=STAGES):
    with ExitStack() as ctx:
        def sb(name, shape, dt=F32):
            return ctx.enter_context(nc.sbuf_tensor(name, shape, dt))

        def sem(name):
            return ctx.enter_context(nc.semaphore(name))

        ps = ctx.enter_context(nc.psum_tensor("ps", [P, 8, 512], F32))
        x = sb("x", [P, TILES, D])
        z2 = sb("z", [P, 2, BT, D])
        zh = sb("zh", [P, KC, BLK], F32R)
        zl = sb("zl", [P, KC, BLK], F32R)
        w1_h = sb("w1_h", [P, E, 2 * D], F32R)
        w1_l = sb("w1_l", [P, E, 2 * D], F32R)
        NST = 2
        stage = sb("stage", [P, NST, 3 * D])
        stage1 = stage
        wr_raw = sb("wr_raw", [P, 2, KC, E])
        wr_h = sb("wr_h", [P, 2, KC, P], F32R)
        wr_l = sb("wr_l", [P, 2, KC, P], F32R)
        pre_c = sb("pre_c", [P, 3, KC])
        post_b = sb("post_b", [P, 3 * D + E])
        ident = sb("ident", [P, P])
        cap_c = sb("cap_c", [P, 1])
        iota_b = sb("iota_b", [P, BT * E])
        gel = sb("gel", [P, 2, BLK])
        act32 = sb("act32", [P, 2, BLK])
        ah = sb("ah", [P, NA, BLK], F32R)
        al = sb("al", [P, NA, BLK], F32R)
        macc = sb("macc", [P, BT, D])
        comb = sb("comb", [P, BT, D])
        tmp = sb("tmp", [P, BT, D])
        sq = sb("sq", [P, BT, D], mybir.dt.bfloat16)
        bn = sb("bn", [P, BT, 6])
        mv = sb("mv", [P, BT, 2])
        zs = sb("zs", [P, BT])
        zs_e = sb("zs_e", [P, BT])
        half = sb("half", [P, BT])
        ssq = sb("ssq", [P, 3, BT])
        ssq_e = sb("ssq_e", [P, 3, BT])
        rinv = sb("rinv", [P, 3, BT])
        small = sb("small", [SA, BLK])
        lgt = small[0:E, :]
        pxs = small[:, :].rearrange("p (s d) -> p s d", s=2)
        lg = sb("lg", [P, BT, E])
        mx = sb("mx", [P, BT, 8])
        mi = sb("mi", [P, BT, 8], U32)
        mif = sb("mif", [P, BT, 8])
        lsh = sb("lsh", [P, BT, E])
        lex = sb("lex", [P, BT, E])
        eq = sb("eq", [P, BT, E, 4])
        selm = sb("selm", [P, BT, E])
        em = sb("em", [P, BT, E])
        esum = sb("esum", [P, BT])
        erec = sb("erec", [P, BT])
        gs = sb("gs", [P, BT, E])
        gs1 = sb("gs1", [P, BT, E])
        aff = sb("aff", [P, 2, BT, E])
        a0 = sb("a0", [SA, 3 * SA])
        r0c = sb("r0c", [P, 1])
        m0 = sb("m0", [P, 2, P])
        pt = sb("pt", [SA, SA])
        mt = gel[:, :, :].rearrange("p s (c d) -> p s c d", c=2)
        att = act32[:, :, :].rearrange("p s (c d) -> p s c d", c=2)

        with ExitStack() as first:
            def sb0(name, shape, dt=F32R):
                return first.enter_context(nc.sbuf_tensor(name, shape, dt))

            w0u_h = sb0("w0u_h", [P, U0, KC, 2, P])
            w0u_l = sb0("w0u_l", [P, U0, KC, 2, P])
            w0d_h = sb0("w0d_h", [P, U0, D])
            w0d_l = sb0("w0d_l", [P, U0, D])
        wa_h = sb("wa_h", [P, WA], F32R)
        wa_l = sb("wa_l", [P, WA], F32R)
        sel = sb("sel", [P, 4, 4, P], F32R)
        bias = sb("bias", [P, 3 * P])
        ch = sb("ch", [P, BLK], F32R)
        cl = sb("cl", [P, BLK], F32R)
        qh = sb("qh", [P, 2, BLK], F32R)
        ql = sb("ql", [P, 2, BLK], F32R)
        kh, kl = ah, al
        qs = sb("qs", [P, HEADS // 2, BLK], F32R)
        ks = sb("ks", [P, HEADS // 2, BLK], F32R)
        va = sb("va", [P, BT, HEADS, SLOT])
        pb = sb("pb", [P, 3, 3 * P])
        pbt = sb("pbt", [P, 2, 4, 3 * P])
        wa_raw = va[:, :, :, :].rearrange("p t h s -> p (t h s)")[:, 0:WA]
        sel_raw = pbt[:, :, :, :].rearrange("p g j q -> p (g j q)")[:, 0:16 * P]
        ot = [b[:, :, :].rearrange("p s (g q) -> p (s g) q", q=SEQ) for b in (gel, act32)]
        on = comb[:, 0:2, :]
        oth = sb("oth", [P, 2, KC, P], F32R)
        otl = sb("otl", [P, 2, KC, P], F32R)
        mark = sb("mark", [P, 1])
        nmin = sb("nmin", [P, 4, 2])
        rec = sb("rec", [P, 2, HEADS])

        x_in_s = sem("x_loaded")
        const_s = sem("consts_loaded")
        stage_s = [sem(f"stage_loaded{i}") for i in range(NST)]
        out_s = sem("out_stored")
        setup_pool = sem("setup_pool")
        wr_split = sem("router_split")
        w_hi = sem("weights_hi")
        w_lo = sem("weights_lo")
        bn_s = sem("ln_stats")
        mv_s = sem("ln_mean_var")
        zse_s = sem("ln_var_eps")
        zs_s = sem("ln_scale")
        z_s = sem("z_ready")
        zt_s = sem("zt_ready")
        zh_s = sem("zh_ready")
        zl_s = sem("zl_ready")
        gu_s = sem("gate_up_ready")
        gelu_s = sem("gelu_ready")
        prod_s = sem("prod_ready")
        ah_s = sem("act_hi_ready")
        al_s = sem("act_lo_ready")
        down_s = sem("down_ready")
        acc_s = sem("moe_accumulated")
        h1_s = sem("hidden1_ready")
        ah1_s = sem("hidden1_hi_ready")
        al1_s = sem("hidden1_lo_ready")
        down1_s = sem("down1_ready")
        lgt_ps_s = sem("logits_t_in_psum")
        lgt_s = sem("logits_t_ready")
        lg_ps_s = sem("logits_in_psum")
        tk = sem("topk_steps")
        lsh_s = sem("logits_shifted")
        lex_s = sem("logits_exp")
        dsq_s = sem("dense_squares")
        msq_s = sem("moe_squares")
        csq_s = sem("sum_squares")
        rms_e_s = sem("rms_eps_added")
        rd_s = sem("dense_rms_ready")
        rm_s = sem("moe_rms_ready")
        rc_s = sem("sum_rms_ready")
        dn_s = sem("dense_normed")
        mn_s = sem("moe_normed")
        comb_s = sem("sum_ready")
        fin_s = sem("ffn_out_ready")
        x_s = [sem(f"x_done{b}") for b in range(2)]
        a0_set = sem("attn0_setup")
        pt_ps_s = sem("attn0_bc_in_psum")
        mt_ps_s = sem("attn0_mt_in_psum")
        mt_s = sem("attn0_mt")
        px_s = sem("attn0_px")
        sc_ps_s = sem("attn0_scores_in_psum")
        att_s = sem("attn0_relu")
        attz_s = sem("attn0_corner")
        xz_s = sem("attn0_xz")
        o0_s = sem("attn0_out_in_psum")
        upd_s = sem("attn0_updated")

        wa_s = sem("attn1_consts_loaded")
        wah_s = sem("attn1_weights_hi")
        wal_s = sem("attn1_weights_lo")
        q_ps = sem("q_in_psum")
        qh_s = sem("q_hi")
        ql_s = sem("q_lo")
        c_ps = sem("ckv_in_psum")
        ch_s = sem("ckv_hi")
        cl_s = sem("ckv_lo")
        k_ps = sem("k_in_psum")
        kh_s = sem("k_hi")
        kl_s = sem("k_lo")
        v_ps = sem("v_in_psum")
        v_s = sem("v_ready")
        st_ps = sem("stack_in_psum")
        sta_s = sem("stack_by_act")
        std_s = sem("stack_by_dve")
        s_ps = sem("scores_in_psum")
        sm_s = sem("scores_biased")
        exp_s = sem("probs_ready")
        t_ps = sem("probs_t_in_psum")
        ptd_s = sem("probs_t_by_dve")
        pta_s = sem("probs_t_by_act")
        pv_ps = sem("pv_in_psum")
        ot_s = sem("out_t_ready")
        ob_ps = sem("out_back_in_psum")
        rec_s = sem("softmax_reciprocal")
        on_s = sem("out_normed")
        o2_ps = sem("out_normed_t_in_psum")
        oth_s = sem("out_hi")
        otl_s = sem("out_lo")
        y_ps = sem("attn1_out_in_psum")
        yt_s = sem("attn1_tile_added")

        block = ctx.enter_context(nc.Block())

        plan, blocks = [], {"ffn0": 0, "ffn1": 0, "attn0": 0, "attn1": 0}
        for s, kind in enumerate(stages):
            plan.append(Stage(s, kind, 2 * s, blocks[kind] * (2 if kind == "attn0" else 1),
                              stages[s - 1] if s else None, stages[s + 1] if s + 1 < len(stages) else None,
                              blocks["ffn0"], blocks["ffn1"]))
            blocks[kind] += 2
        f0, norms = blocks["ffn0"], 2 * len(stages)
        routed = {}
        for st in plan:
            if st.kind.startswith("ffn"):
                for b in range(2):
                    routed[st.kind, st.k + b] = len(routed)

        def zt_count(p):
            return sum(1 for st in plan if st.kind != "attn0" for b in range(2) if st.p + b <= p)

        def units(st, b, kind):
            return {"ffn0": U0, "ffn1": U1}[kind] * ({"ffn0": st.d0, "ffn1": st.d1}[kind] + b * (st.kind == kind))

        def before(st, b):
            return st.kind if b else st.before

        last_ffn0 = max(st.s for st in plan if st.kind == "ffn0")
        TK = 11

        def out_bank(n, t):
            return 5 if t and n % 2 else 7


        @block.sync
        def _(sp):
            for b in range(2):
                sp.dma_start(x[:, BT * b:BT * (b + 1), :],
                             x_in[BLK * b:BLK * (b + 1), :].rearrange("(t p) d -> p t d", p=P)).then_inc(x_in_s, 16)
            sp.dma_start(pre_c[:, :, :], pre).then_inc(const_s, 16)
            for u in range(U0 + U1):
                if u >= NST:
                    sp.wait_ge(w_lo, u - NST + 1)
                src, n = (w0[u], 3 * D) if u < U0 else (w1[u - U0], 2 * D)
                sp.dma_start(stage[:, u % NST, 0:n], src).then_inc(stage_s[u % NST], 16)
            if "attn1" in stages:
                for b in range(2):
                    sp.wait_ge(x_s[b], last_ffn0 + 1)
                sp.dma_start(wa_raw, wa).then_inc(wa_s, 16)
                sp.dma_start(sel_raw, sel_in.rearrange("p a b c -> p (a b c)")).then_inc(wa_s, 16)
                sp.dma_start(bias[:, :], bias_in).then_inc(wa_s, 16)
            for b in range(2):
                sp.wait_ge(x_s[b], len(stages))
                sp.dma_start(out[BLK * b:BLK * (b + 1), :].rearrange("(t p) d -> p t d", p=P),
                             x[:, BT * b:BT * (b + 1), :]).then_inc(out_s, 16)
            sp.wait_ge(out_s, 32)

        @block.gpsimd
        def _(pool):
            nc.gpsimd.memset(half[:, :], -0.5).then_inc(setup_pool, 1)
            pool.wait_ge(setup_pool, 1)
            state = {"rms": 0}

            def ln_scale(p):
                if p >= norms:
                    return
                kind = stages[p // 2]
                if kind == "ffn0":
                    mul, add = 1.0 + RMS_EPS, RMS_EPS * LN_EPS
                else:
                    mul, add = 1.0, LN_EPS
                pool.wait_ge(mv_s, p + 1)
                if p:
                    pool.wait_ge(zs_s, p)
                nc.gpsimd.tensor_scalar(zs_e[:, :], mv[:, :, 1], mul, add, ALU.mult, ALU.add).then_inc(zse_s, 1)
                pool.wait_ge(zse_s, p + 1)
                if p:
                    pool.wait_ge(z_s, p)
                nc.gpsimd.tensor_tensor(zs[:, :], zs_e[:, :], half[:, :], ALU.pow).then_inc(zs_s, 1)

            def rms(i, squares, ready, fb, mul, add):
                pool.wait_ge(squares, fb + 1)
                nc.gpsimd.tensor_scalar(ssq_e[:, i, :], ssq[:, i, :], mul, add, ALU.mult, ALU.add).then_inc(rms_e_s, 1)
                state["rms"] += 1
                pool.wait_ge(rms_e_s, state["rms"])
                nc.gpsimd.tensor_tensor(rinv[:, i, :], ssq_e[:, i, :], half[:, :], ALU.pow).then_inc(ready, 1)

            ln_scale(0)
            for st in plan:
                for b in range(2):
                    if st.kind == "ffn0":
                        rms(0, dsq_s, rd_s, st.k + b, 1.0 / D, RMS_EPS)
                    ln_scale(st.p + b + 1)
                    if st.kind == "ffn0":
                        rms(1, msq_s, rm_s, st.k + b, 1.0 / D, RMS_EPS)
                        rms(2, csq_s, rc_s, st.k + b, 4.0 / D, 4.0 * RMS_EPS)
                    if st.kind == "ffn1" and st.k == 0 and b == 0 and "attn1" in stages:
                        pool.wait_ge(wa_s, 48)
                        nc.gpsimd.tensor_copy(sel[:, :, :, :].rearrange("p a b c -> p (a b c)"), sel_raw)\
                          .then_inc(wal_s, 1)
                if st.kind == "ffn1" and st.k == 0 and "attn1" in stages:
                    pool.wait_ge(wah_s, 1)
                    nc.gpsimd.tensor_tensor(wa_l[:, :], wa_raw, wa_h[:, :].bitcast(F32), ALU.subtract)\
                      .then_inc(wal_s, 1)
                    pool.wait_ge(wal_s, 2)
                    nc.gpsimd.memset(va[:, :, :, :], 0.0).then_inc(wal_s, 1)
                    pool.wait_ge(wal_s, 3)
                    nc.gpsimd.memset(va[:, :, :, HD:HD + 1], 1.0).then_inc(wal_s, 1)

        @block.tensor
        def _(pe):
            def split3(o, lh, ll, rh, rl, start, stop, **kw):
                pe.matmul(o, lh, rh, start=start, stop=False, **kw)
                pe.matmul(o, ll, rh, start=False, stop=False, **kw)
                return pe.matmul(o, lh, rl, start=False, stop=stop, **kw)

            def transposes(p):
                pe.wait_ge(z_s, p + 1)
                if p == 0:
                    pe.wait_ge(const_s, 16 * N_SETUP)
                for kc in range(KC):
                    for t in range(BT):
                        mm = pe.transpose(ps[:, kc, t * P:(t + 1) * P], z2[:, p % 2, t, kc * P:(kc + 1) * P],
                                          ident[:, :])
                mm.then_inc(zt_s, 1)

            def logits_t(which, bank, first):
                if first:
                    pe.wait_ge(wr_split, 1)
                for kc in range(KC):
                    mm = split3(ps[:, bank, :], wr_h[:, which, kc, :], wr_l[:, which, kc, :],
                                zh[:, kc, :], zl[:, kc, :], kc == 0, kc == KC - 1)
                mm.then_inc(lgt_ps_s, 1)

            def logits(bank, n):
                pe.wait_ge(lgt_s, n + 1)
                for t in range(BT):
                    mm = pe.transpose(ps[:, bank, t * E:(t + 1) * E], lgt[:, t * P:(t + 1) * P], ident[0:E, 0:E])
                mm.then_inc(lg_ps_s, 1)

            def left_downs(st, b):
                if before(st, b) == "ffn0":
                    for i in (LAG, 1):
                        down0(units(st, b, "ffn0") - i)
                if before(st, b) == "ffn1":
                    for i in (LAG, 1):
                        down1(units(st, b, "ffn1") - i)

            def block_start(st, b):
                if before(st, b) == "ffn0":
                    pe.wait_ge(prod_s, units(st, b, "ffn0") - 1)
                if before(st, b) == "ffn1":
                    pe.wait_ge(al1_s, units(st, b, "ffn1"))
                transposes(st.p + b)
                left_downs(st, b)

            def split_ready(p):
                pe.wait_ge(zh_s, zt_count(p))
                pe.wait_ge(zl_s, zt_count(p))

            def ffn0(st):
                k = st.k
                for b in range(2):
                    for c in range(U0):
                        n, fb = U0 * (k + b) + c, k + b
                        if c == 0:
                            if before(st, b) != "attn0":
                                block_start(st, b)
                            split_ready(st.p + b)
                        if fb == 0:
                            pe.wait_ge(w_hi, c + 1)
                            pe.wait_ge(w_lo, c + 1)
                        if n >= 2:
                            pe.wait_ge(prod_s, n - 1)
                        for g in range(2):
                            for kc in range(KC):
                                mm = split3(ps[:, 2 * (n % 2) + g, :], w0u_h[:, c, kc, g, :], w0u_l[:, c, kc, g, :],
                                            zh[:, kc, :], zl[:, kc, :], kc == 0, kc == KC - 1)
                        mm.then_inc(gu_s, 1)
                        if c == 1:
                            if before(st, b) == "attn0":
                                for i in range(2):
                                    pe.wait_ge(x_s[i], st.s)
                            elif fb:
                                pe.wait_ge(acc_s, E * fb - 1)
                            logits_t(0, 6, fb == 0)
                        if c == 3:
                            logits(6, routed["ffn0", fb])
                        if c >= LAG:
                            down0(n - LAG)

            def down0(n):
                fb, c = divmod(n, U0)
                pe.wait_ge(ah_s, n + 1)
                pe.wait_ge(al_s, n + 1)
                if c == 0 and fb:
                    pe.wait_ge(acc_s, E * fb)
                if c == J0:
                    pe.wait_ge(tk, TK * routed["ffn0", fb] + 1)
                if c == J0 + 1:
                    pe.wait_ge(dn_s, fb + 1)
                if c >= J0 + 2:
                    pe.wait_ge(acc_s, E * fb + c - J0 - 1)
                base = 4 if c < J0 or (c - J0) % 2 else 6
                for t in range(BT):
                    o = ps[:, base + t // 2, (t % 2) * D:(t % 2 + 1) * D]
                    start = (c == 0 and t % 2 == 0) if c < J0 else True
                    mm = split3(o, ah[:, n % NA, t * P:(t + 1) * P], al[:, n % NA, t * P:(t + 1) * P],
                                w0d_h[:, c, :], w0d_l[:, c, :], start, c >= J0 - 1, skip_group_check=c < J0)
                mm.then_inc(down_s, 1)

            def ffn1(st):
                k = st.k
                for b in range(2):
                    for c in range(U1):
                        n, fb = U1 * (k + b) + c, k + b
                        last_out = before(st, b) == "attn1"
                        if c == 0:
                            block_start(st, b)
                            if last_out:
                                out_back(3, 0)
                                out_back(3, 1)
                            split_ready(st.p + b)
                            if before(st, b) == "ffn0":
                                pe.wait_ge(prod_s, U0 * f0)
                            if fb:
                                pe.wait_ge(tk, TK * routed["ffn1", fb - 1] + 1)
                            logits_t(1, 3, not f0)
                            if last_out:
                                out_turn(3, 0)
                                out_turn(3, 1)
                        if c == 1 and last_out:
                            out_project(3, 0)
                            out_project(3, 1)
                        if fb == 0:
                            pe.wait_ge(w_hi, U0 + c + 1)
                            pe.wait_ge(w_lo, U0 + c + 1)
                        if n >= 3:
                            pe.wait_ge(al1_s, n - 2)
                        for kc in range(KC):
                            mm = split3(ps[:, n % 3, :], w1_h[:, c, kc * P:(kc + 1) * P], w1_l[:, c, kc * P:(kc + 1) * P],
                                        zh[:, kc, :], zl[:, kc, :], kc == 0, kc == KC - 1)
                        mm.then_inc(h1_s, 1)
                        if c == 1:
                            logits(3, routed["ffn1", fb])
                        if c >= LAG:
                            down1(n - LAG)

            def down1(n):
                c, slot = n % U1, (U0 * f0 + n) % NA
                pe.wait_ge(al1_s, n + 1)
                if f0 or n >= 2:
                    pe.wait_ge(acc_s, E * f0 + n - 1)
                if "attn1" in stages and n == U1 * 2:
                    pe.wait_ge(yt_s, 8)
                for t in range(BT):
                    mm = split3(ps[:, 6 - 2 * (n % 2) + t // 2, (t % 2) * D:(t % 2 + 1) * D],
                                ah[:, slot, t * P:(t + 1) * P], al[:, slot, t * P:(t + 1) * P],
                                w1_h[:, c, D:], w1_l[:, c, D:], True, True)
                mm.then_inc(down1_s, 1)

            def attn1(st):
                p = st.p
                for b in range(2):
                    block_start(st, b)
                    if b:
                        out_back(1, 0)
                        out_back(1, 1)
                    pe.wait_ge(wal_s, 4)
                    split_ready(p + b)
                    for m in range(2):
                        for kc in range(KC):
                            w = W_Q + kc * D + m * P
                            mm = split3(ps[:, 2 + m, :], wa_h[:, w:w + P], wa_l[:, w:w + P], zh[:, kc, :], zl[:, kc, :],
                                        kc == 0, kc == KC - 1)
                        mm.then_inc(q_ps, 1)
                        if b:
                            for t in range(2):
                                (out_project if m else out_turn)(1, t)
                    if b == 0 and st.before == "ffn1":
                        pe.wait_ge(acc_s, E * f0 + U1 * st.d1)
                    for kc in range(KC):
                        w = W_C + kc * P
                        mm = split3(ps[:, 4, :], wa_h[:, w:w + P], wa_l[:, w:w + P], zh[:, kc, :], zl[:, kc, :],
                                    kc == 0, kc == KC - 1)
                    mm.then_inc(c_ps, 1)
                    for s in range(4):
                        stack(b, s)
                    pe.wait_ge(ch_s, b + 1)
                    pe.wait_ge(cl_s, b + 1)
                    if b:
                        pe.wait_ge(yt_s, 4)
                    for m in range(2):
                        w = W_K + m * P
                        split3(ps[:, 5 + m, :], wa_h[:, w:w + P], wa_l[:, w:w + P], ch[:, :], cl[:, :], True, True)\
                            .then_inc(k_ps, 1)
                    for t in range(BT):
                        mm = split3(ps[:, 7 * (1 - t // 2), (t % 2) * D:(t % 2 + 1) * D], ch[:, t * P:(t + 1) * P],
                                    cl[:, t * P:(t + 1) * P], wa_h[:, W_V:W_V + D], wa_l[:, W_V:W_V + D], True, True)
                    mm.then_inc(v_ps, 1)
                    for s in range(4, HEADS):
                        stack(b, s)
                    pe.wait_ge(sta_s, 8 * (b + 1))
                    pe.wait_ge(std_s, 8 * (b + 1))
                    pe.wait_ge(v_s, b + 1)
                    for hb in range(2 * HEADS):
                        hd = 2 * HEADS * b + hb
                        scores(hd)
                        if hb >= 1:
                            probs_turn(hd - 1)
                        if hb % 4 == 3 and hb >= 7:
                            pv(hd // 4 - 1)
                        if hb >= HEADS + 4 and (hb - HEADS - 4) % 2 == 0:
                            t, i = divmod((hb - HEADS - 4) // 2, 3)
                            (out_back, out_turn, out_project)[i](2 * b, t)
                    probs_turn(2 * HEADS * (b + 1) - 1)
                    pv(8 * (b + 1) - 1)
                if st.after != "ffn1":
                    for step in (out_back, out_turn, out_project):
                        step(3, 0)
                        step(3, 1)

            def stack(b, s):
                half, i = divmod(s, HEADS // 2)
                m, pair = divmod(i, 4)
                if half == 0:
                    pe.wait_ge(qh_s, 2 * b + m + 1)
                    pe.wait_ge(ql_s, 2 * b + m + 1)
                else:
                    pe.wait_ge(kh_s, 2 * b + m + 1)
                    pe.wait_ge(kl_s, 2 * b + m + 1)
                if s == 2:
                    pe.wait_ge(ql_s, 2 * b + 2)
                if s == 3:
                    pe.wait_ge(cl_s, b + 1)
                if s >= 4:
                    done = (HEADS * b + s - 4) // 2 + 1
                    pe.wait_ge(std_s if s % 2 else sta_s, done)
                hi, lo = (qh, ql) if half == 0 else (kh, kl)
                pe.matmul(ps[:, 1 + s % 4, :], sel[:, 2 * half, pair, :], hi[:, m, :], start=True, stop=False)
                pe.matmul(ps[:, 1 + s % 4, :], sel[:, 2 * half + 1, pair, :], lo[:, m, :], start=False, stop=True)\
                  .then_inc(st_ps, 1)

            def scores(hd):
                t0, h = (hd // HEADS % 2) * SEQ, hd % HEADS
                r0, r1 = STEP * (h % 2), STEP * (h % 2) + ROWS
                if hd >= 3:
                    pe.wait_ge(exp_s, hd - 2)
                pe.matmul(ps[:, hd % 3, 0:P], qs[r0:r1, h // 2, t0:t0 + P], ks[r0:r1, h // 2, t0:t0 + P],
                          start=True, stop=True)
                pe.matmul(ps[:, hd % 3, P:3 * P], qs[r0:r1, h // 2, t0 + P:t0 + 2 * P],
                          ks[r0:r1, h // 2, t0:t0 + 2 * P], start=True, stop=True).then_inc(s_ps, 1)

            def probs_turn(hd):
                pe.wait_ge(exp_s, hd + 1)
                if hd >= 2:
                    if (hd - 2) % 4 == 3:
                        pe.wait_ge(pta_s, (hd - 2) // 4 + 1)
                    else:
                        pe.wait_ge(ptd_s, 3 * ((hd - 2) // 4) + (hd - 2) % 4 + 1)
                for c in range(3):
                    mm = pe.transpose(ps[:, 3 + hd % 2, c * P:(c + 1) * P], pb[:, hd % 3, c * P:(c + 1) * P],
                                      ident[:, :])
                mm.then_inc(t_ps, 1)

            def pv(g):
                n, gi = divmod(g, 4)
                pe.wait_ge(ptd_s, 3 * (g + 1))
                pe.wait_ge(pta_s, g + 1)
                if g >= 2:
                    pe.wait_ge(ot_s, g - 1)
                for c in range(2):
                    for j in range(4):
                        o = ps[SLOT * j:SLOT * (j + 1), 5 + g % 2, c * P:SEQ]
                        mm = pe.matmul(o, va[:, 2 * (n % 2) + c, 4 * gi + j, :],
                                       pbt[:, g % 2, j, c * SEQ:SEQ + c * P], start=c == 0, stop=c == 1,
                                       skip_group_check=True, tile_position=(0, SLOT * j))
                mm.then_inc(pv_ps, 1)

            def out_back(n, t):
                pe.wait_ge(ot_s, 4 * (n + 1))
                if n:
                    pe.wait_ge(yt_s, 2 * n + t * (1 - n % 2))
                elif t:
                    pe.wait_ge(yt_s, 1)
                else:
                    pe.wait_ge(v_s, 1)
                for g in range(4):
                    mm = pe.transpose(ps[:, out_bank(n, t), g * P:(g + 1) * P], ot[n % 2][:, g, t * P:(t + 1) * P],
                                      ident[:, :])
                mm.then_inc(ob_ps, 1)

            def out_turn(n, t):
                pe.wait_ge(on_s, 2 * n + t + 1)
                for kc in range(KC):
                    mm = pe.transpose(ps[:, out_bank(n, t), kc * P:(kc + 1) * P], on[:, t, kc * P:(kc + 1) * P],
                                      ident[:, :])
                mm.then_inc(o2_ps, 1)

            def out_project(n, t):
                pe.wait_ge(oth_s, 2 * n + t + 1)
                pe.wait_ge(otl_s, 2 * n + t + 1)
                for kc in range(KC):
                    w = W_O + kc * D
                    mm = split3(ps[:, out_bank(n, t), 0:D], oth[:, t, kc, :], otl[:, t, kc, :],
                                wa_h[:, w:w + D], wa_l[:, w:w + D], kc == 0, kc == KC - 1)
                mm.then_inc(y_ps, 1)

            def attn0(st):
                p, k = st.p, st.k
                pe.wait_ge(const_s, 16 * N_SETUP)
                left_downs(st, 0)
                pe.wait_ge(acc_s, E * st.d0)
                pe.wait_ge(prod_s, U0 * st.d0)
                pe.matmul(ps[0:SA, 7, 0:SA], a0[:, 2 * SA:3 * SA], a0[:, SA:2 * SA], start=True, stop=True)\
                  .then_inc(pt_ps_s, 1)
                for b in range(2):
                    z = z2[:, (p + b) % 2, :, :]
                    pe.wait_ge(z_s, p + b + 1)
                    pe.wait_ge(a0_set, 3)
                    if b:
                        pe.wait_ge(mt_s, k + 2)
                        pe.wait_ge(px_s, k + 2)
                    for i in range(2):
                        for c in range(2):
                            for t in range(2):
                                pe.matmul(ps[:, i, c * D + t * P:c * D + (t + 1) * P],
                                          z[:, 2 * i + t, c * P:(c + 1) * P], m0[:, t, :], start=True, stop=True)
                        pe.matmul(ps[0:SA, 2 + i, 0:D], pt[:, :], z[0:SA, 2 * i, :], start=True, stop=True)\
                          .then_inc(mt_ps_s, 1)
                    if b:
                        pe.wait_ge(att_s, k + 2)
                    for i in range(2):
                        pe.wait_ge(px_s, k + 2 * b + i + 1)
                        for c in range(2):
                            mm = pe.matmul(ps[:, 4 + i, c * D:(c + 1) * D], z[0:SA, 2 * i, c * P:(c + 1) * P],
                                           pxs[:, i, :], start=True, stop=True)
                        mm.then_inc(sc_ps_s, 1)
                    if b:
                        pe.wait_ge(x_s[0], st.s + 1)
                        if st.after:
                            pe.wait_ge(mt_s, k + 4)
                            transposes(p + 2)
                    for i in range(2):
                        pe.wait_ge(mt_s, k + 2 * b + i + 1)
                        pe.wait_ge(attz_s, k + 2 * b + i + 1)
                        for dt in range(2):
                            for c in range(2):
                                mm = pe.matmul(ps[:, 6 + i, dt * D:(dt + 1) * D], mt[:, i, c, dt * P:(dt + 1) * P],
                                               att[:, i, c, :], start=c == 0, stop=c == 1)
                        mm.then_inc(o0_s, 1)

            for st in plan:
                {"ffn0": ffn0, "ffn1": ffn1, "attn0": attn0, "attn1": attn1}[st.kind](st)
            last = st._replace(before=st.kind, d0=f0, d1=blocks["ffn1"])
            left_downs(last, 0)

        @block.scalar
        def _(act):
            def weights_hi(u):
                act.wait_ge(stage_s[u % NST], 16 * (u // NST + 1))
                raw = stage[:, u % NST, :]
                if u < U0:
                    if u == 0:
                        act.wait_ge(const_s, 16 * N_SETUP)
                    for kc in range(KC):
                        nc.scalar.activation(w0u_h[:, u, kc, :, :], raw[:, kc * D:(kc + 1) * D], ACT.Copy,
                                             scale=pre_c[:, int(u >= J0), kc:kc + 1])
                    nc.scalar.activation(w0d_h[:, u, :], raw[:, 2 * D:3 * D], ACT.Copy).then_inc(w_hi, 1)
                else:
                    nc.scalar.activation(w1_h[:, u - U0, :], raw[:, 0:2 * D], ACT.Copy).then_inc(w_hi, 1)

            def z_hi(p):
                act.wait_ge(zt_s, zt_count(p))
                for kc in range(KC):
                    a = nc.scalar.activation(zh[:, kc, :], ps[:, kc, :], ACT.Copy)
                a.then_inc(zh_s, 1)

            def squares(i, src, wait, before, done, fb):
                act.wait_ge(*wait)
                if before[1]:
                    act.wait_ge(*before)
                for t in range(BT):
                    a = nc.scalar.activation(sq[:, t, :], src(t), ACT.Square, accum_out=ssq[:, i, t:t + 1])
                a.then_inc(done, 1)

            def exps(n):
                act.wait_ge(lsh_s, n + 1)
                nc.scalar.activation(lex[:, :, :], lsh[:, :, :], ACT.Exp).then_inc(lex_s, 1)

            def gelu(n):
                act.wait_ge(gu_s, n + 1)
                if n >= 2:
                    act.wait_ge(prod_s, n - 1)
                nc.scalar.activation(gel[:, n % 2, :], ps[:, 2 * (n % 2), :], ACT.Gelu_apprx_tanh).then_inc(gelu_s, 1)

            def act_hi(n):
                act.wait_ge(prod_s, n + 1)
                if n >= NA:
                    act.wait_ge(down_s, n - NA + 1)
                nc.scalar.activation(ah[:, n % NA, :], act32[:, n % 2, :], ACT.Copy).then_inc(ah_s, 1)

            def moe_squares(fb):
                squares(1, lambda t: macc[:, t, :], (acc_s, E * (fb + 1)), (dsq_s, fb + 1), msq_s, fb)

            def sum_squares(fb):
                squares(2, lambda t: comb[:, t, :], (comb_s, fb + 1), (msq_s, fb + 1), csq_s, fb)

            def left_hi(st, b):
                if before(st, b) == "ffn0":
                    act_hi(units(st, b, "ffn0") - 1)

            def ffn0(st):
                p, k = st.p, st.k
                for b in range(2):
                    for c in range(U0):
                        n, fb = U0 * (k + b) + c, k + b
                        if c == 0 and before(st, b) != "attn0":
                            left_hi(st, b)
                            z_hi(p + b)
                        if fb == 0 and c + 2 < U0:
                            weights_hi(c + 2)
                        if fb == 1 and c < U1:
                            weights_hi(U0 + c)
                        gelu(n)
                        if c:
                            act_hi(n - 1)
                        if before(st, b) == "ffn0" and c == 2:
                            moe_squares(fb - 1)
                        if before(st, b) == "ffn0" and c == 4:
                            sum_squares(fb - 1)
                        if c == 6:
                            exps(routed["ffn0", fb])
                        if c == J0 + 1:
                            squares(0, lambda t: ps[:, 4 + t // 2, (t % 2) * D:(t % 2 + 1) * D],
                                    (down_s, U0 * fb + J0), (csq_s, fb), dsq_s, fb)
                if st.after is None:
                    act_hi(U0 * (k + 2) - 1)
                    moe_squares(k + 1)
                    sum_squares(k + 1)

            def ffn1(st):
                p, k = st.p, st.k
                for b in range(2):
                    for c in range(U1):
                        n, fb = U1 * (k + b) + c, k + b
                        if c == 0:
                            left_hi(st, b)
                            z_hi(p + b)
                            if before(st, b) == "attn1":
                                out_hi(3, 0)
                                out_hi(3, 1)
                        act.wait_ge(h1_s, n + 1)
                        if n >= NA:
                            act.wait_ge(down1_s, n - NA + 1)
                        nc.scalar.activation(ah[:, (U0 * f0 + n) % NA, :], ps[:, n % 3, :], ACT.Relu).then_inc(ah1_s, 1)
                        if c == 2:
                            exps(routed["ffn1", fb])
                        if before(st, b) == "ffn0" and c == 1:
                            moe_squares(f0 - 1)
                        if before(st, b) == "ffn0" and c == 3:
                            sum_squares(f0 - 1)
                        if fb == 1 and c == 2 and "attn1" in stages:
                            act.wait_ge(wa_s, 48)
                            nc.scalar.activation(wa_h[:, :], wa_raw, ACT.Copy).then_inc(wah_s, 1)

            def attn1(st):
                p = st.p
                for b in range(2):
                    z_hi(p + b)
                    for m in range(2):
                        act.wait_ge(q_ps, 2 * b + m + 1)
                        nc.scalar.activation(qh[:, m, :], ps[:, 2 + m, :], ACT.Copy, scale=-(HD ** -0.5))\
                          .then_inc(qh_s, 1)
                        if b and m == 0:
                            out_hi(1, 0)
                            out_hi(1, 1)
                    act.wait_ge(c_ps, b + 1)
                    nc.scalar.activation(ch[:, :], ps[:, 4, :], ACT.Copy).then_inc(ch_s, 1)
                    for m in range(2):
                        act.wait_ge(k_ps, 2 * b + m + 1)
                        nc.scalar.activation(kh[:, m, :], ps[:, 5 + m, :], ACT.Copy).then_inc(kh_s, 1)
                    for s in range(0, HEADS, 2):
                        act.wait_ge(st_ps, HEADS * b + s + 1)
                        dst = (qs if s < HEADS // 2 else ks)[:, s % (HEADS // 2), :]
                        nc.scalar.activation(dst, ps[:, 1 + s % 4, :], ACT.Copy).then_inc(sta_s, 1)
                    for hb in range(2 * HEADS):
                        hd = 2 * HEADS * b + hb
                        act.wait_ge(sm_s, hd + 1)
                        if hd >= 3:
                            act.wait_ge(t_ps, hd - 2)
                        nc.scalar.activation(pb[:, hd % 3, 0:P], ps[:, hd % 3, 0:P], ACT.Exp,
                                             bias=nmin[:, hd % 4, 0:1], scale=-1.0)
                        nc.scalar.activation(pb[:, hd % 3, P:3 * P], ps[:, hd % 3, P:3 * P], ACT.Exp,
                                             bias=nmin[:, hd % 4, 1:2], scale=-1.0).then_inc(exp_s, 1)
                        if hb % 4 == 1 and hb >= 5:
                            probs_t(hd - 2)
                        if hb % 4 == 3 and hb >= 7:
                            out_t(hd // 4 - 1)
                        if hb == HEADS + 7:
                            out_hi(2 * b, 0)
                        if hb == HEADS + 13:
                            out_hi(2 * b, 1)
                    probs_t(2 * HEADS * (b + 1) - 1)
                    out_t(8 * (b + 1) - 1)
                if st.after != "ffn1":
                    out_hi(3, 0)
                    out_hi(3, 1)

            def probs_t(hd):
                act.wait_ge(t_ps, hd + 1)
                if hd >= 8:
                    act.wait_ge(pv_ps, hd // 4 - 1)
                nc.scalar.activation(pbt[:, hd // 4 % 2, hd % 4, :], ps[:, 3 + hd % 2, 0:3 * P], ACT.Copy)\
                  .then_inc(pta_s, 1)

            def out_t(g):
                act.wait_ge(pv_ps, g + 1)
                if g >= 8:
                    act.wait_ge(ob_ps, 2 * (g // 4 - 1))
                nc.scalar.activation(ot[g // 4 % 2][:, g % 4, :], ps[:, 5 + g % 2, 0:SEQ], ACT.Copy).then_inc(ot_s, 1)

            def out_hi(n, t):
                act.wait_ge(o2_ps, 2 * n + t + 1)
                nc.scalar.activation(oth[:, t, :, :].rearrange("p c q -> p (c q)"), ps[:, out_bank(n, t), 0:D], ACT.Copy)\
                  .then_inc(oth_s, 1)

            def attn0(st):
                k = st.k
                left_hi(st, 0)
                for b in range(2):
                    for i in range(2):
                        n = k + 2 * b + i
                        act.wait_ge(mt_ps_s, n + 1)
                        if b:
                            act.wait_ge(o0_s, n - 1)
                        elif i == 0:
                            act.wait_ge(prod_s, U0 * st.d0)
                        nc.scalar.activation(mt[:, i, :, :], ps[:, i, :], ACT.Copy).then_inc(mt_s, 1)
                    if b == 0:
                        moe_squares(st.d0 - 1)
                    for i in range(2):
                        n = k + 2 * b + i
                        act.wait_ge(sc_ps_s, n + 1)
                        if n == k:
                            act.wait_ge(al_s, U0 * st.d0)
                        nc.scalar.activation(att[:, i, :, :], ps[:, 4 + i, :], ACT.Relu).then_inc(att_s, 1)
                    if b == 0:
                        sum_squares(st.d0 - 1)
                if st.after:
                    z_hi(st.p + 2)

            act.dma_start(ident[:, :], ident_in).then_inc(const_s, 16)
            act.dma_start(wr_raw[:, :, :, :], wr).then_inc(const_s, 16)
            act.dma_start(post_b[:, :], posts.partition_broadcast(P)).then_inc(const_s, 16)
            act.dma_start(iota_b[:, :], iota_in.partition_broadcast(P)).then_inc(const_s, 16)
            act.dma_start(a0[:, :], att0).then_inc(const_s, 16)
            act.dma_start(r0c[:, :], r0.partition_broadcast(P)).then_inc(const_s, 16)
            act.dma_start(cap_c[:, :], cap_in).then_inc(const_s, 16)
            if "ffn0" in stages:
                weights_hi(0)
                weights_hi(1)
            for st in plan:
                {"ffn0": ffn0, "ffn1": ffn1, "attn0": attn0, "attn1": attn1}[st.kind](st)

        @block.vector
        def _(dve):
            steps = {"tk": 0}
            step = sem("setup_dve")
            V = nc.vector

            def weights_lo(u):
                dve.wait_ge(w_hi, u + 1)
                raw = stage[:, u % NST, :]
                if u < U0:
                    for kc in range(KC):
                        V.scalar_tensor_tensor(w0u_l[:, u, kc, :, :].rearrange("p g m -> p (g m)"), raw[:, kc * D:(kc + 1) * D],
                                               pre_c[:, int(u >= J0), kc:kc + 1],
                                               w0u_h[:, u, kc, :, :].rearrange("p g m -> p (g m)").bitcast(F32),
                                               ALU.mult, ALU.subtract)
                    V.tensor_tensor(w0d_l[:, u, :], raw[:, 2 * D:3 * D], w0d_h[:, u, :].bitcast(F32),
                                    ALU.subtract).then_inc(w_lo, 1)
                else:
                    V.tensor_tensor(w1_l[:, u - U0, :], raw[:, 0:2 * D], w1_h[:, u - U0, :].bitcast(F32),
                                    ALU.subtract).then_inc(w_lo, 1)

            def router_weights():
                dve.wait_ge(const_s, 16 * N_SETUP)
                V.memset(wr_h[:, :, :, :].bitcast(F32), 0.0)
                V.memset(wr_l[:, :, :, :].bitcast(F32), 0.0).then_inc(step, 1)
                dve.wait_ge(step, 1)
                for kc in range(KC):
                    V.tensor_scalar(wr_raw[:, 0, kc, :], wr_raw[:, 0, kc, :], pre_c[:, 2, kc:kc + 1], ROOT,
                                    ALU.mult, ALU.mult).then_inc(step, 1)
                dve.wait_ge(step, 1 + KC)
                V.tensor_copy(wr_h[:, :, :, 0:E], wr_raw[:, :, :, :]).then_inc(step, 1)
                dve.wait_ge(step, 2 + KC)
                V.tensor_tensor(wr_l[:, :, :, 0:E], wr_raw[:, :, :, :], wr_h[:, :, :, 0:E].bitcast(F32),
                                ALU.subtract).then_inc(wr_split, 1)

            def ln_stats(p):
                b = p % 2
                if p < 2:
                    dve.wait_ge(x_in_s, 32)
                else:
                    dve.wait_ge(x_s[b], p // 2)
                for t in range(BT):
                    i = V.bn_stats(bn[:, t, :], x[:, BT * b + t, :])
                i.then_inc(bn_s, 1)
                dve.wait_ge(bn_s, p + 1)
                if p:
                    dve.wait_ge(z_s, p)
                for t in range(BT):
                    i = V.bn_aggr(mv[:, t, :], bn[:, t, :])
                i.then_inc(mv_s, 1)

            def normalise(p):
                b = p % 2
                dve.wait_ge(zs_s, p + 1)
                if p >= 2:
                    st = plan[p // 2 - 1]
                    if st.kind == "attn0":
                        dve.wait_ge(sc_ps_s, st.k + 2 * b + 2)
                        dve.wait_ge(xz_s, st.k + 2 * b + 2)
                    else:
                        dve.wait_ge(zt_s, zt_count(p - 2))
                for t in range(BT):
                    i = V.tensor_scalar(z2[:, b, t, :], x[:, BT * b + t, :], mv[:, t, 0:1], zs[:, t:t + 1],
                                        ALU.subtract, ALU.mult)
                i.then_inc(z_s, 1)

            def z_lo(p):
                dve.wait_ge(zh_s, zt_count(p))
                for kc in range(KC):
                    i = V.tensor_tensor(zl[:, kc, :], ps[:, kc, :], zh[:, kc, :].bitcast(F32), ALU.subtract)
                i.then_inc(zl_s, 1)

            def logits_t_out(n, bank):
                dve.wait_ge(lgt_ps_s, n + 1)
                V.tensor_copy(lgt, ps[0:E, bank, :]).then_inc(lgt_s, 1)

            def tstep(i):
                i.then_inc(tk, 1)
                steps["tk"] += 1

            def tdone():
                dve.wait_ge(tk, steps["tk"])

            def shift_logits(n, bank, top):
                dve.wait_ge(lg_ps_s, n + 1)
                tstep(V.tensor_copy(lg[:, :, :].rearrange("p t e -> p (t e)"), ps[:, bank, 0:BT * E]))
                tdone()
                for t in range(BT):
                    i = V.max(mx[:, t, :], lg[:, t, :])
                tstep(i)
                tdone()
                V.tensor_tensor(lsh[:, :, :], lg[:, :, :], mx[:, :, 0:1].broadcast_to([P, BT, E]),
                                ALU.subtract).then_inc(lsh_s, 1)
                for t in range(BT):
                    i = V.max_index(mi[:, t, :], mx[:, t, :], lg[:, t, :])
                tstep(i)
                tdone()
                tstep(V.tensor_copy(mif[:, :, :], mi[:, :, :]))
                tdone()
                for r in range(top):
                    i = V.tensor_tensor(eq[:, :, :, r], iota_b[:, :].rearrange("p (t e) -> p t e", t=BT),
                                        mif[:, :, r:r + 1].broadcast_to([P, BT, E]), ALU.is_equal)
                tstep(i)
                tdone()
                tstep(V.tensor_reduce(selm[:, :, :], eq[:, :, :, 0:top], AX.X, ALU.add))

            def expert_weights(n, kind, slot):
                dve.wait_ge(lex_s, n + 1)
                tdone()
                tstep(V.tensor_tensor(em[:, :, :], lex[:, :, :], selm[:, :, :], ALU.mult))
                tdone()
                tstep(V.tensor_reduce(esum[:, :], em[:, :, :], AX.X, ALU.add))
                tdone()
                tstep(V.reciprocal(erec[:, :], esum[:, :]))
                tdone()
                tstep(V.tensor_tensor(gs[:, :, :], em[:, :, :], erec[:, :].rearrange("p (t o) -> p t o", o=1)
                                      .broadcast_to([P, BT, E]), ALU.mult))
                tdone()
                if kind == "ffn0":
                    pes = post_b[:, 3 * D:3 * D + E].rearrange("p (o e) -> p o e", o=1).broadcast_to([P, BT, E])
                    tstep(V.tensor_tensor(aff[:, slot, :, :], gs[:, :, :], pes, ALU.mult))
                else:
                    V.tensor_scalar(gs1[:, :, :], gs[:, :, :], 1.0, None, ALU.add).then_inc(step, 1)
                    steps["f1"] = steps.get("f1", 0) + 1
                    dve.wait_ge(step, 2 + KC + 2 * steps["f1"] - 1)
                    V.tensor_tensor(gs1[:, :, :], gs1[:, :, :], gs[:, :, :], ALU.subtract).then_inc(step, 1)
                    dve.wait_ge(step, 2 + KC + 2 * steps["f1"])
                    tstep(V.tensor_tensor(aff[:, slot, :, :], gs1[:, :, :], selm[:, :, :], ALU.mult))
                assert steps["tk"] == TK * (n + 1)

            def accumulate(ready, count, total, e, base, slot, n_tk):
                dve.wait_ge(ready, count)
                if e == 0:
                    dve.wait_ge(tk, n_tk)
                if total:
                    dve.wait_ge(acc_s, total)
                for t in range(BT):
                    o = ps[:, base + t // 2, (t % 2) * D:(t % 2 + 1) * D]
                    a = aff[:, slot, t, e:e + 1]
                    if e == 0:
                        i = V.tensor_scalar(macc[:, t, :], o, a, None, ALU.mult)
                    else:
                        i = V.scalar_tensor_tensor(macc[:, t, :], o, a, macc[:, t, :], ALU.mult, ALU.add)
                i.then_inc(acc_s, 1)

            def acc0(n):
                fb, c = divmod(n, U0)
                if c < J0:
                    return
                e = c - J0
                if e == 0 and fb:
                    dve.wait_ge(mn_s, fb)
                accumulate(down_s, n + 1, E * fb + e, e, 6 if e % 2 == 0 else 4, fb % 2,
                           TK * (routed["ffn0", fb] + 1))

            def product(n):
                dve.wait_ge(gelu_s, n + 1)
                if n >= 2:
                    dve.wait_ge(ah_s, n - 1)
                    dve.wait_ge(al_s, n - 1)
                V.tensor_tensor(act32[:, n % 2, :], gel[:, n % 2, :], ps[:, 2 * (n % 2) + 1, :], ALU.mult)\
                 .then_inc(prod_s, 1)

            def act_lo(n):
                dve.wait_ge(ah_s, n + 1)
                if n >= NA:
                    dve.wait_ge(down_s, n - NA + 1)
                V.tensor_tensor(al[:, n % NA, :], act32[:, n % 2, :], ah[:, n % NA, :].bitcast(F32), ALU.subtract)\
                 .then_inc(al_s, 1)

            def dense_norm(fb):
                dve.wait_ge(rd_s, fb + 1)
                if fb:
                    dve.wait_ge(fin_s, fb)
                for t in range(BT):
                    i = V.scalar_tensor_tensor(comb[:, t, :], ps[:, 4 + t // 2, (t % 2) * D:(t % 2 + 1) * D],
                                               rinv[:, 0, t:t + 1], post_b[:, 0:D], ALU.mult, ALU.mult)
                i.then_inc(dn_s, 1)

            def moe_norm(fb):
                dve.wait_ge(rm_s, fb + 1)
                dve.wait_ge(dn_s, fb + 1)
                if fb:
                    dve.wait_ge(x_s[(fb - 1) % 2], x_count(fb - 1))
                for t in range(BT):
                    i = V.scalar_tensor_tensor(tmp[:, t, :], macc[:, t, :], rinv[:, 1, t:t + 1],
                                               post_b[:, D:2 * D], ALU.mult, ALU.mult)
                i.then_inc(mn_s, 1)
                dve.wait_ge(mn_s, fb + 1)
                V.tensor_tensor(comb[:, :, :], comb[:, :, :], tmp[:, :, :], ALU.add).then_inc(comb_s, 1)

            def finish0(fb, b):
                dve.wait_ge(rc_s, fb + 1)
                dve.wait_ge(comb_s, fb + 1)
                for t in range(BT):
                    i = V.scalar_tensor_tensor(tmp[:, t, :], comb[:, t, :], rinv[:, 2, t:t + 1],
                                               post_b[:, 2 * D:3 * D], ALU.mult, ALU.mult)
                i.then_inc(fin_s, 1)
                dve.wait_ge(fin_s, fb + 1)
                xb = x[:, BT * b:BT * (b + 1), :]
                V.tensor_tensor(xb, xb, tmp[:, :, :], ALU.add).then_inc(x_s[b], 1)

            def x_count(fb):
                return [st.s for st in plan if st.kind == "ffn0" and st.k == fb // 2 * 2][0] + 1

            def left_lo(st, b):
                if before(st, b) == "ffn0":
                    act_lo(units(st, b, "ffn0") - 1)
                left_acc(st, b, 3)

            def left_acc(st, b, i):
                if before(st, b) == "ffn0":
                    acc0(units(st, b, "ffn0") - i)
                if before(st, b) == "ffn1":
                    acc1(units(st, b, "ffn1") - i)

            def prepare(p, part):
                if p < norms:
                    (normalise if part else ln_stats)(p)

            def ffn0(st):
                p, k = st.p, st.k
                for b in range(2):
                    for c in range(U0):
                        n, fb = U0 * (k + b) + c, k + b
                        if c == 0 and before(st, b) != "attn0":
                            left_lo(st, b)
                            z_lo(p + b)
                        if fb == 0 and c + 2 < U0:
                            weights_lo(c + 2)
                        if fb == 1 and c < U1:
                            weights_lo(U0 + c)
                        product(n)
                        if c:
                            act_lo(n - 1)
                        if c < 2 and before(st, b) == "ffn0":
                            left_acc(st, b, 2 - c)
                        if c >= 3:
                            acc0(n - 3)
                        if c == 2:
                            logits_t_out(routed["ffn0", fb], 6)
                        if c == 4:
                            shift_logits(routed["ffn0", fb], 6, 2)
                        if c == 7:
                            expert_weights(routed["ffn0", fb], "ffn0", fb % 2)
                        if c == J0 + 2:
                            dense_norm(fb)
                        if b and c == 4:
                            moe_norm(fb - 1)
                        if b and c == 6:
                            finish0(fb - 1, 0)
                        if c == 12 or c == 13:
                            prepare(p + b + 1, c - 12)
                if st.after is None:
                    last = U0 * (k + 2)
                    act_lo(last - 1)
                    for i in (3, 2, 1):
                        acc0(last - i)
                    moe_norm(k + 1)
                    finish0(k + 1, 1)

            def ffn1(st):
                p, k = st.p, st.k
                for b in range(2):
                    for c in range(U1):
                        n, fb = U1 * (k + b) + c, k + b
                        after_ffn0, after_attn1 = (before(st, b) == kind for kind in ("ffn0", "attn1"))
                        if c == 0:
                            left_lo(st, b)
                            if after_attn1:
                                out_norm(3, 0)
                                out_norm(3, 1)
                            z_lo(p + b)
                            logits_t_out(routed["ffn1", fb], 3)
                            if after_attn1:
                                out_lo(3, 0)
                                out_lo(3, 1)
                        if c < 2:
                            left_acc(st, b, 2 - c)
                        if c == 3 and after_ffn0:
                            moe_norm(f0 - 1)
                        if c >= 3:
                            acc1(n - 3)
                        slot = (U0 * f0 + n) % NA
                        dve.wait_ge(ah1_s, n + 1)
                        if n >= NA:
                            dve.wait_ge(down1_s, n - NA + 1)
                        V.scalar_tensor_tensor(al[:, slot, :], ps[:, n % 3, :], 0.0, ah[:, slot, :].bitcast(F32),
                                               ALU.max, ALU.subtract).then_inc(al1_s, 1)
                        if c == 1 and after_attn1:
                            out_add(st.p - 2, 3, 0)
                            out_add(st.p - 2, 3, 1)
                        if c == 1:
                            shift_logits(routed["ffn1", fb], 3, 4)
                        if c == 2:
                            expert_weights(routed["ffn1", fb], "ffn1", fb % 2)
                        if c == 5 and after_ffn0:
                            finish0(f0 - 1, 1)
                        first = 6 if b == 0 else 4
                        if c == first or c == first + 1:
                            prepare(p + b + 1, c - first)
                if st.after is None:
                    for i in (3, 2, 1):
                        acc1(U1 * (k + 2) - i)

            def stage_of(fb):
                return [st.s for st in plan if st.kind == "ffn1" and st.k == fb // 2 * 2][0]

            def acc1(n):
                fb, e = divmod(n, U1)
                b = fb % 2
                if e == 0 and fb:
                    dve.wait_ge(x_s[1 - b], stage_of(fb - 1) + 1)
                elif e == 0 and f0:
                    dve.wait_ge(mn_s, f0)
                accumulate(down1_s, n + 1, E * f0 + n, e, 6 - 2 * (n % 2), b, TK * (routed["ffn1", fb] + 1))
                if e == E - 1:
                    dve.wait_ge(acc_s, E * f0 + n + 1)
                    xb = x[:, BT * b:BT * (b + 1), :]
                    V.scalar_tensor_tensor(xb, macc[:, :, :], 0.5, xb, ALU.mult, ALU.add).then_inc(x_s[b], 1)

            def attn1(st):
                p = st.p
                for b in range(2):
                    left_acc(st, b, 3)
                    if b:
                        out_norm(1, 0)
                        out_norm(1, 1)
                    z_lo(p + b)
                    for m in range(2):
                        dve.wait_ge(qh_s, 2 * b + m + 1)
                        V.scalar_tensor_tensor(ql[:, m, :], ps[:, 2 + m, :], -(HD ** -0.5), qh[:, m, :].bitcast(F32),
                                               ALU.mult, ALU.subtract).then_inc(ql_s, 1)
                        if b:
                            for t in range(2):
                                if m:
                                    out_add(p, 1, t)
                                else:
                                    out_lo(1, t)
                        else:
                            left_acc(st, b, 2 - m)
                    dve.wait_ge(ch_s, b + 1)
                    V.tensor_tensor(cl[:, :], ps[:, 4, :], ch[:, :].bitcast(F32), ALU.subtract).then_inc(cl_s, 1)
                    for s in (1, 3):
                        stack_out(b, s)
                    for m in range(2):
                        dve.wait_ge(kh_s, 2 * b + m + 1)
                        V.tensor_tensor(kl[:, m, :], ps[:, 5 + m, :], kh[:, m, :].bitcast(F32), ALU.subtract)\
                         .then_inc(kl_s, 1)
                    dve.wait_ge(v_ps, b + 1)
                    for t in range(BT):
                        v = ps[:, 7 * (1 - t // 2), (t % 2) * D:(t % 2 + 1) * D].rearrange("p (h d) -> p h d", d=HD)
                        i = V.tensor_copy(va[:, t, :, 0:HD], v)
                    i.then_inc(v_s, 1)
                    for s in range(5, HEADS, 2):
                        stack_out(b, s)
                    for hb in range(2 * HEADS):
                        hd = 2 * HEADS * b + hb
                        bias_min(hd)
                        if hb >= 2 and (hd - 2) % 4 != 3:
                            probs_t(hd - 2)
                        if hb == 6 or hb == 10:
                            prepare(p + b + 1, hb // 8)
                        if hb >= HEADS + 4 and hb % 2:
                            t, i = divmod((hb - HEADS - 4) // 2, 3)
                            if i == 2:
                                out_add(p, 2 * b, t)
                            else:
                                (out_norm, out_lo)[i](2 * b, t)
                    probs_t(2 * HEADS * (b + 1) - 2)
                if st.after != "ffn1":
                    for t in range(2):
                        out_norm(3, t)
                    for t in range(2):
                        out_lo(3, t)
                    for t in range(2):
                        out_add(p, 3, t)

            def stack_out(b, s):
                dve.wait_ge(st_ps, HEADS * b + s + 1)
                V.tensor_copy((qs if s < HEADS // 2 else ks)[:, s % (HEADS // 2), :], ps[:, 1 + s % 4, :])\
                 .then_inc(std_s, 1)

            def bias_min(hd):
                dve.wait_ge(s_ps, hd + 1)
                if hd >= 4:
                    dve.wait_ge(exp_s, hd - 3)
                if hd == 0:
                    dve.wait_ge(wa_s, 48)
                for c, (lo, hi) in enumerate(((0, P), (P, 3 * P))):
                    s = ps[:, hd % 3, lo:hi]
                    i = V.tensor_tensor_reduce(s, s, bias[:, lo:hi], 1.0, FAR, ALU.add, ALU.min,
                                               nmin[:, hd % 4, c:c + 1])
                i.then_inc(sm_s, 1)

            def probs_t(hd):
                dve.wait_ge(t_ps, hd + 1)
                if hd >= 8:
                    dve.wait_ge(pv_ps, hd // 4 - 1)
                V.tensor_copy(pbt[:, hd // 4 % 2, hd % 4, :], ps[:, 3 + hd % 2, 0:3 * P]).then_inc(ptd_s, 1)

            def out_norm(n, t):
                c = 2 * n + t + 1
                dve.wait_ge(ob_ps, c)
                if c > 2:
                    dve.wait_ge(o2_ps, c - 2)
                o = ps[:, out_bank(n, t), :].rearrange("p (h s) -> p h s", s=SLOT)
                V.reciprocal(rec[:, t, :], o[:, :, HD]).then_inc(rec_s, 1)
                dve.wait_ge(rec_s, c)
                V.tensor_tensor(on[:, t, :].rearrange("p (h d) -> p h d", d=HD), o[:, :, 0:HD],
                                rec[:, t, :].rearrange("p (h o) -> p h o", o=1).broadcast_to([P, HEADS, HD]),
                                ALU.mult).then_inc(on_s, 1)

            def out_lo(n, t):
                dve.wait_ge(oth_s, 2 * n + t + 1)
                V.tensor_tensor(otl[:, t, :, :].rearrange("p c q -> p (c q)"), ps[:, out_bank(n, t), 0:D],
                                oth[:, t, :, :].rearrange("p c q -> p (c q)").bitcast(F32), ALU.subtract)\
                 .then_inc(otl_s, 1)

            def out_add(p, n, t):
                c = 2 * n + t + 1
                dve.wait_ge(y_ps, c)
                xt = x[:, 2 * n + t, :]
                V.tensor_tensor(xt, xt, ps[:, out_bank(n, t), 0:D], ALU.add).then_inc(yt_s, 1)
                if t == 1 and n % 2:
                    dve.wait_ge(yt_s, c)
                    V.memset(mark[:, :], 0.0).then_inc(x_s[n // 2], 1)

            def attn0_setup():
                dve.wait_ge(const_s, 16 * N_SETUP)
                for t in range(2):
                    i = V.tensor_scalar(m0[:, t, :], ident[:, :], r0c[:, 0:1], None, ALU.mult)
                i.then_inc(a0_set, 1)
                dve.wait_ge(a0_set, 1)
                V.tensor_copy(m0[0:SA, 0, 0:SA], a0[:, 0:SA]).then_inc(a0_set, 1)

            def attn0(st):
                p, k = st.p, st.k
                left_lo(st, 0)
                left_acc(st, 0, 2)
                left_acc(st, 0, 1)
                dve.wait_ge(pt_ps_s, k // 4 + 1)
                V.tensor_copy(pt[:, :], ps[0:SA, 7, 0:SA]).then_inc(a0_set, 1)
                for b in range(2):
                    z = z2[:, (p + b) % 2, :, :]
                    for i in range(2):
                        n = k + 2 * b + i
                        dve.wait_ge(mt_ps_s, n + 1)
                        if b:
                            dve.wait_ge(sc_ps_s, n - 1)
                        V.tensor_copy(pxs[:, i, :], ps[0:SA, 2 + i, 0:D]).then_inc(px_s, 1)
                    for i in range(2):
                        xb = x[:, 4 * b + 2 * i:4 * b + 2 * i + 2, :]
                        V.tensor_tensor(xb, xb, z[:, 2 * i:2 * i + 2, :], ALU.add).then_inc(xz_s, 1)
                    for i in range(2):
                        dve.wait_ge(att_s, k + 2 * b + i + 1)
                        V.tensor_tensor(att[96:P, i, 1, D - 1:D], att[96:P, i, 1, D - 1:D], cap_c[96:P, :], ALU.min)\
                         .then_inc(attz_s, 1)
                    if b == 0:
                        moe_norm(st.d0 - 1)
                    elif st.after:
                        z_lo(p + 2)
                    for i in range(2):
                        n = k + 2 * b + i
                        dve.wait_ge(o0_s, n + 1)
                        dve.wait_ge(xz_s, n + 1)
                        xb = x[:, 4 * b + 2 * i:4 * b + 2 * i + 2, :]
                        V.tensor_tensor(xb, xb, ps[:, 6 + i, :].rearrange("p (t d) -> p t d", t=2), ALU.add)\
                         .then_inc(x_s[b] if i else upd_s, 1)
                    if b == 0:
                        finish0(st.d0 - 1, 1)
                        for q in (p + 1, p + 2):
                            prepare(q, 0)
                            prepare(q, 1)

            router_weights()
            if "attn0" in stages:
                attn0_setup()
            prepare(0, 0)
            prepare(0, 1)
            for st in plan:
                if st.kind == "ffn0" and st.k == 0:
                    weights_lo(0)
                    weights_lo(1)
                {"ffn0": ffn0, "ffn1": ffn1, "attn0": attn0, "attn1": attn1}[st.kind](st)


def kernel(**inputs):
    import numpy as np
    import concourse.bacc as bacc
    from concourse.bass_utils import run_bass_kernel_spmd

    a = {k: np.asarray(v) for k, v in inputs.items()}
    f = {k[7:]: v for k, v in a.items() if k.startswith("L0_ffn_")}
    dense = [f[n].reshape(KC, P, J0, P) for n in ("w_gate", "w_up")]
    dense = np.stack(dense).transpose(3, 2, 1, 0, 4)
    moe = [f[n].reshape(E, KC, P, P) for n in ("we_gate", "we_up")]
    moe = np.stack(moe).transpose(1, 3, 2, 0, 4)
    down = np.concatenate([f["w_down"].reshape(J0, P, D), f["we_down"]])
    w0 = np.concatenate([np.concatenate([dense, moe]).reshape(U0, P, 2 * D), down], axis=2)
    w1u = a["L1_ffn_w1"].reshape(E, P, KC, P).transpose(0, 3, 2, 1).reshape(E, P, D)
    w1 = np.concatenate([w1u, a["L1_ffn_w2"].transpose(0, 2, 1)], axis=2)
    wr = np.stack([f["router_w"].reshape(KC, P, E), a["L1_ffn_wg"].reshape(KC, P, E)]).transpose(2, 0, 1, 3)
    pre = np.stack([f[n].reshape(KC, P) for n in ("rn_pre1", "rn_pre2", "router_scale")]).transpose(2, 0, 1)
    posts = np.concatenate([f["rn_post1"], f["rn_post2"], f["rn_post"], f["per_expert_scale"]])
    att0 = np.concatenate([a["L0_attn_A_l"].T, a["L0_attn_B_l"], a["L0_attn_C_l"]], axis=1)
    cap = np.full((P, 1), 3.4028235e38, np.float32)
    cap[P - 1] = 0.0
    t = {n: a["L1_attn_" + n].T for n in ("w_q", "w_dkv", "w_uk", "w_uv", "w_o")}
    chunks = {n: v.reshape(-1, P, v.shape[1]).transpose(1, 0, 2).reshape(P, -1) for n, v in t.items()}
    wa = np.concatenate([chunks[n] for n in ("w_q", "w_dkv", "w_uk", "w_uv", "w_o")], axis=1)
    sel = np.zeros((P, 4, 4, P), np.float32)
    for pair in range(4):
        for e in range(2):
            for r in range(HD):
                for part, kinds in enumerate(((0, 2), (1, 2), (0, 3))):
                    for kind in kinds:
                        sel[(2 * pair + e) * HD + r, kind, pair, STEP * e + HD * part + r] = 1.0
    q, j = np.arange(SEQ)[:, None], np.arange(SEQ)[None, :]
    far = np.where(j <= q, 0.0625 * (q - j), FAR).astype(np.float32)
    bias = np.concatenate([far[:P, :P], far[P:, :]], axis=1)
    arrays = {
        "x": a["L0_attn_Z_in"].reshape(TOKENS, D), "w0": w0, "w1": w1, "wr": wr, "pre": pre, "posts": posts,
        "att0": att0, "r0": a["L0_attn_r_l"], "ident": np.eye(P, dtype=np.float32), "cap": cap,
        "iota": np.tile(np.arange(E, dtype=np.float32), BT), "wa": wa, "sel": sel, "bias": bias,
    }
    arrays = {k: np.ascontiguousarray(v) for k, v in arrays.items()}
    nc = bacc.Bacc("TRN2", target_bir_lowering=False, num_devices=1)
    args = [nc.dram_tensor(f"in_{k}_dram", v.shape, mybir.dt.from_np(v.dtype), kind="ExternalInput").ap()
            for k, v in arrays.items()]
    out = nc.dram_tensor("out_dram", (TOKENS, D), F32, kind="ExternalOutput").ap()
    program(nc, *args, out)
    got = run_bass_kernel_spmd(nc, [{f"in_{k}_dram": v for k, v in arrays.items()}], core_ids=[0])
    return got.results[0]["out_dram"].reshape(4, SEQ, D)
```

```python
from collections import namedtuple
from contextlib import ExitStack

import concourse.bass as bass
from concourse import mybir

F32 = mybir.dt.float32
F32R = mybir.dt.float32r
U32 = mybir.dt.uint32
ALU = mybir.AluOpType
ACT = mybir.ActivationFunctionType
AX = mybir.AxisListType

P = 128
D = 256
TOKENS = 1024
TILES = TOKENS // P
BT = 4
BLK = BT * P
KC = D // P
E = 8
J0 = 8
U0 = J0 + E
U1 = E
LN_EPS = 1e-5
RMS_EPS = 1e-6
ROOT = float(D) ** -0.5
SA = 32
HEADS = 16
HD = D // HEADS
SLOT = 32
SEQ = 256
LAG = 2

STAGES = ["ffn0", "attn0", "ffn0", "ffn1", "attn1", "ffn1"]

WA = 2 * D + 2 * P + D + D + 2 * D
W_Q, W_C, W_K, W_V, W_O = 0, 2 * D, 3 * D, 4 * D, 5 * D
ROWS = 3 * HD
STEP = 64
Stage = namedtuple("Stage", "s kind p k before after d0 d1")
FAR = 3.0e38
NA = 3
N_SETUP = 6


def program(nc, x_in, w0, w1, wr, pre, posts, att0, r0, ident_in, cap_in, iota_in, wa, sel_in, bias_in, out,
            stages=STAGES):
    with ExitStack() as ctx:
        def sb(name, shape, dt=F32):
            return ctx.enter_context(nc.sbuf_tensor(name, shape, dt))

        def sem(name):
            return ctx.enter_context(nc.semaphore(name))

        ps = ctx.enter_context(nc.psum_tensor("ps", [P, 8, 512], F32))
        x = sb("x", [P, TILES, D])
        z2 = sb("z", [P, 2, BT, D])
        zh = sb("zh", [P, KC, BLK], F32R)
        zl = sb("zl", [P, KC, BLK], F32R)
        w1_h = sb("w1_h", [P, E, 2 * D], F32R)
        w1_l = sb("w1_l", [P, E, 2 * D], F32R)
        NST = 2
        stage = sb("stage", [P, NST, 3 * D])
        stage1 = stage
        wr_raw = sb("wr_raw", [P, 2, KC, E])
        wr_h = sb("wr_h", [P, 2, KC, P], F32R)
        wr_l = sb("wr_l", [P, 2, KC, P], F32R)
        pre_c = sb("pre_c", [P, 3, KC])
        post_b = sb("post_b", [P, 3 * D + E])
        ident = sb("ident", [P, P])
        cap_c = sb("cap_c", [P, 1])
        iota_b = sb("iota_b", [P, BT * E])
        gel = sb("gel", [P, 2, BLK])
        act32 = sb("act32", [P, 2, BLK])
        ah = sb("ah", [P, NA, BLK], F32R)
        al = sb("al", [P, NA, BLK], F32R)
        macc = sb("macc", [P, BT, D])
        comb = sb("comb", [P, BT, D])
        tmp = sb("tmp", [P, BT, D])
        sq = sb("sq", [P, BT, D], mybir.dt.bfloat16)
        bn = sb("bn", [P, BT, 6])
        mv = sb("mv", [P, BT, 2])
        zs = sb("zs", [P, BT])
        zs_e = sb("zs_e", [P, BT])
        half = sb("half", [P, BT])
        ssq = sb("ssq", [P, 3, BT])
        ssq_e = sb("ssq_e", [P, 3, BT])
        rinv = sb("rinv", [P, 3, BT])
        small = sb("small", [SA, BLK])
        lgt = small[0:E, :]
        pxs = small[:, :].rearrange("p (s d) -> p s d", s=2)
        lg = sb("lg", [P, BT, E])
        mx = sb("mx", [P, BT, 8])
        mi = sb("mi", [P, BT, 8], U32)
        mif = sb("mif", [P, BT, 8])
        lsh = sb("lsh", [P, BT, E])
        lex = sb("lex", [P, BT, E])
        eq = sb("eq", [P, BT, E, 4])
        selm = sb("selm", [P, BT, E])
        em = sb("em", [P, BT, E])
        esum = sb("esum", [P, BT])
        erec = sb("erec", [P, BT])
        gs = sb("gs", [P, BT, E])
        gs1 = sb("gs1", [P, BT, E])
        aff = sb("aff", [P, 2, BT, E])
        a0 = sb("a0", [SA, 3 * SA])
        r0c = sb("r0c", [P, 1])
        m0 = sb("m0", [P, 2, P])
        pt = sb("pt", [SA, SA])
        macc1 = gel[:, :, :].rearrange("p s (t d) -> p (s t) d", d=D)
        mt = gel[:, :, :].rearrange("p s (c d) -> p s c d", c=2)
        att = act32[:, :, :].rearrange("p s (c d) -> p s c d", c=2)

        with ExitStack() as first:
            def sb0(name, shape, dt=F32R):
                return first.enter_context(nc.sbuf_tensor(name, shape, dt))

            w0u_h = sb0("w0u_h", [P, U0, KC, 2, P])
            w0u_l = sb0("w0u_l", [P, U0, KC, 2, P])
            w0d_h = sb0("w0d_h", [P, U0, D])
            w0d_l = sb0("w0d_l", [P, U0, D])
        wa_h = sb("wa_h", [P, WA], F32R)
        wa_l = sb("wa_l", [P, WA], F32R)
        sel = sb("sel", [P, 4, 4, P], F32R)
        bias = sb("bias", [P, 3 * P])
        ch = sb("ch", [P, BLK], F32R)
        cl = sb("cl", [P, BLK], F32R)
        qh = sb("qh", [P, 2, BLK], F32R)
        ql = sb("ql", [P, 2, BLK], F32R)
        kh, kl = ah, al
        qs = sb("qs", [P, HEADS // 2, BLK], F32R)
        ks = sb("ks", [P, HEADS // 2, BLK], F32R)
        va = sb("va", [P, BT, HEADS, SLOT])
        pb = sb("pb", [P, 4, 3 * P])
        pbt = sb("pbt", [P, 2, 4, 3 * P])
        wa_raw = va[:, :, :, :].rearrange("p t h s -> p (t h s)")[:, 0:WA]
        sel_raw = pbt[:, :, :, :].rearrange("p g j q -> p (g j q)")[:, 0:16 * P]
        ot = [b[:, :, :].rearrange("p s (g q) -> p (s g) q", q=SEQ) for b in (gel, act32)]
        on = comb[:, 0:2, :]
        oth = sb("oth", [P, 2, KC, P], F32R)
        otl = sb("otl", [P, 2, KC, P], F32R)
        mark = sb("mark", [P, 1])
        nmin = sb("nmin", [P, 4, 2])
        rec = sb("rec", [P, 2, HEADS])

        x_in_s = [sem(f"x_loaded{b}") for b in range(2)]
        ident_s = sem("ident_loaded")
        pre_s = sem("pre_weights_loaded")
        const_s = sem("consts_loaded")
        stage_s = [sem(f"stage_loaded{i}") for i in range(NST)]
        out_s = sem("out_stored")
        setup_pool = sem("setup_pool")
        wr_split = sem("router_split")
        w_hi = sem("weights_hi")
        w_lo = sem("weights_lo")
        bn_s = sem("ln_stats")
        mv_s = sem("ln_mean_var")
        zse_s = sem("ln_var_eps")
        zs_s = sem("ln_scale")
        z_s = sem("z_ready")
        zt_s = sem("zt_ready")
        zh_s = sem("zh_ready")
        zl_s = sem("zl_ready")
        gu_s = sem("gate_up_ready")
        gelu_s = sem("gelu_ready")
        prod_s = sem("prod_ready")
        ah_s = sem("act_hi_ready")
        al_s = sem("act_lo_ready")
        down_s = sem("down_ready")
        acc_s = sem("moe_accumulated")
        h1_s = sem("hidden1_ready")
        ah1_s = sem("hidden1_hi_ready")
        al1_s = sem("hidden1_lo_ready")
        down1_s = sem("down1_ready")
        lgt_ps_s = sem("logits_t_in_psum")
        lgt_s = sem("logits_t_ready")
        lg_ps_s = sem("logits_in_psum")
        tk = sem("topk_steps")
        lsh_s = sem("logits_shifted")
        lex_s = sem("logits_exp")
        dsq_s = sem("dense_squares")
        msq_s = sem("moe_squares")
        csq_s = sem("sum_squares")
        vsq_s = sem("squares_by_dve")
        rms_e_s = sem("rms_eps_added")
        rd_s = sem("dense_rms_ready")
        rm_s = sem("moe_rms_ready")
        rc_s = sem("sum_rms_ready")
        dn_s = sem("dense_normed")
        mn_s = sem("moe_normed")
        comb_s = sem("sum_ready")
        fin_s = sem("ffn_out_ready")
        x_s = [sem(f"x_done{b}") for b in range(2)]
        a0_set = sem("attn0_setup")
        pt_ps_s = sem("attn0_bc_in_psum")
        mt_ps_s = sem("attn0_mt_in_psum")
        mt_s = sem("attn0_mt")
        px_s = sem("attn0_px")
        sc_ps_s = sem("attn0_scores_in_psum")
        att_s = sem("attn0_relu")
        attz_s = sem("attn0_corner")
        xz_s = sem("attn0_xz")
        o0_s = sem("attn0_out_in_psum")
        upd_s = sem("attn0_updated")

        wa_s = sem("attn1_weights_loaded")
        sel_in_s = sem("attn1_consts_loaded")
        sel_s = sem("attn1_selectors")
        wah_s = sem("attn1_weights_hi")
        wal_s = sem("attn1_weights_lo")
        q_ps = sem("q_in_psum")
        qh_s = sem("q_hi")
        ql_s = sem("q_lo")
        c_ps = sem("ckv_in_psum")
        ch_s = sem("ckv_hi")
        cl_s = sem("ckv_lo")
        k_ps = sem("k_in_psum")
        kh_s = sem("k_hi")
        kl_s = sem("k_lo")
        v_ps = sem("v_in_psum")
        v_s = sem("v_ready")
        st_ps = sem("stack_in_psum")
        sta_s = sem("stack_by_act")
        std_s = sem("stack_by_dve")
        s_ps = sem("scores_in_psum")
        sm_s = sem("scores_biased")
        exp_s = sem("probs_ready")
        t_ps = sem("probs_t_in_psum")
        ptd_s = sem("probs_t_by_dve")
        pta_s = sem("probs_t_by_act")
        pv_ps = sem("pv_in_psum")
        ot_s = sem("out_t_ready")
        ob_ps = sem("out_back_in_psum")
        rec_s = sem("softmax_reciprocal")
        on_s = sem("out_normed")
        o2_ps = sem("out_normed_t_in_psum")
        oth_s = sem("out_hi")
        otl_s = sem("out_lo")
        y_ps = sem("attn1_out_in_psum")
        yt_s = sem("attn1_tile_added")

        block = ctx.enter_context(nc.Block())

        plan, blocks = [], {"ffn0": 0, "ffn1": 0, "attn0": 0, "attn1": 0}
        for s, kind in enumerate(stages):
            plan.append(Stage(s, kind, 2 * s, blocks[kind] * (2 if kind == "attn0" else 1),
                              stages[s - 1] if s else None, stages[s + 1] if s + 1 < len(stages) else None,
                              blocks["ffn0"], blocks["ffn1"]))
            blocks[kind] += 2
        f0, norms = blocks["ffn0"], 2 * len(stages)
        routed = {}
        for st in plan:
            if st.kind.startswith("ffn"):
                for b in range(2):
                    routed[st.kind, st.k + b] = len(routed)

        def zt_count(p):
            return sum(1 for st in plan if st.kind != "attn0" for b in range(2) if st.p + b <= p)

        def units(st, b, kind):
            return {"ffn0": U0, "ffn1": U1}[kind] * ({"ffn0": st.d0, "ffn1": st.d1}[kind] + b * (st.kind == kind))

        def before(st, b):
            return st.kind if b else st.before

        blocks_before_attn1 = [st.d1 for st in plan if st.kind == "attn1"][0] if "attn1" in stages else 0

        def prepare_at(st, b):
            return 5 if b == 0 else 4

        last_ffn0 = max(st.s for st in plan if st.kind == "ffn0")
        WL = 4
        TK = 11

        by_act = (1, 3)

        def copied(hd):
            mine = [j for j in range(4) if (j in by_act) == (hd % 4 in by_act)]
            return pta_s if hd % 4 in by_act else ptd_s, len(mine) * (hd // 4) + mine.index(hd % 4) + 1

        def pv_bank(g):
            return 2 if g % 8 == 7 else 5

        def score_bank(hd):
            return hd % (2 * HEADS) % 3

        def turn_bank(hd):
            return (3, 4, 6)[hd % 3]

        def out_bank(n, t):
            return 5 if t and n % 2 else 7


        @block.sync
        def _(sp):
            def load_x(b):
                sp.dma_start(x[:, BT * b:BT * (b + 1), :],
                             x_in[BLK * b:BLK * (b + 1), :].rearrange("(t p) d -> p t d", p=P)).then_inc(x_in_s[b], 16)

            load_x(0)
            for u in range(U0 + U1):
                if u >= NST:
                    sp.wait_ge(w_lo, u - NST + 1)
                src, n = (w0[u], 3 * D) if u < U0 else (w1[u - U0], 2 * D)
                sp.dma_start(stage[:, u % NST, 0:n], src).then_inc(stage_s[u % NST], 16)
                if u == NST - 1:
                    load_x(1)
            if "attn1" in stages:
                for b in range(2):
                    sp.wait_ge(x_s[b], last_ffn0 + 1)
                sp.dma_start(wa_raw, wa).then_inc(wa_s, 16)
                sp.dma_start(sel_raw, sel_in.rearrange("p a b c -> p (a b c)")).then_inc(sel_in_s, 16)
                sp.dma_start(bias[:, :], bias_in).then_inc(sel_in_s, 16)
            for b in range(2):
                sp.wait_ge(x_s[b], len(stages))
                sp.dma_start(out[BLK * b:BLK * (b + 1), :].rearrange("(t p) d -> p t d", p=P),
                             x[:, BT * b:BT * (b + 1), :]).then_inc(out_s, 16)
            sp.wait_ge(out_s, 32)

        @block.gpsimd
        def _(pool):
            nc.gpsimd.memset(half[:, :], -0.5).then_inc(setup_pool, 1)
            nc.gpsimd.memset(wr_h[:, :, :, :].bitcast(F32), 0.0).then_inc(setup_pool, 1)
            nc.gpsimd.memset(wr_l[:, :, :, :].bitcast(F32), 0.0).then_inc(setup_pool, 1)
            pool.wait_ge(setup_pool, 1)
            state = {"rms": 0}

            def ln_scale(p):
                if p >= norms:
                    return
                kind = stages[p // 2]
                if kind == "ffn0":
                    mul, add = 1.0 + RMS_EPS, RMS_EPS * LN_EPS
                else:
                    mul, add = 1.0, LN_EPS
                pool.wait_ge(mv_s, p + 1)
                if p:
                    pool.wait_ge(zs_s, p)
                nc.gpsimd.tensor_scalar(zs_e[:, :], mv[:, :, 1], mul, add, ALU.mult, ALU.add).then_inc(zse_s, 1)
                pool.wait_ge(zse_s, p + 1)
                if p:
                    pool.wait_ge(z_s, p)
                nc.gpsimd.tensor_tensor(zs[:, :], zs_e[:, :], half[:, :], ALU.pow).then_inc(zs_s, 1)

            def rms(i, squares, ready, fb, mul, add):
                pool.wait_ge(squares, fb + 1)
                nc.gpsimd.tensor_scalar(ssq_e[:, i, :], ssq[:, i, :], mul, add, ALU.mult, ALU.add).then_inc(rms_e_s, 1)
                state["rms"] += 1
                pool.wait_ge(rms_e_s, state["rms"])
                nc.gpsimd.tensor_tensor(rinv[:, i, :], ssq_e[:, i, :], half[:, :], ALU.pow).then_inc(ready, 1)

            def split_squares(fb, count):
                for k, st in enumerate(st for st in plan if st.kind == "attn0"):
                    if fb == st.d0 - 1:
                        pool.wait_ge(vsq_s, 2 * k + count)

            def moe_rms(fb):
                split_squares(fb, 1)
                rms(1, msq_s, rm_s, fb, 1.0 / D, RMS_EPS)

            def sum_rms(fb):
                split_squares(fb, 2)
                rms(2, csq_s, rc_s, fb, 4.0 / D, 4.0 * RMS_EPS)

            def hidden_lo(st, b):
                for c in range(U1):
                    n = U1 * (st.k + b) + c
                    slot = (U0 * f0 + n) % NA
                    pool.wait_ge(ah1_s, n + 1)
                    if n >= NA:
                        pool.wait_ge(down1_s, n - NA + 1)
                    nc.gpsimd.tensor_tensor(al[:, slot, :], act32[:, n % 2, :], ah[:, slot, :].bitcast(F32),
                                            ALU.subtract).then_inc(al1_s, 1)
                    if before(st, b) == "ffn0" and c == 1:
                        moe_rms(f0 - 1)
                        pool.wait_ge(mn_s, f0)
                        nc.gpsimd.tensor_tensor(comb[:, :, :], comb[:, :, :], tmp[:, :, :], ALU.add).then_inc(comb_s, 1)
                    if before(st, b) == "ffn0" and c == 4:
                        sum_rms(f0 - 1)
                    if c == prepare_at(st, b):
                        ln_scale(st.p + b + 1)
                    if st.k + b == 1 and c >= U1 - WL and "attn1" in stages:
                        i = c - (U1 - WL)
                        cols = slice(i * WA // WL, (i + 1) * WA // WL)
                        if i == 0:
                            pool.wait_ge(wah_s, 1)
                        nc.gpsimd.tensor_tensor(wa_l[:, cols], wa_raw[:, cols], wa_h[:, cols].bitcast(F32),
                                                ALU.subtract).then_inc(wal_s, 1)

            ln_scale(0)
            for st in plan:
                for b in range(2):
                    if st.kind == "ffn1":
                        hidden_lo(st, b)
                    else:
                        ln_scale(st.p + b + 1)
                    if st.kind == "ffn0":
                        rms(0, dsq_s, rd_s, st.k + b, 1.0 / D, RMS_EPS)
                    if st.kind == "ffn0" and not (b and st.after == "ffn1"):
                        moe_rms(st.k + b)
                        sum_rms(st.k + b)
                if st.kind == "ffn1" and st.k == 0 and "attn1" in stages:
                    pool.wait_ge(wal_s, WL)
                    nc.gpsimd.memset(va[:, :, :, :], 0.0).then_inc(wal_s, 1)
                    pool.wait_ge(wal_s, WL + 1)
                    nc.gpsimd.memset(va[:, :, :, HD:HD + 1], 1.0).then_inc(wal_s, 1)

        @block.tensor
        def _(pe):
            def split3(o, lh, ll, rh, rl, start, stop, **kw):
                pe.matmul(o, lh, rh, start=start, stop=False, **kw)
                pe.matmul(o, ll, rh, start=False, stop=False, **kw)
                return pe.matmul(o, lh, rl, start=False, stop=stop, **kw)

            def transposes(p):
                pe.wait_ge(z_s, p + 1)
                if p == 0:
                    pe.wait_ge(ident_s, 16)
                for kc in range(KC):
                    for t in range(BT):
                        mm = pe.transpose(ps[:, kc, t * P:(t + 1) * P], z2[:, p % 2, t, kc * P:(kc + 1) * P],
                                          ident[:, :])
                mm.then_inc(zt_s, 1)

            def logits_t(which, bank, first):
                if first:
                    pe.wait_ge(wr_split, 1)
                for kc in range(KC):
                    mm = split3(ps[:, bank, :], wr_h[:, which, kc, :], wr_l[:, which, kc, :],
                                zh[:, kc, :], zl[:, kc, :], kc == 0, kc == KC - 1)
                mm.then_inc(lgt_ps_s, 1)

            def logits(bank, n):
                pe.wait_ge(lgt_s, n + 1)
                for t in range(BT):
                    mm = pe.transpose(ps[:, bank, t * E:(t + 1) * E], lgt[:, t * P:(t + 1) * P], ident[0:E, 0:E])
                mm.then_inc(lg_ps_s, 1)

            def left_downs(st, b):
                if before(st, b) == "ffn0":
                    for i in (LAG, 1):
                        down0(units(st, b, "ffn0") - i)
                if before(st, b) == "ffn1":
                    for i in (LAG, 1):
                        down1(units(st, b, "ffn1") - i)

            def block_start(st, b):
                if before(st, b) == "ffn0":
                    pe.wait_ge(prod_s, units(st, b, "ffn0") - 1)
                if before(st, b) == "ffn1":
                    pe.wait_ge(ah1_s, units(st, b, "ffn1"))
                if before(st, b) != "attn1":
                    transposes(st.p + b)
                left_downs(st, b)

            def split_ready(p):
                pe.wait_ge(zh_s, zt_count(p))
                pe.wait_ge(zl_s, zt_count(p))

            def ffn0(st):
                k = st.k
                for b in range(2):
                    for c in range(U0):
                        n, fb = U0 * (k + b) + c, k + b
                        if c == 0:
                            if before(st, b) != "attn0":
                                block_start(st, b)
                            split_ready(st.p + b)
                        if fb == 0:
                            pe.wait_ge(w_hi, c + 1)
                            pe.wait_ge(w_lo, c + 1)
                        if n >= 2:
                            pe.wait_ge(prod_s, n - 1)
                        for g in range(2):
                            for kc in range(KC):
                                mm = split3(ps[:, 2 * (n % 2) + g, :], w0u_h[:, c, kc, g, :], w0u_l[:, c, kc, g, :],
                                            zh[:, kc, :], zl[:, kc, :], kc == 0, kc == KC - 1)
                        mm.then_inc(gu_s, 1)
                        if c == 1:
                            if before(st, b) == "attn0":
                                for i in range(2):
                                    pe.wait_ge(x_s[i], st.s)
                            elif fb:
                                pe.wait_ge(acc_s, E * fb - 1)
                            logits_t(0, 6, fb == 0)
                        if c == 3:
                            logits(6, routed["ffn0", fb])
                        if c >= LAG:
                            down0(n - LAG)

            def down0(n):
                fb, c = divmod(n, U0)
                pe.wait_ge(ah_s, n + 1)
                pe.wait_ge(al_s, n + 1)
                if c == 0 and fb:
                    pe.wait_ge(acc_s, E * fb)
                if c == J0 and fb == 0 and "attn0" in stages:
                    pe.wait_ge(a0_set, 3)
                if c == J0:
                    pe.wait_ge(tk, TK * routed["ffn0", fb] + 1)
                if c == J0 + 1:
                    pe.wait_ge(dn_s, fb + 1)
                if c >= J0 + 2:
                    pe.wait_ge(acc_s, E * fb + c - J0 - 1)
                base = 4 if c < J0 or (c - J0) % 2 else 6
                for t in range(BT):
                    o = ps[:, base + t // 2, (t % 2) * D:(t % 2 + 1) * D]
                    start = (c == 0 and t % 2 == 0) if c < J0 else True
                    mm = split3(o, ah[:, n % NA, t * P:(t + 1) * P], al[:, n % NA, t * P:(t + 1) * P],
                                w0d_h[:, c, :], w0d_l[:, c, :], start, c >= J0 - 1, skip_group_check=c < J0)
                mm.then_inc(down_s, 1)

            def ffn1(st):
                k = st.k
                for b in range(2):
                    for c in range(U1):
                        n, fb = U1 * (k + b) + c, k + b
                        last_out = before(st, b) == "attn1"
                        if c == 0:
                            block_start(st, b)
                            if last_out:
                                out_back(3, 0)
                                out_back(3, 1)
                            split_ready(st.p + b)
                            if before(st, b) == "ffn0":
                                pe.wait_ge(prod_s, U0 * f0)
                            if fb:
                                pe.wait_ge(tk, TK * routed["ffn1", fb - 1] + 1)
                            logits_t(1, 3, not f0)
                            if last_out:
                                out_turn(3, 0)
                                out_turn(3, 1)
                        if c == 1 and last_out:
                            out_project(3, 0)
                            out_project(3, 1)
                        if fb == 0:
                            pe.wait_ge(w_hi, U0 + c + 1)
                            pe.wait_ge(w_lo, U0 + c + 1)
                        if n >= 3:
                            pe.wait_ge(ah1_s, n - 2)
                        for kc in range(KC):
                            mm = split3(ps[:, n % 3, :], w1_h[:, c, kc * P:(kc + 1) * P], w1_l[:, c, kc * P:(kc + 1) * P],
                                        zh[:, kc, :], zl[:, kc, :], kc == 0, kc == KC - 1)
                        mm.then_inc(h1_s, 1)
                        if c == 1:
                            logits(3, routed["ffn1", fb])
                        if c >= LAG:
                            down1(n - LAG)

            def down1(n):
                c, slot = n % U1, (U0 * f0 + n) % NA
                pe.wait_ge(al1_s, n + 1)
                if f0 or n >= 2:
                    pe.wait_ge(acc_s, E * f0 + n - 1)
                if "attn1" in stages and n == U1 * 2:
                    pe.wait_ge(yt_s, 8)
                for t in range(BT):
                    mm = split3(ps[:, 6 - 2 * (n % 2) + t // 2, (t % 2) * D:(t % 2 + 1) * D],
                                ah[:, slot, t * P:(t + 1) * P], al[:, slot, t * P:(t + 1) * P],
                                w1_h[:, c, D:], w1_l[:, c, D:], True, True)
                mm.then_inc(down1_s, 1)

            def attn1(st):
                p = st.p
                for b in range(2):
                    block_start(st, b)
                    if b:
                        out_back(1, 0)
                        out_back(1, 1)
                    pe.wait_ge(wal_s, WL)
                    pe.wait_ge(sel_s, 1)
                    split_ready(p + b)
                    for m in range(2):
                        for kc in range(KC):
                            w = W_Q + kc * D + m * P
                            mm = split3(ps[:, 2 + m, :], wa_h[:, w:w + P], wa_l[:, w:w + P], zh[:, kc, :], zl[:, kc, :],
                                        kc == 0, kc == KC - 1)
                        mm.then_inc(q_ps, 1)
                        if b:
                            for t in range(2):
                                (out_project if m else out_turn)(1, t)
                    for kc in range(KC):
                        w = W_C + kc * P
                        mm = split3(ps[:, 0, :], wa_h[:, w:w + P], wa_l[:, w:w + P], zh[:, kc, :], zl[:, kc, :],
                                    kc == 0, kc == KC - 1)
                    mm.then_inc(c_ps, 1)
                    for s in range(4):
                        stack(b, s)
                    pe.wait_ge(ch_s, b + 1)
                    pe.wait_ge(cl_s, b + 1)
                    if b:
                        pe.wait_ge(yt_s, 4)
                    for m in range(2):
                        w = W_K + m * P
                        split3(ps[:, 5 + m, :], wa_h[:, w:w + P], wa_l[:, w:w + P], ch[:, :], cl[:, :], True, True)\
                            .then_inc(k_ps, 1)
                    for t in range(BT):
                        mm = split3(ps[:, 7 * (1 - t // 2), (t % 2) * D:(t % 2 + 1) * D], ch[:, t * P:(t + 1) * P],
                                    cl[:, t * P:(t + 1) * P], wa_h[:, W_V:W_V + D], wa_l[:, W_V:W_V + D], True, True)
                    mm.then_inc(v_ps, 1)
                    for s in range(4, HEADS):
                        stack(b, s)
                        if s == 11:
                            pe.wait_ge(sta_s, 8 * b + 5)
                            pe.wait_ge(v_s, b + 1)
                            scores(2 * HEADS * b)
                    for hb in range(2 * HEADS):
                        hd = 2 * HEADS * b + hb
                        if hb == 0:
                            continue
                        if hb < HEADS:
                            s = HEADS // 2 + hb // 2
                            pe.wait_ge(std_s if s % 2 else sta_s, 8 * b + s // 2 + 1)
                        if hb < 3:
                            pe.wait_ge((sta_s, std_s)[hb - 1], 8 * b + 7)
                        scores(hd)
                        if hb == 2:
                            pe.wait_ge(sta_s, 8 * (b + 1))
                            pe.wait_ge(std_s, 8 * (b + 1))
                            pe.wait_ge(v_s, b + 1)
                        if hb >= 3:
                            probs_turn(hd - 3)
                        if hb % 4 in (1, 2) and hb >= 8:
                            pv(hd // 4 - 2, hb % 4 - 1)
                        for i, (at, step) in enumerate(zip((7, 9, 12, 14), 2 * (out_back, out_turn, out_project))):
                            if hb == HEADS + at:
                                step(2 * b, i // 3)
                    probs_turn(2 * HEADS * (b + 1) - 3)
                    out_turn(2 * b, 1)
                    probs_turn(2 * HEADS * (b + 1) - 2)
                    for c in range(2):
                        pv(8 * (b + 1) - 2, c)
                    probs_turn(2 * HEADS * (b + 1) - 1)
                    if b == 0 or st.after:
                        transposes(p + b + 1)
                    out_project(2 * b, 1)
                    for c in range(2):
                        pv(8 * (b + 1) - 1, c)
                if st.after != "ffn1":
                    for step in (out_back, out_turn, out_project):
                        step(3, 0)
                        step(3, 1)

            def stack(b, s):
                half, i = divmod(s, HEADS // 2)
                m, pair = divmod(i, 4)
                if half == 0:
                    pe.wait_ge(qh_s, 2 * b + m + 1)
                    pe.wait_ge(ql_s, 2 * b + m + 1)
                else:
                    pe.wait_ge(kh_s, 2 * b + m + 1)
                    pe.wait_ge(kl_s, 2 * b + m + 1)
                if s == 2:
                    pe.wait_ge(ql_s, 2 * b + 2)
                if s == 3 and b == 0:
                    pe.wait_ge(acc_s, E * f0 + U1 * blocks_before_attn1)
                if s >= 4:
                    done = (HEADS * b + s - 4) // 2 + 1
                    pe.wait_ge(std_s if s % 2 else sta_s, done)
                hi, lo = (qh, ql) if half == 0 else (kh, kl)
                pe.matmul(ps[:, 1 + s % 4, :], sel[:, 2 * half, pair, :], hi[:, m, :], start=True, stop=False)
                pe.matmul(ps[:, 1 + s % 4, :], sel[:, 2 * half + 1, pair, :], lo[:, m, :], start=False, stop=True)\
                  .then_inc(st_ps, 1)

            def scores(hd):
                t0, h = (hd // HEADS % 2) * SEQ, hd % HEADS
                r0, r1 = STEP * (h % 2), STEP * (h % 2) + ROWS
                if hd >= 3:
                    pe.wait_ge(exp_s, hd - 2)
                pe.matmul(ps[:, score_bank(hd), 0:P], qs[r0:r1, h // 2, t0:t0 + P], ks[r0:r1, h // 2, t0:t0 + P],
                          start=True, stop=True)
                pe.matmul(ps[:, score_bank(hd), P:3 * P], qs[r0:r1, h // 2, t0 + P:t0 + 2 * P],
                          ks[r0:r1, h // 2, t0:t0 + 2 * P], start=True, stop=True).then_inc(s_ps, 1)

            def probs_turn(hd):
                pe.wait_ge(exp_s, hd + 1)
                if hd >= 3:
                    pe.wait_ge(*copied(hd - 3))
                for c in range(3):
                    mm = pe.transpose(ps[:, turn_bank(hd), c * P:(c + 1) * P], pb[:, hd % 4, c * P:(c + 1) * P],
                                      ident[:, :])
                mm.then_inc(t_ps, 1)

            def pv(g, c):
                n, gi = divmod(g, 4)
                if c == 0:
                    for j in (2, 3):
                        pe.wait_ge(*copied(4 * g + j))
                    if g and pv_bank(g) == 5:
                        pe.wait_ge(ot_s, g)
                for j in range(4):
                    o = ps[SLOT * j:SLOT * (j + 1), pv_bank(g), g % 2 * SEQ + c * P:(g % 2 + 1) * SEQ]
                    mm = pe.matmul(o, va[:, 2 * (n % 2) + c, 4 * gi + j, :],
                                   pbt[:, g % 2, j, c * SEQ:SEQ + c * P], start=c == 0, stop=c == 1,
                                   skip_group_check=True, tile_position=(0, SLOT * j))
                if c == 1:
                    mm.then_inc(pv_ps, 1)

            def out_back(n, t):
                pe.wait_ge(ot_s, 4 * (n + 1))
                if n:
                    pe.wait_ge(yt_s, 2 * n + t * (1 - n % 2))
                elif t:
                    pe.wait_ge(yt_s, 1)
                else:
                    pe.wait_ge(v_s, 1)
                for g in range(4):
                    mm = pe.transpose(ps[:, out_bank(n, t), g * P:(g + 1) * P], ot[n % 2][:, g, t * P:(t + 1) * P],
                                      ident[:, :])
                mm.then_inc(ob_ps, 1)

            def out_turn(n, t):
                pe.wait_ge(on_s, 2 * n + t + 1)
                for kc in range(KC):
                    mm = pe.transpose(ps[:, out_bank(n, t), kc * P:(kc + 1) * P], on[:, t, kc * P:(kc + 1) * P],
                                      ident[:, :])
                mm.then_inc(o2_ps, 1)

            def out_project(n, t):
                pe.wait_ge(oth_s, 2 * n + t + 1)
                pe.wait_ge(otl_s, 2 * n + t + 1)
                for kc in range(KC):
                    w = W_O + kc * D
                    mm = split3(ps[:, out_bank(n, t), 0:D], oth[:, t, kc, :], otl[:, t, kc, :],
                                wa_h[:, w:w + D], wa_l[:, w:w + D], kc == 0, kc == KC - 1)
                mm.then_inc(y_ps, 1)

            def attn0(st):
                p, k = st.p, st.k
                left_downs(st, 0)
                pe.wait_ge(prod_s, U0 * st.d0)
                for b in range(2):
                    z = z2[:, (p + b) % 2, :, :]
                    pe.wait_ge(z_s, p + b + 1)
                    pe.wait_ge(a0_set, 3)
                    if b:
                        pe.wait_ge(mt_s, k + 2)
                        pe.wait_ge(px_s, k + 2)
                    for i in range(2):
                        for c in range(2):
                            for t in range(2):
                                pe.matmul(ps[:, i, c * D + t * P:c * D + (t + 1) * P],
                                          z[:, 2 * i + t, c * P:(c + 1) * P], m0[:, t, :], start=True, stop=True)
                        pe.matmul(ps[0:SA, 2 + i, 0:D], pt[:, :], z[0:SA, 2 * i, :], start=True, stop=True)\
                          .then_inc(mt_ps_s, 1)
                    if b:
                        pe.wait_ge(att_s, k + 2)
                    else:
                        pe.wait_ge(acc_s, E * st.d0)
                    for i in range(2):
                        pe.wait_ge(px_s, k + 2 * b + i + 1)
                        for c in range(2):
                            mm = pe.matmul(ps[:, 4 + i, c * D:(c + 1) * D], z[0:SA, 2 * i, c * P:(c + 1) * P],
                                           pxs[:, i, :], start=True, stop=True)
                        mm.then_inc(sc_ps_s, 1)
                    if b:
                        pe.wait_ge(x_s[0], st.s + 1)
                        if st.after:
                            pe.wait_ge(mt_s, k + 4)
                            transposes(p + 2)
                    for i in range(2):
                        pe.wait_ge(mt_s, k + 2 * b + i + 1)
                        pe.wait_ge(attz_s, k + 2 * b + i + 1)
                        for dt in range(2):
                            for c in range(2):
                                mm = pe.matmul(ps[:, 6 + i, dt * D:(dt + 1) * D], mt[:, i, c, dt * P:(dt + 1) * P],
                                               att[:, i, c, :], start=c == 0, stop=c == 1)
                        mm.then_inc(o0_s, 1)

            if "attn0" in stages:
                pe.wait_ge(const_s, 16 * N_SETUP)
                pe.matmul(ps[0:SA, 7, 0:SA], a0[:, 2 * SA:3 * SA], a0[:, SA:2 * SA], start=True, stop=True)\
                  .then_inc(pt_ps_s, 1)
            for st in plan:
                {"ffn0": ffn0, "ffn1": ffn1, "attn0": attn0, "attn1": attn1}[st.kind](st)
            last = st._replace(before=st.kind, d0=f0, d1=blocks["ffn1"])
            left_downs(last, 0)

        @block.scalar
        def _(act):
            def weights_hi(u):
                act.wait_ge(stage_s[u % NST], 16 * (u // NST + 1))
                raw = stage[:, u % NST, :]
                if u < U0:
                    if u == 0:
                        act.wait_ge(pre_s, 16)
                    for kc in range(KC):
                        nc.scalar.activation(w0u_h[:, u, kc, :, :], raw[:, kc * D:(kc + 1) * D], ACT.Copy,
                                             scale=pre_c[:, int(u >= J0), kc:kc + 1])
                    nc.scalar.activation(w0d_h[:, u, :], raw[:, 2 * D:3 * D], ACT.Copy).then_inc(w_hi, 1)
                else:
                    nc.scalar.activation(w1_h[:, u - U0, :], raw[:, 0:2 * D], ACT.Copy).then_inc(w_hi, 1)

            def z_hi(p):
                act.wait_ge(zt_s, zt_count(p))
                for kc in range(KC):
                    a = nc.scalar.activation(zh[:, kc, :], ps[:, kc, :], ACT.Copy)
                a.then_inc(zh_s, 1)

            def squares(i, src, wait, before, done, tiles=BT):
                act.wait_ge(*wait)
                if before[1]:
                    act.wait_ge(*before)
                for t in range(tiles):
                    a = nc.scalar.activation(sq[:, t, :], src(t), ACT.Square, accum_out=ssq[:, i, t:t + 1])
                a.then_inc(done, 1)

            def logits_t_out(n, bank):
                act.wait_ge(lgt_ps_s, n + 1)
                nc.scalar.activation(lgt, ps[0:E, bank, :], ACT.Copy).then_inc(lgt_s, 1)

            def exps(n):
                act.wait_ge(lsh_s, n + 1)
                nc.scalar.activation(lex[:, :, :], lsh[:, :, :], ACT.Exp).then_inc(lex_s, 1)

            def gelu(n):
                act.wait_ge(gu_s, n + 1)
                if n >= 2:
                    act.wait_ge(prod_s, n - 1)
                nc.scalar.activation(gel[:, n % 2, :], ps[:, 2 * (n % 2), :], ACT.Gelu_apprx_tanh).then_inc(gelu_s, 1)

            def act_hi(n):
                act.wait_ge(prod_s, n + 1)
                if n >= NA:
                    act.wait_ge(down_s, n - NA + 1)
                nc.scalar.activation(ah[:, n % NA, :], act32[:, n % 2, :], ACT.Copy).then_inc(ah_s, 1)

            def moe_squares(fb, tiles=BT):
                squares(1, lambda t: macc[:, t, :], (acc_s, E * (fb + 1)), (dsq_s, fb + 1), msq_s, tiles)

            def sum_squares(fb, tiles=BT):
                squares(2, lambda t: comb[:, t, :], (comb_s, fb + 1), (msq_s, fb + 1), csq_s, tiles)

            def left_hi(st, b):
                if before(st, b) == "ffn0":
                    act_hi(units(st, b, "ffn0") - 1)

            def ffn0(st):
                p, k = st.p, st.k
                for b in range(2):
                    for c in range(U0):
                        n, fb = U0 * (k + b) + c, k + b
                        if c == 0 and before(st, b) != "attn0":
                            left_hi(st, b)
                            z_hi(p + b)
                        if fb == 0 and c == 0:
                            weights_hi(1)
                        if fb == 0 and c + 2 < U0:
                            weights_hi(c + 2)
                        if fb == 1 and c < U1:
                            weights_hi(U0 + c)
                        if c:
                            act_hi(n - 1)
                        if c == 2:
                            logits_t_out(routed["ffn0", fb], 6)
                        gelu(n)
                        if before(st, b) == "ffn0" and c == 2:
                            moe_squares(fb - 1)
                        if before(st, b) == "ffn0" and c == 4:
                            sum_squares(fb - 1)
                        if c == 6:
                            exps(routed["ffn0", fb])
                        if c == J0 + 1:
                            squares(0, lambda t: ps[:, 4 + t // 2, (t % 2) * D:(t % 2 + 1) * D],
                                    (down_s, U0 * fb + J0), (csq_s, fb), dsq_s)
                if st.after is None:
                    act_hi(U0 * (k + 2) - 1)
                    moe_squares(k + 1)
                    sum_squares(k + 1)

            def ffn1(st):
                p, k = st.p, st.k
                for b in range(2):
                    for c in range(U1):
                        n, fb = U1 * (k + b) + c, k + b
                        if c == 0:
                            left_hi(st, b)
                            if before(st, b) != "attn1":
                                z_hi(p + b)
                            if before(st, b) == "attn1":
                                out_hi(3, 0)
                                out_hi(3, 1)
                            logits_t_out(routed["ffn1", fb], 3)
                        act.wait_ge(h1_s, n + 1)
                        if n >= NA:
                            act.wait_ge(down1_s, n - NA + 1)
                        if n >= 2:
                            act.wait_ge(al1_s, n - 1)
                        elif n == 0 and f0:
                            act.wait_ge(al_s, U0 * f0)
                        if c == 0 and before(st, b) == "attn1":
                            act.wait_ge(ob_ps, 8)
                        nc.scalar.activation(act32[:, n % 2, :], ps[:, n % 3, :], ACT.Relu)
                        nc.scalar.activation(ah[:, (U0 * f0 + n) % NA, :], ps[:, n % 3, :], ACT.Relu).then_inc(ah1_s, 1)
                        if c == 2:
                            exps(routed["ffn1", fb])
                        if before(st, b) == "ffn0" and c == 1:
                            moe_squares(f0 - 1)
                        if before(st, b) == "ffn0" and c == 4:
                            sum_squares(f0 - 1)
                        if fb == 1 and c == 2 and "attn1" in stages:
                            act.wait_ge(wa_s, 16)
                            nc.scalar.activation(wa_h[:, :], wa_raw, ACT.Copy).then_inc(wah_s, 1)
                        if fb == 1 and c == 4 and "attn1" in stages:
                            act.wait_ge(sel_in_s, 32)
                            nc.scalar.activation(sel[:, :, :, :].rearrange("p a b c -> p (a b c)"), sel_raw,
                                                 ACT.Copy).then_inc(sel_s, 1)

            def attn1(st):
                p = st.p
                for b in range(2):
                    if b == 0:
                        z_hi(p)
                    for m in range(2):
                        act.wait_ge(q_ps, 2 * b + m + 1)
                        nc.scalar.activation(qh[:, m, :], ps[:, 2 + m, :], ACT.Copy, scale=-(HD ** -0.5))\
                          .then_inc(qh_s, 1)
                        if b and m == 0:
                            out_hi(1, 0)
                            out_hi(1, 1)
                    act.wait_ge(c_ps, b + 1)
                    nc.scalar.activation(ch[:, :], ps[:, 0, :], ACT.Copy).then_inc(ch_s, 1)
                    for m in range(2):
                        act.wait_ge(k_ps, 2 * b + m + 1)
                        nc.scalar.activation(kh[:, m, :], ps[:, 5 + m, :], ACT.Copy).then_inc(kh_s, 1)
                    for s in range(0, HEADS, 2):
                        act.wait_ge(st_ps, HEADS * b + s + 1)
                        dst = (qs if s < HEADS // 2 else ks)[:, s % (HEADS // 2), :]
                        nc.scalar.activation(dst, ps[:, 1 + s % 4, :], ACT.Copy).then_inc(sta_s, 1)
                    for hb in range(2 * HEADS):
                        hd = 2 * HEADS * b + hb
                        if hb >= 4 and hd % 4 in by_act:
                            probs_t(hd - 4)
                        if hb == HEADS + 10:
                            out_hi(2 * b, 0)
                        act.wait_ge(sm_s, hd + 1)
                        if hd >= 4:
                            act.wait_ge(t_ps, hd - 3)
                        nc.scalar.activation(pb[:, hd % 4, 0:P], ps[:, score_bank(hd), 0:P], ACT.Exp,
                                             bias=nmin[:, hd % 4, 0:1], scale=-1.0)
                        nc.scalar.activation(pb[:, hd % 4, P:3 * P], ps[:, score_bank(hd), P:3 * P], ACT.Exp,
                                             bias=nmin[:, hd % 4, 1:2], scale=-1.0).then_inc(exp_s, 1)
                        if hb % 4 == 2 and hb >= 8:
                            out_t(hd // 4 - 2)
                    for i in (4, 3, 2, 1):
                        if (4 - i) in by_act:
                            probs_t(2 * HEADS * (b + 1) - i)
                    out_hi(2 * b, 1)
                    if b == 0 or st.after:
                        z_hi(p + b + 1)
                    out_t(8 * (b + 1) - 2)
                    out_t(8 * (b + 1) - 1)
                if st.after != "ffn1":
                    out_hi(3, 0)
                    out_hi(3, 1)

            def probs_t(hd):
                act.wait_ge(t_ps, hd + 1)
                if hd >= 8:
                    act.wait_ge(pv_ps, hd // 4 - 1)
                nc.scalar.activation(pbt[:, hd // 4 % 2, hd % 4, :], ps[:, turn_bank(hd), 0:3 * P], ACT.Copy)\
                  .then_inc(pta_s, 1)

            def out_t(g):
                act.wait_ge(pv_ps, g + 1)
                if g >= 8:
                    act.wait_ge(ob_ps, 2 * (g // 4 - 1))
                nc.scalar.activation(ot[g // 4 % 2][:, g % 4, :], ps[:, pv_bank(g), g % 2 * SEQ:(g % 2 + 1) * SEQ], ACT.Copy).then_inc(ot_s, 1)

            def out_hi(n, t):
                act.wait_ge(o2_ps, 2 * n + t + 1)
                nc.scalar.activation(oth[:, t, :, :].rearrange("p c q -> p (c q)"), ps[:, out_bank(n, t), 0:D], ACT.Copy)\
                  .then_inc(oth_s, 1)

            def attn0(st):
                k = st.k
                left_hi(st, 0)
                moe_squares(st.d0 - 1, 2)
                for b in range(2):
                    for i in range(2):
                        n = k + 2 * b + i
                        act.wait_ge(mt_ps_s, n + 1)
                        if b:
                            act.wait_ge(o0_s, n - 1)
                        elif i == 0:
                            act.wait_ge(prod_s, U0 * st.d0)
                        nc.scalar.activation(mt[:, i, :, :], ps[:, i, :], ACT.Copy).then_inc(mt_s, 1)
                    for i in range(2):
                        n = k + 2 * b + i
                        act.wait_ge(sc_ps_s, n + 1)
                        if n == k:
                            act.wait_ge(al_s, U0 * st.d0)
                        nc.scalar.activation(att[:, i, :, :], ps[:, 4 + i, :], ACT.Relu).then_inc(att_s, 1)
                    if b == 0:
                        sum_squares(st.d0 - 1, 2)
                if st.after:
                    z_hi(st.p + 2)

            act.dma_start(pre_c[:, :, :], pre).then_inc(pre_s, 16)
            act.dma_start(ident[:, :], ident_in).then_inc(ident_s, 16)
            act.dma_start(wr_raw[:, :, :, :], wr).then_inc(const_s, 16)
            act.dma_start(a0[:, :], att0).then_inc(const_s, 16)
            act.dma_start(r0c[:, :], r0.partition_broadcast(P)).then_inc(const_s, 16)
            act.dma_start(cap_c[:, :], cap_in).then_inc(const_s, 16)
            act.dma_start(iota_b[:, :], iota_in.partition_broadcast(P)).then_inc(const_s, 16)
            act.dma_start(post_b[:, :], posts.partition_broadcast(P)).then_inc(const_s, 16)
            if "ffn0" in stages:
                weights_hi(0)
            for st in plan:
                {"ffn0": ffn0, "ffn1": ffn1, "attn0": attn0, "attn1": attn1}[st.kind](st)

        @block.vector
        def _(dve):
            steps = {"tk": 0}
            step = sem("setup_dve")
            V = nc.vector

            def weights_lo(u):
                dve.wait_ge(w_hi, u + 1)
                raw = stage[:, u % NST, :]
                if u < U0:
                    for kc in range(KC):
                        V.scalar_tensor_tensor(w0u_l[:, u, kc, :, :].rearrange("p g m -> p (g m)"), raw[:, kc * D:(kc + 1) * D],
                                               pre_c[:, int(u >= J0), kc:kc + 1],
                                               w0u_h[:, u, kc, :, :].rearrange("p g m -> p (g m)").bitcast(F32),
                                               ALU.mult, ALU.subtract)
                    V.tensor_tensor(w0d_l[:, u, :], raw[:, 2 * D:3 * D], w0d_h[:, u, :].bitcast(F32),
                                    ALU.subtract).then_inc(w_lo, 1)
                else:
                    V.tensor_tensor(w1_l[:, u - U0, :], raw[:, 0:2 * D], w1_h[:, u - U0, :].bitcast(F32),
                                    ALU.subtract).then_inc(w_lo, 1)

            def router_weights():
                dve.wait_ge(const_s, 16 * N_SETUP)
                dve.wait_ge(pre_s, 16)
                dve.wait_ge(setup_pool, 3)
                for kc in range(KC):
                    V.tensor_scalar(wr_raw[:, 0, kc, :], wr_raw[:, 0, kc, :], pre_c[:, 2, kc:kc + 1], ROOT,
                                    ALU.mult, ALU.mult).then_inc(step, 1)
                dve.wait_ge(step, KC)
                V.tensor_copy(wr_h[:, :, :, 0:E], wr_raw[:, :, :, :]).then_inc(step, 1)
                dve.wait_ge(step, 1 + KC)
                V.tensor_tensor(wr_l[:, :, :, 0:E], wr_raw[:, :, :, :], wr_h[:, :, :, 0:E].bitcast(F32),
                                ALU.subtract).then_inc(wr_split, 1)

            def ln_stats(p):
                b = p % 2
                if p < 2:
                    dve.wait_ge(x_in_s[b], 16)
                else:
                    dve.wait_ge(x_s[b], p // 2)
                for t in range(BT):
                    i = V.bn_stats(bn[:, t, :], x[:, BT * b + t, :])
                i.then_inc(bn_s, 1)
                dve.wait_ge(bn_s, p + 1)
                if p:
                    dve.wait_ge(z_s, p)
                for t in range(BT):
                    i = V.bn_aggr(mv[:, t, :], bn[:, t, :])
                i.then_inc(mv_s, 1)

            def normalise(p):
                b = p % 2
                dve.wait_ge(zs_s, p + 1)
                if p >= 2:
                    st = plan[p // 2 - 1]
                    if st.kind == "attn0":
                        dve.wait_ge(sc_ps_s, st.k + 2 * b + 2)
                        dve.wait_ge(xz_s, st.k + 2 * b + 2)
                    else:
                        dve.wait_ge(zt_s, zt_count(p - 2))
                for t in range(BT):
                    i = V.tensor_scalar(z2[:, b, t, :], x[:, BT * b + t, :], mv[:, t, 0:1], zs[:, t:t + 1],
                                        ALU.subtract, ALU.mult)
                i.then_inc(z_s, 1)

            def z_lo(p):
                dve.wait_ge(zh_s, zt_count(p))
                for kc in range(KC):
                    i = V.tensor_tensor(zl[:, kc, :], ps[:, kc, :], zh[:, kc, :].bitcast(F32), ALU.subtract)
                i.then_inc(zl_s, 1)

            def tstep(i):
                i.then_inc(tk, 1)
                steps["tk"] += 1

            def tdone():
                dve.wait_ge(tk, steps["tk"])

            def shift_logits(n, bank, top):
                dve.wait_ge(lg_ps_s, n + 1)
                tstep(V.tensor_copy(lg[:, :, :].rearrange("p t e -> p (t e)"), ps[:, bank, 0:BT * E]))
                tdone()
                for t in range(BT):
                    i = V.max(mx[:, t, :], lg[:, t, :])
                tstep(i)
                tdone()
                V.tensor_tensor(lsh[:, :, :], lg[:, :, :], mx[:, :, 0:1].broadcast_to([P, BT, E]),
                                ALU.subtract).then_inc(lsh_s, 1)
                for t in range(BT):
                    i = V.max_index(mi[:, t, :], mx[:, t, :], lg[:, t, :])
                tstep(i)
                tdone()
                tstep(V.tensor_copy(mif[:, :, :], mi[:, :, :]))
                tdone()
                for r in range(top):
                    i = V.tensor_tensor(eq[:, :, :, r], iota_b[:, :].rearrange("p (t e) -> p t e", t=BT),
                                        mif[:, :, r:r + 1].broadcast_to([P, BT, E]), ALU.is_equal)
                tstep(i)
                tdone()
                tstep(V.tensor_reduce(selm[:, :, :], eq[:, :, :, 0:top], AX.X, ALU.add))

            def expert_weights(n, kind, slot):
                dve.wait_ge(lex_s, n + 1)
                tdone()
                tstep(V.tensor_tensor(em[:, :, :], lex[:, :, :], selm[:, :, :], ALU.mult))
                tdone()
                tstep(V.tensor_reduce(esum[:, :], em[:, :, :], AX.X, ALU.add))
                tdone()
                tstep(V.reciprocal(erec[:, :], esum[:, :]))
                tdone()
                tstep(V.tensor_tensor(gs[:, :, :], em[:, :, :], erec[:, :].rearrange("p (t o) -> p t o", o=1)
                                      .broadcast_to([P, BT, E]), ALU.mult))
                tdone()
                if kind == "ffn0":
                    pes = post_b[:, 3 * D:3 * D + E].rearrange("p (o e) -> p o e", o=1).broadcast_to([P, BT, E])
                    tstep(V.tensor_tensor(aff[:, slot, :, :], gs[:, :, :], pes, ALU.mult))
                else:
                    V.tensor_scalar(gs1[:, :, :], gs[:, :, :], 1.0, None, ALU.add).then_inc(step, 1)
                    steps["f1"] = steps.get("f1", 0) + 1
                    dve.wait_ge(step, 1 + KC + 2 * steps["f1"] - 1)
                    V.tensor_tensor(gs1[:, :, :], gs1[:, :, :], gs[:, :, :], ALU.subtract).then_inc(step, 1)
                    dve.wait_ge(step, 1 + KC + 2 * steps["f1"])
                    tstep(V.tensor_tensor(aff[:, slot, :, :], gs1[:, :, :], selm[:, :, :], ALU.mult))
                assert steps["tk"] == TK * (n + 1)

            def accumulate(sums, ready, count, total, e, base, slot, n_tk):
                dve.wait_ge(ready, count)
                if e == 0:
                    dve.wait_ge(tk, n_tk)
                if total:
                    dve.wait_ge(acc_s, total)
                for t in range(BT):
                    o = ps[:, base + t // 2, (t % 2) * D:(t % 2 + 1) * D]
                    a = aff[:, slot, t, e:e + 1]
                    if e == 0:
                        i = V.tensor_scalar(sums[:, t, :], o, a, None, ALU.mult)
                    else:
                        i = V.scalar_tensor_tensor(sums[:, t, :], o, a, sums[:, t, :], ALU.mult, ALU.add)
                i.then_inc(acc_s, 1)

            def acc0(n):
                fb, c = divmod(n, U0)
                if c < J0:
                    return
                e = c - J0
                if e == 0 and fb:
                    dve.wait_ge(mn_s, fb)
                accumulate(macc, down_s, n + 1, E * fb + e, e, 6 if e % 2 == 0 else 4, fb % 2,
                           TK * (routed["ffn0", fb] + 1))

            def product(n):
                dve.wait_ge(gelu_s, n + 1)
                if n >= 2:
                    dve.wait_ge(ah_s, n - 1)
                    dve.wait_ge(al_s, n - 1)
                V.tensor_tensor(act32[:, n % 2, :], gel[:, n % 2, :], ps[:, 2 * (n % 2) + 1, :], ALU.mult)\
                 .then_inc(prod_s, 1)

            def act_lo(n):
                dve.wait_ge(ah_s, n + 1)
                if n >= NA:
                    dve.wait_ge(down_s, n - NA + 1)
                V.tensor_tensor(al[:, n % NA, :], act32[:, n % 2, :], ah[:, n % NA, :].bitcast(F32), ALU.subtract)\
                 .then_inc(al_s, 1)

            def dense_norm(fb):
                dve.wait_ge(rd_s, fb + 1)
                if fb:
                    dve.wait_ge(fin_s, fb)
                for t in range(BT):
                    i = V.scalar_tensor_tensor(comb[:, t, :], ps[:, 4 + t // 2, (t % 2) * D:(t % 2 + 1) * D],
                                               rinv[:, 0, t:t + 1], post_b[:, 0:D], ALU.mult, ALU.mult)
                i.then_inc(dn_s, 1)

            def moe_norm(fb):
                dve.wait_ge(rm_s, fb + 1)
                dve.wait_ge(dn_s, fb + 1)
                if fb:
                    dve.wait_ge(x_s[(fb - 1) % 2], x_count(fb - 1))
                for t in range(BT):
                    i = V.scalar_tensor_tensor(tmp[:, t, :], macc[:, t, :], rinv[:, 1, t:t + 1],
                                               post_b[:, D:2 * D], ALU.mult, ALU.mult)
                i.then_inc(mn_s, 1)
                if fb < f0 - 1 or plan[-1].kind == "ffn0":
                    dve.wait_ge(mn_s, fb + 1)
                    V.tensor_tensor(comb[:, :, :], comb[:, :, :], tmp[:, :, :], ALU.add).then_inc(comb_s, 1)

            def finish0(fb, b):
                dve.wait_ge(rc_s, fb + 1)
                dve.wait_ge(comb_s, fb + 1)
                for t in range(BT):
                    i = V.scalar_tensor_tensor(tmp[:, t, :], comb[:, t, :], rinv[:, 2, t:t + 1],
                                               post_b[:, 2 * D:3 * D], ALU.mult, ALU.mult)
                i.then_inc(fin_s, 1)
                dve.wait_ge(fin_s, fb + 1)
                xb = x[:, BT * b:BT * (b + 1), :]
                V.tensor_tensor(xb, xb, tmp[:, :, :], ALU.add).then_inc(x_s[b], 1)

            def x_count(fb):
                return [st.s for st in plan if st.kind == "ffn0" and st.k == fb // 2 * 2][0] + 1

            def left_lo(st, b):
                left_acc(st, b, 3)
                if before(st, b) == "ffn0":
                    act_lo(units(st, b, "ffn0") - 1)

            def left_acc(st, b, i, later=False):
                if before(st, b) == "ffn0":
                    acc0(units(st, b, "ffn0") - i)
                if before(st, b) == "ffn1":
                    acc1(units(st, b, "ffn1") - i, later)

            def prepare(p, part):
                if p < norms:
                    (normalise if part else ln_stats)(p)

            def ffn0(st):
                p, k = st.p, st.k
                for b in range(2):
                    for c in range(U0):
                        n, fb = U0 * (k + b) + c, k + b
                        if c == 0 and before(st, b) != "attn0":
                            left_lo(st, b)
                            z_lo(p + b)
                        if fb == 0 and c == 0:
                            weights_lo(1)
                        if fb == 0 and c + 2 < U0:
                            weights_lo(c + 2)
                        if fb == 0 and c == 0:
                            router_weights()
                        if fb == 0 and c == 3 and "attn0" in stages:
                            attn0_setup()
                        if fb == 1 and c < U1:
                            weights_lo(U0 + c)
                        if c:
                            act_lo(n - 1)
                        if c < 2 and before(st, b) == "ffn0":
                            left_acc(st, b, 2 - c)
                        if c >= 3:
                            acc0(n - 3)
                        product(n)
                        if c == 5:
                            shift_logits(routed["ffn0", fb], 6, 2)
                        if c == 8:
                            expert_weights(routed["ffn0", fb], "ffn0", fb % 2)
                        if c == J0 + 2:
                            dense_norm(fb)
                        if b and c == 4:
                            moe_norm(fb - 1)
                        if b and c == 6:
                            finish0(fb - 1, 0)
                        if c in ((6, 7), (7, 9))[b]:
                            prepare(p + b + 1, ((6, 7), (7, 9))[b].index(c))
                if st.after is None:
                    last = U0 * (k + 2)
                    act_lo(last - 1)
                    for i in (3, 2, 1):
                        acc0(last - i)
                    moe_norm(k + 1)
                    finish0(k + 1, 1)

            def ffn1(st):
                p, k = st.p, st.k
                for b in range(2):
                    for c in range(U1):
                        n, fb = U1 * (k + b) + c, k + b
                        after_ffn0, after_attn1 = (before(st, b) == kind for kind in ("ffn0", "attn1"))
                        if c == 0:
                            left_lo(st, b)
                            z_lo(p + b)
                            if after_attn1:
                                out_norm(3, 0)
                                out_norm(3, 1)
                            if after_attn1:
                                out_lo(3, 0)
                                out_lo(3, 1)
                        if c < 2:
                            left_acc(st, b, 2 - c)
                        if c >= 3:
                            acc1(n - 3)
                        if c == 1 and after_attn1:
                            out_add(st.p - 2, 3, 0)
                            out_add(st.p - 2, 3, 1)
                        if c == 1:
                            shift_logits(routed["ffn1", fb], 3, 4)
                        if c == 2 and after_ffn0:
                            moe_norm(f0 - 1)
                        if c == 2:
                            expert_weights(routed["ffn1", fb], "ffn1", fb % 2)
                        if c == 5 and after_ffn0:
                            finish0(f0 - 1, 1)
                        first = prepare_at(st, b)
                        if c == first or c == first + 1:
                            prepare(p + b + 1, c - first)
                if st.after is None:
                    for i in (3, 2, 1):
                        acc1(U1 * (k + 2) - i)

            def stage_of(fb):
                return [st.s for st in plan if st.kind == "ffn1" and st.k == fb // 2 * 2][0]

            def acc1(n, later=False):
                fb, e = divmod(n, U1)
                b = fb % 2
                if e == 0 and fb:
                    dve.wait_ge(x_s[1 - b], stage_of(fb - 1) + 1)
                elif e == 0 and f0:
                    dve.wait_ge(prod_s, U0 * f0)
                if e == 0 and fb == 2 and "attn1" in stages:
                    dve.wait_ge(ob_ps, 6)
                accumulate(macc1, down1_s, n + 1, E * f0 + n, e, 6 - 2 * (n % 2), b, TK * (routed["ffn1", fb] + 1))
                if e == E - 1 and not later:
                    finish1(fb)

            def finish1(fb):
                b = fb % 2
                dve.wait_ge(acc_s, E * f0 + U1 * (fb + 1))
                xb = x[:, BT * b:BT * (b + 1), :]
                V.scalar_tensor_tensor(xb, macc1[:, :, :], 0.5, xb, ALU.mult, ALU.add).then_inc(x_s[b], 1)

            def attn1(st):
                p = st.p
                for b in range(2):
                    left_acc(st, b, 3)
                    z_lo(p + b)
                    if b:
                        out_norm(1, 0)
                        out_norm(1, 1)
                    for m in range(2):
                        dve.wait_ge(qh_s, 2 * b + m + 1)
                        V.scalar_tensor_tensor(ql[:, m, :], ps[:, 2 + m, :], -(HD ** -0.5), qh[:, m, :].bitcast(F32),
                                               ALU.mult, ALU.subtract).then_inc(ql_s, 1)
                        if b:
                            for t in range(2):
                                if m:
                                    out_add(p, 1, t)
                                else:
                                    out_lo(1, t)
                        else:
                            left_acc(st, b, 2 - m, later=True)
                    dve.wait_ge(ch_s, b + 1)
                    V.tensor_tensor(cl[:, :], ps[:, 0, :], ch[:, :].bitcast(F32), ALU.subtract).then_inc(cl_s, 1)
                    for s in (1, 3):
                        stack_out(b, s)
                    if before(st, b) == "ffn1":
                        finish1(st.d1 - 1)
                    for m in range(2):
                        dve.wait_ge(kh_s, 2 * b + m + 1)
                        V.tensor_tensor(kl[:, m, :], ps[:, 5 + m, :], kh[:, m, :].bitcast(F32), ALU.subtract)\
                         .then_inc(kl_s, 1)
                    dve.wait_ge(v_ps, b + 1)
                    dve.wait_ge(wal_s, WL + 2)
                    for t in range(BT):
                        v = ps[:, 7 * (1 - t // 2), (t % 2) * D:(t % 2 + 1) * D].rearrange("p (h d) -> p h d", d=HD)
                        i = V.tensor_copy(va[:, t, :, 0:HD], v)
                    i.then_inc(v_s, 1)
                    for s in range(5, HEADS, 2):
                        if s == 13:
                            bias_min(2 * HEADS * b)
                        stack_out(b, s)
                    for hb in range(2 * HEADS):
                        hd = 2 * HEADS * b + hb
                        if hb in (HEADS + 8, HEADS + 15):
                            out_norm(2 * b, hb // (HEADS + 15))
                        if hb == HEADS + 11:
                            out_lo(2 * b, 0)
                        if hb == HEADS + 13:
                            out_add(p, 2 * b, 0)
                        if hb:
                            bias_min(hd)
                        if hb >= 4 and hd % 4 not in by_act:
                            probs_t(hd - 4)
                        if hb == 6 or hb == 10:
                            prepare(p + b + 1, hb // 8)
                    for i in (4, 3, 2, 1):
                        if (4 - i) not in by_act:
                            probs_t(2 * HEADS * (b + 1) - i)
                    out_lo(2 * b, 1)
                    out_add(p, 2 * b, 1)
                if st.after != "ffn1":
                    for t in range(2):
                        out_norm(3, t)
                    for t in range(2):
                        out_lo(3, t)
                    for t in range(2):
                        out_add(p, 3, t)

            def stack_out(b, s):
                dve.wait_ge(st_ps, HEADS * b + s + 1)
                V.tensor_copy((qs if s < HEADS // 2 else ks)[:, s % (HEADS // 2), :], ps[:, 1 + s % 4, :])\
                 .then_inc(std_s, 1)

            def bias_min(hd):
                dve.wait_ge(s_ps, hd + 1)
                if hd >= 4:
                    dve.wait_ge(exp_s, hd - 3)
                if hd == 0:
                    dve.wait_ge(sel_in_s, 32)
                for c, (lo, hi) in enumerate(((0, P), (P, 3 * P))):
                    s = ps[:, score_bank(hd), lo:hi]
                    i = V.tensor_tensor_reduce(s, s, bias[:, lo:hi], 1.0, FAR, ALU.add, ALU.min,
                                               nmin[:, hd % 4, c:c + 1])
                i.then_inc(sm_s, 1)

            def probs_t(hd):
                dve.wait_ge(t_ps, hd + 1)
                if hd >= 8:
                    dve.wait_ge(pv_ps, hd // 4 - 1)
                V.tensor_copy(pbt[:, hd // 4 % 2, hd % 4, :], ps[:, turn_bank(hd), 0:3 * P]).then_inc(ptd_s, 1)

            def out_norm(n, t):
                c = 2 * n + t + 1
                dve.wait_ge(ob_ps, c)
                if c > 2:
                    dve.wait_ge(o2_ps, c - 2)
                o = ps[:, out_bank(n, t), :].rearrange("p (h s) -> p h s", s=SLOT)
                V.reciprocal(rec[:, t, :], o[:, :, HD]).then_inc(rec_s, 1)
                dve.wait_ge(rec_s, c)
                V.tensor_tensor(on[:, t, :].rearrange("p (h d) -> p h d", d=HD), o[:, :, 0:HD],
                                rec[:, t, :].rearrange("p (h o) -> p h o", o=1).broadcast_to([P, HEADS, HD]),
                                ALU.mult).then_inc(on_s, 1)

            def out_lo(n, t):
                dve.wait_ge(oth_s, 2 * n + t + 1)
                V.tensor_tensor(otl[:, t, :, :].rearrange("p c q -> p (c q)"), ps[:, out_bank(n, t), 0:D],
                                oth[:, t, :, :].rearrange("p c q -> p (c q)").bitcast(F32), ALU.subtract)\
                 .then_inc(otl_s, 1)

            def out_add(p, n, t):
                c = 2 * n + t + 1
                dve.wait_ge(y_ps, c)
                xt = x[:, 2 * n + t, :]
                V.tensor_tensor(xt, xt, ps[:, out_bank(n, t), 0:D], ALU.add).then_inc(yt_s, 1)
                if t == 1 and n % 2:
                    dve.wait_ge(yt_s, c)
                    V.memset(mark[:, :], 0.0).then_inc(x_s[n // 2], 1)

            def last_squares(i, src, wait):
                dve.wait_ge(*wait)
                if i == 1:
                    dve.wait_ge(dsq_s, wait[1] // E)
                else:
                    dve.wait_ge(msq_s, wait[1])
                for t in (2, 3):
                    s = V.tensor_tensor_reduce(sq[:, t, :], src[:, t, :], src[:, t, :], 1.0, 0.0, ALU.mult, ALU.add,
                                               ssq[:, i, t:t + 1])
                s.then_inc(vsq_s, 1)

            def attn0_setup():
                dve.wait_ge(const_s, 16 * N_SETUP)
                for t in range(2):
                    i = V.tensor_scalar(m0[:, t, :], ident[:, :], r0c[:, 0:1], None, ALU.mult)
                i.then_inc(a0_set, 1)
                dve.wait_ge(a0_set, 1)
                V.tensor_copy(m0[0:SA, 0, 0:SA], a0[:, 0:SA]).then_inc(a0_set, 1)
                dve.wait_ge(pt_ps_s, 1)
                V.tensor_copy(pt[:, :], ps[0:SA, 7, 0:SA]).then_inc(a0_set, 1)

            def attn0(st):
                p, k = st.p, st.k
                left_lo(st, 0)
                left_acc(st, 0, 2)
                left_acc(st, 0, 1)
                last_squares(1, macc, (acc_s, E * st.d0))
                for b in range(2):
                    z = z2[:, (p + b) % 2, :, :]
                    for i in range(2):
                        n = k + 2 * b + i
                        dve.wait_ge(mt_ps_s, n + 1)
                        if b:
                            dve.wait_ge(sc_ps_s, n - 1)
                        V.tensor_copy(pxs[:, i, :], ps[0:SA, 2 + i, 0:D]).then_inc(px_s, 1)
                    if b:
                        prepare(p + 2, 1)
                    if b == 0:
                        moe_norm(st.d0 - 1)
                        last_squares(2, comb, (comb_s, st.d0))
                    for i in range(2):
                        xb = x[:, 4 * b + 2 * i:4 * b + 2 * i + 2, :]
                        V.tensor_tensor(xb, xb, z[:, 2 * i:2 * i + 2, :], ALU.add).then_inc(xz_s, 1)
                    for i in range(2):
                        dve.wait_ge(att_s, k + 2 * b + i + 1)
                        V.tensor_tensor(att[96:P, i, 1, D - 1:D], att[96:P, i, 1, D - 1:D], cap_c[96:P, :], ALU.min)\
                         .then_inc(attz_s, 1)
                    if b == 0:
                        finish0(st.d0 - 1, 1)
                        prepare(p + 1, 0)
                        prepare(p + 1, 1)
                    elif st.after:
                        z_lo(p + 2)
                    for i in range(2):
                        n = k + 2 * b + i
                        dve.wait_ge(o0_s, n + 1)
                        dve.wait_ge(xz_s, n + 1)
                        xb = x[:, 4 * b + 2 * i:4 * b + 2 * i + 2, :]
                        V.tensor_tensor(xb, xb, ps[:, 6 + i, :].rearrange("p (t d) -> p t d", t=2), ALU.add)\
                         .then_inc(x_s[b] if i else upd_s, 1)
                    if b == 0:
                        prepare(p + 2, 0)

            if "ffn0" not in stages:
                router_weights()
            prepare(0, 0)
            prepare(0, 1)
            for st in plan:
                if st.kind == "ffn0" and st.k == 0:
                    weights_lo(0)
                {"ffn0": ffn0, "ffn1": ffn1, "attn0": attn0, "attn1": attn1}[st.kind](st)


def kernel(**inputs):
    import numpy as np
    import concourse.bacc as bacc
    from concourse.bass_utils import run_bass_kernel_spmd

    a = {k: np.asarray(v) for k, v in inputs.items()}
    f = {k[7:]: v for k, v in a.items() if k.startswith("L0_ffn_")}
    dense = [f[n].reshape(KC, P, J0, P) for n in ("w_gate", "w_up")]
    dense = np.stack(dense).transpose(3, 2, 1, 0, 4)
    moe = [f[n].reshape(E, KC, P, P) for n in ("we_gate", "we_up")]
    moe = np.stack(moe).transpose(1, 3, 2, 0, 4)
    down = np.concatenate([f["w_down"].reshape(J0, P, D), f["we_down"]])
    w0 = np.concatenate([np.concatenate([dense, moe]).reshape(U0, P, 2 * D), down], axis=2)
    w1u = a["L1_ffn_w1"].reshape(E, P, KC, P).transpose(0, 3, 2, 1).reshape(E, P, D)
    w1 = np.concatenate([w1u, a["L1_ffn_w2"].transpose(0, 2, 1)], axis=2)
    wr = np.stack([f["router_w"].reshape(KC, P, E), a["L1_ffn_wg"].reshape(KC, P, E)]).transpose(2, 0, 1, 3)
    pre = np.stack([f[n].reshape(KC, P) for n in ("rn_pre1", "rn_pre2", "router_scale")]).transpose(2, 0, 1)
    posts = np.concatenate([f["rn_post1"], f["rn_post2"], f["rn_post"], f["per_expert_scale"]])
    att0 = np.concatenate([a["L0_attn_A_l"].T, a["L0_attn_B_l"], a["L0_attn_C_l"]], axis=1)
    cap = np.full((P, 1), 3.4028235e38, np.float32)
    cap[P - 1] = 0.0
    t = {n: a["L1_attn_" + n].T for n in ("w_q", "w_dkv", "w_uk", "w_uv", "w_o")}
    chunks = {n: v.reshape(-1, P, v.shape[1]).transpose(1, 0, 2).reshape(P, -1) for n, v in t.items()}
    wa = np.concatenate([chunks[n] for n in ("w_q", "w_dkv", "w_uk", "w_uv", "w_o")], axis=1)
    sel = np.zeros((P, 4, 4, P), np.float32)
    for pair in range(4):
        for e in range(2):
            for r in range(HD):
                for part, kinds in enumerate(((0, 2), (1, 2), (0, 3))):
                    for kind in kinds:
                        sel[(2 * pair + e) * HD + r, kind, pair, STEP * e + HD * part + r] = 1.0
    q, j = np.arange(SEQ)[:, None], np.arange(SEQ)[None, :]
    far = np.where(j <= q, 0.0625 * (q - j), FAR).astype(np.float32)
    bias = np.concatenate([far[:P, :P], far[P:, :]], axis=1)
    arrays = {
        "x": a["L0_attn_Z_in"].reshape(TOKENS, D), "w0": w0, "w1": w1, "wr": wr, "pre": pre, "posts": posts,
        "att0": att0, "r0": a["L0_attn_r_l"], "ident": np.eye(P, dtype=np.float32), "cap": cap,
        "iota": np.tile(np.arange(E, dtype=np.float32), BT), "wa": wa, "sel": sel, "bias": bias,
    }
    arrays = {k: np.ascontiguousarray(v) for k, v in arrays.items()}
    nc = bacc.Bacc("TRN2", target_bir_lowering=False, num_devices=1)
    args = [nc.dram_tensor(f"in_{k}_dram", v.shape, mybir.dt.from_np(v.dtype), kind="ExternalInput").ap()
            for k, v in arrays.items()]
    out = nc.dram_tensor("out_dram", (TOKENS, D), F32, kind="ExternalOutput").ap()
    program(nc, *args, out)
    got = run_bass_kernel_spmd(nc, [{f"in_{k}_dram": v for k, v in arrays.items()}], core_ids=[0])
    return got.results[0]["out_dram"].reshape(4, SEQ, D)
```
